# Optimizing a Trainium2 kernel written in Bass

```python
import numpy as np
import jax
import jax.numpy as jnp

def _softmax(x, axis=-1):
    return jax.nn.softmax(x, axis=axis)

def _gelu(x):
    return jax.nn.gelu(x, approximate=True)

def _silu(x):
    return jax.nn.silu(x)

def _sigmoid(x):
    return jax.nn.sigmoid(x)

def _layernorm(x, axis=-1, eps=1e-05):
    m = jnp.mean(x, axis=axis, keepdims=True)
    v = jnp.var(x, axis=axis, keepdims=True)
    return (x - m) / jnp.sqrt(v + eps)

def _scatter_add(tgt, idx, src, axis=0):
    return tgt.at[idx].add(src)

def _segment_sum(src, seg, n):
    return jax.ops.segment_sum(src, seg, n)
kernel_name = 'mk_macaron_d1_jaxref_r4_03c174'

def setup_inputs(seed: int=0):
    np.random.seed(seed)
    _w = jnp.asarray

    def _L0_attn_setup():
        import jax, jax.numpy as jnp
        import numpy as np
        DIM = 256
        D_STATE = 32
        HEADDIM = 64
        EXPAND = 2
        CHUNK = 64
        D_INNER = EXPAND * DIM
        NHEADS = D_INNER // HEADDIM
        ROPE_DIM = int(0.5 * D_STATE)
        D_IN_PROJ = 2 * D_INNER + 2 * D_STATE + NHEADS
        B_SZ = 4
        L = 1024

        def _segsum(a):
            T = a.shape[-1]
            cs = jnp.cumsum(a, axis=-1)
            d = cs[..., :, None] - cs[..., None, :]
            mask = jnp.tril(jnp.ones((T, T), bool))
            return jnp.where(mask, d, -jnp.inf)

        def _rope(v):
            t = jnp.arange(v.shape[1], dtype=jnp.float32)
            inv_freq = 1.0 / 10000.0 ** (jnp.arange(0, ROPE_DIM, 2, dtype=jnp.float32) / ROPE_DIM)
            ang = t[:, None] * inv_freq[None, :]
            cos, sin = (jnp.cos(ang)[None], jnp.sin(ang)[None])
            vr, vp = (v[..., :ROPE_DIM], v[..., ROPE_DIM:])
            v1, v2 = (vr[..., 0::2], vr[..., 1::2])
            r = jnp.stack([v1 * cos - v2 * sin, v1 * sin + v2 * cos], axis=-1)
            return jnp.concatenate([r.reshape(vr.shape), vp], axis=-1)
        key = jax.random.key(seed)
        ks = jax.random.split(key, 8)
        return {'x': jax.random.normal(ks[0], (B_SZ, L, DIM), jnp.float32), 'ln_w': jnp.ones((DIM,), jnp.float32), 'ln_b': jnp.zeros((DIM,), jnp.float32), 'W_in': jax.random.normal(ks[1], (DIM, D_IN_PROJ), jnp.float32) * 0.02, 'dt_bias': jax.random.uniform(ks[2], (NHEADS,), jnp.float32, -4.0, -1.0), 'A_log': jnp.log(jax.random.uniform(ks[3], (NHEADS,), jnp.float32, 1.0, 16.0)), 'D': jax.random.normal(ks[4], (NHEADS,), jnp.float32) * 0.1 + 1.0, 'rms_w': jnp.ones((D_INNER,), jnp.float32), 'W_out': jax.random.normal(ks[5], (D_INNER, DIM), jnp.float32) * 0.02}
    _L0_attn_in = _L0_attn_setup()

    def _L0_ffn_setup():
        import jax, jax.numpy as jnp
        import numpy as np
        DIM = 256
        DEPTH = 2
        HEADS = 8
        DIM_HEAD = 64
        WINDOW = 128
        INNER = HEADS * DIM_HEAD
        HID = int(DIM * 4 * 2 / 3)
        B, N = (2, 2048)
        QK_SCALE = 8.0

        def shift_token(t):
            t1, t2 = jnp.split(t, 2, axis=-1)
            t2 = jnp.pad(t2, ((0, 0), (1, 0), (0, 0)))[:, :-1]
            return jnp.concatenate([t1, t2], axis=-1)

        def l2norm(t):
            return t / jnp.clip(jnp.linalg.norm(t, axis=-1, keepdims=True), 1e-12)

        def rotate_half(x):
            x1, x2 = jnp.split(x, 2, axis=-1)
            return jnp.concatenate([-x2, x1], axis=-1)

        def rotary_xpos(q, k):
            n = q.shape[-2]
            half_idx = jnp.arange(0, DIM_HEAD, 2, dtype=jnp.float32)
            inv_freq = 1.0 / 10000.0 ** (half_idx / DIM_HEAD)
            t = jnp.arange(n, dtype=jnp.float32)
            freqs = t[:, None] * inv_freq[None, :]
            freqs = jnp.concatenate([freqs, freqs], axis=-1)
            base = (half_idx + 0.4 * DIM_HEAD) / (1.4 * DIM_HEAD)
            power = (t - n // 2) / float(WINDOW // 2)
            scale = base[None, :] ** power[:, None]
            scale = jnp.concatenate([scale, scale], axis=-1)
            cos, sin = (jnp.cos(freqs), jnp.sin(freqs))
            q = q * cos * scale + rotate_half(q) * sin * scale
            k = k * cos / scale + rotate_half(k) * sin / scale
            return (q, k)

        def local_attention(q, k, v):
            b, h, n, d = q.shape
            w = n // WINDOW
            bq = q.reshape(b, h, w, WINDOW, d) * QK_SCALE
            bk = k.reshape(b, h, w, WINDOW, d)
            bv = v.reshape(b, h, w, WINDOW, d)

            def look_around(t):
                p = jnp.pad(t, ((0, 0), (0, 0), (1, 0), (0, 0), (0, 0)))
                return jnp.concatenate([p[:, :, :w], p[:, :, 1:]], axis=3)
            bk, bv = (look_around(bk), look_around(bv))
            bt = jnp.arange(n).reshape(w, WINDOW)
            btp = jnp.pad(bt, ((1, 0), (0, 0)), constant_values=-1)
            btk = jnp.concatenate([btp[:w], btp[1:]], axis=1)
            sim = jnp.einsum('bhwid,bhwjd->bhwij', bq, bk)
            i = bt[:, :, None]
            j = btk[:, None, :]
            mask = (i < j) | (i > j + WINDOW) | (j == -1)
            sim = jnp.where(mask, -jnp.finfo(sim.dtype).max, sim)
            attn = jax.nn.softmax(sim, axis=-1)
            out = jnp.einsum('bhwij,bhwjd->bhwid', attn, bv)
            return out.reshape(b, h, n, d)

        def _layer(x, wqkv, qs, ksc, wo, lg, lb, w1, b1, w2, b2):
            b, n, _ = x.shape
            h = shift_token(x)
            qkv = h @ wqkv
            q, k, v = jnp.split(qkv, 3, axis=-1)
            to_heads = lambda t: t.reshape(b, n, HEADS, DIM_HEAD).transpose(0, 2, 1, 3)
            q, k, v = (to_heads(q), to_heads(k), to_heads(v))
            q = l2norm(q) * qs
            k = l2norm(k) * ksc
            q, k = rotary_xpos(q, k)
            o = local_attention(q, k, v)
            o = o.transpose(0, 2, 1, 3).reshape(b, n, INNER)
            x = x + o @ wo
            h = shift_token(x)
            mu = h.mean(-1, keepdims=True)
            var = h.var(-1, keepdims=True)
            h = (h - mu) / jnp.sqrt(var + 1e-05) * lg + lb
            h = h @ w1 + b1
            a, g = jnp.split(h, 2, axis=-1)
            h = a * jax.nn.gelu(g, approximate=False)
            x = x + h @ w2 + b2
            return x
        key = jax.random.key(seed)
        ks = jax.random.split(key, 6)
        return {'x': jax.random.normal(ks[0], (B, N, DIM), jnp.float32), 'wqkv': jax.random.normal(ks[1], (DEPTH, DIM, 3 * INNER), jnp.float32) * 0.02, 'q_scale': jnp.ones((DEPTH, DIM_HEAD), jnp.float32), 'k_scale': jnp.ones((DEPTH, DIM_HEAD), jnp.float32), 'wo': jax.random.normal(ks[2], (DEPTH, INNER, DIM), jnp.float32) * 0.02, 'ln_g': jnp.ones((DEPTH, DIM), jnp.float32), 'ln_b': jnp.zeros((DEPTH, DIM), jnp.float32), 'w1': jax.random.normal(ks[3], (DEPTH, DIM, 2 * HID), jnp.float32) * 0.02, 'b1': jnp.zeros((DEPTH, 2 * HID), jnp.float32), 'w2': jax.random.normal(ks[4], (DEPTH, HID, DIM), jnp.float32) * 0.02, 'b2': jnp.zeros((DEPTH, DIM), jnp.float32)}
    _L0_ffn_in = _L0_ffn_setup()
    _d = {'L0_attn_x': _L0_attn_in['x'], 'L0_attn_ln_w': _L0_attn_in['ln_w'], 'L0_attn_ln_b': _L0_attn_in['ln_b'], 'L0_attn_W_in': _L0_attn_in['W_in'], 'L0_attn_dt_bias': _L0_attn_in['dt_bias'], 'L0_attn_A_log': _L0_attn_in['A_log'], 'L0_attn_D': _L0_attn_in['D'], 'L0_attn_rms_w': _L0_attn_in['rms_w'], 'L0_attn_W_out': _L0_attn_in['W_out'], 'L0_ffn_wqkv': _L0_ffn_in['wqkv'], 'L0_ffn_q_scale': _L0_ffn_in['q_scale'], 'L0_ffn_k_scale': _L0_ffn_in['k_scale'], 'L0_ffn_wo': _L0_ffn_in['wo'], 'L0_ffn_ln_g': _L0_ffn_in['ln_g'], 'L0_ffn_ln_b': _L0_ffn_in['ln_b'], 'L0_ffn_w1': _L0_ffn_in['w1'], 'L0_ffn_b1': _L0_ffn_in['b1'], 'L0_ffn_w2': _L0_ffn_in['w2'], 'L0_ffn_b2': _L0_ffn_in['b2']}
    _x0 = _d['L0_attn_x']
    _d['L0_attn_x'] = jax.random.normal(jax.random.fold_in(jax.random.key(seed), 1), (1, 4096, 256), dtype=_x0.dtype)
    del _x0
    return _d

def reference(L0_attn_x, L0_attn_ln_w, L0_attn_ln_b, L0_attn_W_in, L0_attn_dt_bias, L0_attn_A_log, L0_attn_D, L0_attn_rms_w, L0_attn_W_out, L0_ffn_wqkv, L0_ffn_q_scale, L0_ffn_k_scale, L0_ffn_wo, L0_ffn_ln_g, L0_ffn_ln_b, L0_ffn_w1, L0_ffn_b1, L0_ffn_w2, L0_ffn_b2):

    def _L0_attn_ref(x, ln_w, ln_b, W_in, dt_bias, A_log, D, rms_w, W_out):
        import jax, jax.numpy as jnp
        import numpy as np
        DIM = 256
        D_STATE = 32
        HEADDIM = 64
        EXPAND = 2
        CHUNK = 64
        D_INNER = EXPAND * DIM
        NHEADS = D_INNER // HEADDIM
        ROPE_DIM = int(0.5 * D_STATE)
        D_IN_PROJ = 2 * D_INNER + 2 * D_STATE + NHEADS
        B_SZ = 4
        L = 1024

        def _segsum(a):
            T = a.shape[-1]
            cs = jnp.cumsum(a, axis=-1)
            d = cs[..., :, None] - cs[..., None, :]
            mask = jnp.tril(jnp.ones((T, T), bool))
            return jnp.where(mask, d, -jnp.inf)

        def _rope(v):
            t = jnp.arange(v.shape[1], dtype=jnp.float32)
            inv_freq = 1.0 / 10000.0 ** (jnp.arange(0, ROPE_DIM, 2, dtype=jnp.float32) / ROPE_DIM)
            ang = t[:, None] * inv_freq[None, :]
            cos, sin = (jnp.cos(ang)[None], jnp.sin(ang)[None])
            vr, vp = (v[..., :ROPE_DIM], v[..., ROPE_DIM:])
            v1, v2 = (vr[..., 0::2], vr[..., 1::2])
            r = jnp.stack([v1 * cos - v2 * sin, v1 * sin + v2 * cos], axis=-1)
            return jnp.concatenate([r.reshape(vr.shape), vp], axis=-1)
        B, Ls, _ = x.shape
        mu = jnp.mean(x, -1, keepdims=True)
        var = jnp.var(x, -1, keepdims=True)
        h = (x - mu) * jax.lax.rsqrt(var + 1e-06) * ln_w + ln_b
        zxbcdt = h @ W_in
        z = zxbcdt[..., :D_INNER]
        xs = jax.nn.silu(zxbcdt[..., D_INNER:2 * D_INNER])
        Bc = jax.nn.silu(zxbcdt[..., 2 * D_INNER:2 * D_INNER + D_STATE])
        Cc = jax.nn.silu(zxbcdt[..., 2 * D_INNER + D_STATE:2 * D_INNER + 2 * D_STATE])
        dt = jax.nn.softplus(zxbcdt[..., -NHEADS:] + dt_bias)
        Bc, Cc = (_rope(Bc), _rope(Cc))
        A = -jnp.exp(A_log)
        xh = xs.reshape(B, Ls, NHEADS, HEADDIM)
        nc = Ls // CHUNK
        Xc = (xh * dt[..., None]).reshape(B, nc, CHUNK, NHEADS, HEADDIM)
        a = (dt * A).reshape(B, nc, CHUNK, NHEADS).transpose(0, 3, 1, 2)
        Bk = Bc.reshape(B, nc, CHUNK, D_STATE)
        Ck = Cc.reshape(B, nc, CHUNK, D_STATE)
        A_cs = jnp.cumsum(a, axis=-1)
        Lmat = jnp.exp(_segsum(a))
        scores = jnp.einsum('bcln,bcsn->bcls', Ck, Bk)
        M = scores[:, None] * Lmat
        Yd = jnp.einsum('bhcls,bcshp->bclhp', M, Xc)
        decay_states = jnp.exp(A_cs[..., -1:] - A_cs)
        states = jnp.einsum('bcln,bhcl,bclhp->bchpn', Bk, decay_states, Xc)
        states = jnp.concatenate([jnp.zeros_like(states[:, :1]), states], axis=1)
        dc = jnp.exp(_segsum(jnp.pad(A_cs[..., -1], ((0, 0), (0, 0), (1, 0)))))
        states_in = jnp.einsum('bhzc,bchpn->bzhpn', dc, states)[:, :-1]
        Yo = jnp.einsum('bcln,bchpn,bhcl->bclhp', Ck, states_in, jnp.exp(A_cs))
        y = (Yd + Yo).reshape(B, Ls, NHEADS, HEADDIM) + xh * D[None, None, :, None]
        y = y.reshape(B, Ls, D_INNER)
        y = y * jax.nn.silu(z)
        y = y * jax.lax.rsqrt(jnp.mean(y * y, -1, keepdims=True) + 1e-06) * rms_w
        return x + y @ W_out

    def _L0_ffn_ref(x, wqkv, q_scale, k_scale, wo, ln_g, ln_b, w1, b1, w2, b2):
        import jax, jax.numpy as jnp
        import numpy as np
        DIM = 256
        DEPTH = 2
        HEADS = 8
        DIM_HEAD = 64
        WINDOW = 128
        INNER = HEADS * DIM_HEAD
        HID = int(DIM * 4 * 2 / 3)
        B, N = (2, 2048)
        QK_SCALE = 8.0

        def shift_token(t):
            t1, t2 = jnp.split(t, 2, axis=-1)
            t2 = jnp.pad(t2, ((0, 0), (1, 0), (0, 0)))[:, :-1]
            return jnp.concatenate([t1, t2], axis=-1)

        def l2norm(t):
            return t / jnp.clip(jnp.linalg.norm(t, axis=-1, keepdims=True), 1e-12)

        def rotate_half(x):
            x1, x2 = jnp.split(x, 2, axis=-1)
            return jnp.concatenate([-x2, x1], axis=-1)

        def rotary_xpos(q, k):
            n = q.shape[-2]
            half_idx = jnp.arange(0, DIM_HEAD, 2, dtype=jnp.float32)
            inv_freq = 1.0 / 10000.0 ** (half_idx / DIM_HEAD)
            t = jnp.arange(n, dtype=jnp.float32)
            freqs = t[:, None] * inv_freq[None, :]
            freqs = jnp.concatenate([freqs, freqs], axis=-1)
            base = (half_idx + 0.4 * DIM_HEAD) / (1.4 * DIM_HEAD)
            power = (t - n // 2) / float(WINDOW // 2)
            scale = base[None, :] ** power[:, None]
            scale = jnp.concatenate([scale, scale], axis=-1)
            cos, sin = (jnp.cos(freqs), jnp.sin(freqs))
            q = q * cos * scale + rotate_half(q) * sin * scale
            k = k * cos / scale + rotate_half(k) * sin / scale
            return (q, k)

        def local_attention(q, k, v):
            b, h, n, d = q.shape
            w = n // WINDOW
            bq = q.reshape(b, h, w, WINDOW, d) * QK_SCALE
            bk = k.reshape(b, h, w, WINDOW, d)
            bv = v.reshape(b, h, w, WINDOW, d)

            def look_around(t):
                p = jnp.pad(t, ((0, 0), (0, 0), (1, 0), (0, 0), (0, 0)))
                return jnp.concatenate([p[:, :, :w], p[:, :, 1:]], axis=3)
            bk, bv = (look_around(bk), look_around(bv))
            bt = jnp.arange(n).reshape(w, WINDOW)
            btp = jnp.pad(bt, ((1, 0), (0, 0)), constant_values=-1)
            btk = jnp.concatenate([btp[:w], btp[1:]], axis=1)
            sim = jnp.einsum('bhwid,bhwjd->bhwij', bq, bk)
            i = bt[:, :, None]
            j = btk[:, None, :]
            mask = (i < j) | (i > j + WINDOW) | (j == -1)
            sim = jnp.where(mask, -jnp.finfo(sim.dtype).max, sim)
            attn = jax.nn.softmax(sim, axis=-1)
            out = jnp.einsum('bhwij,bhwjd->bhwid', attn, bv)
            return out.reshape(b, h, n, d)

        def _layer(x, wqkv, qs, ksc, wo, lg, lb, w1, b1, w2, b2):
            b, n, _ = x.shape
            h = shift_token(x)
            qkv = h @ wqkv
            q, k, v = jnp.split(qkv, 3, axis=-1)
            to_heads = lambda t: t.reshape(b, n, HEADS, DIM_HEAD).transpose(0, 2, 1, 3)
            q, k, v = (to_heads(q), to_heads(k), to_heads(v))
            q = l2norm(q) * qs
            k = l2norm(k) * ksc
            q, k = rotary_xpos(q, k)
            o = local_attention(q, k, v)
            o = o.transpose(0, 2, 1, 3).reshape(b, n, INNER)
            x = x + o @ wo
            h = shift_token(x)
            mu = h.mean(-1, keepdims=True)
            var = h.var(-1, keepdims=True)
            h = (h - mu) / jnp.sqrt(var + 1e-05) * lg + lb
            h = h @ w1 + b1
            a, g = jnp.split(h, 2, axis=-1)
            h = a * jax.nn.gelu(g, approximate=False)
            x = x + h @ w2 + b2
            return x
        for l in range(DEPTH):
            x = _layer(x, wqkv[l], q_scale[l], k_scale[l], wo[l], ln_g[l], ln_b[l], w1[l], b1[l], w2[l], b2[l])
        return x
    x = L0_attn_x
    x = x + 0.5 * _L0_ffn_ref(_layernorm(x, axis=-1), L0_ffn_wqkv, L0_ffn_q_scale, L0_ffn_k_scale, L0_ffn_wo, L0_ffn_ln_g, L0_ffn_ln_b, L0_ffn_w1, L0_ffn_b1, L0_ffn_w2, L0_ffn_b2)
    x = x + _L0_attn_ref(_layernorm(x, axis=-1), L0_attn_ln_w, L0_attn_ln_b, L0_attn_W_in, L0_attn_dt_bias, L0_attn_A_log, L0_attn_D, L0_attn_rms_w, L0_attn_W_out)
    x = x + 0.5 * _L0_ffn_ref(_layernorm(x, axis=-1), L0_ffn_wqkv, L0_ffn_q_scale, L0_ffn_k_scale, L0_ffn_wo, L0_ffn_ln_g, L0_ffn_ln_b, L0_ffn_w1, L0_ffn_b1, L0_ffn_w2, L0_ffn_b2)
    return x

_drawn_inputs = setup_inputs


def setup_inputs(seed=0):
    import zlib

    import numpy as np

    out = dict(_drawn_inputs(seed))
    spreads = {'L0_attn_ln_w': (1.0, 0.2),
     'L0_attn_ln_b': (0.0, 0.314),
     'L0_attn_rms_w': (1.0, 0.2),
     'L0_ffn_q_scale': (1.0, 0.6),
     'L0_ffn_k_scale': (1.0, 0.6),
     'L0_ffn_ln_g': (1.0, 0.6),
     'L0_ffn_ln_b': (0.0, 0.8),
     'L0_ffn_b1': (0.0, 0.8),
     'L0_ffn_b2': (0.0, 0.1)}
    factors = {'L0_attn_dt_bias': 8.0, 'L0_attn_A_log': 8.0, 'L0_ffn_wqkv': 3.663, 'L0_ffn_wo': 3.589}
    for name, (base, spread) in spreads.items():
        noise = np.random.default_rng([zlib.crc32(name.encode()), seed]).standard_normal(out[name].shape)
        drawn = base * np.exp(spread * noise) if base else spread * noise
        out[name] = jnp.asarray(drawn.astype(out[name].dtype))
    for name, factor in factors.items():
        out[name] = (out[name] * factor).astype(out[name].dtype)
    return out
```

```python
import numpy as np
import concourse.bass as bass
from concourse import mybir
from contextlib import ExitStack

F32 = mybir.dt.float32
F32R = mybir.dt.float32r
BF16 = mybir.dt.bfloat16
ALU = mybir.AluOpType
ACT = mybir.ActivationFunctionType
AX = mybir.AxisListType

P = 128
N = 4096
DIM = 256
KT = DIM // P
HEADS, HD = 8, 64
INNER = HEADS * HD
OT = INNER // P
HID = 682
HC = -(-HID // P)
HTAIL = HID - (HC - 1) * P
LAYERS = 2
QW = 4
QUAD = QW * P
QUADS = N // QUAD
TRIPS = LAYERS * QUADS
REGION = (QUADS + 1) * QUAD
QK_SCALE = 8.0
MASKED = -1.0e30
EPS_LN = 1e-5

D_STATE = 32
ROPE_DIM = D_STATE // 2
NH = INNER // HD
D_IN = 2 * INNER + 2 * D_STATE + NH
BCDT = 2 * D_STATE + NH
EPS_SSM = 1e-6
LOG1P_TERMS = 8
DTB, NEGA, DHALF = 0, NH, 2 * NH
LNW = 3 * NH
LNBM = LNW + KT
RMSW = LNBM + KT
MSMALL = RMSW + OT

FAC = 0
B2 = FAC + 4 * HD
LG, LB = B2 + DIM, B2 + DIM + KT
B1A = LB + KT
B1G = B1A + HC
SMALL = B1G + HC


def pair_heads(hp):
    h = 4 * (hp // 2) + hp % 2
    return h, h + 2


def region_row(g):
    return (g + (g >> 3) + 1) * QUAD


def macaron_program(nc, t, blocks=(0, 1), mamba=True):
    ctx = ExitStack()
    with ctx:
        def sb(name, shape, dt=F32):
            return ctx.enter_context(nc.sbuf_tensor(name, shape, dt))

        def ps(name, cols):
            return ctx.enter_context(nc.psum_tensor(name, [P, cols], F32))

        def sem(name):
            return ctx.enter_context(nc.semaphore(name))

        ident = sb("ident", [P, P])
        ident_b = sb("ident_b", [P, P], BF16)
        mask = sb("mask", [P, 3 * 4 * P], BF16)
        halfpow = sb("halfpow", [P, 16])
        eps = sb("eps", [P, 2, QW])
        gap = sb("gap", [P, 1])
        zrow = sb("zrow", [1, DIM])
        small_raw = sb("small_raw", [P, LAYERS, SMALL])
        small = sb("small", [P, SMALL])
        wqkv_raw = sb("wqkv_raw", [P, KT, 3 * INNER])
        wo_raw = sb("wo_raw", [P, OT, DIM])
        w1_raw = sb("w1_raw", [P, KT, 2, HC * P])
        w2_raw = sb("w2_raw", [P, HC, DIM])
        wqkv = [sb(f"wqkv_{s}", [P, KT, 3 * INNER], F32R) for s in ("hi", "lo")]
        wo = [sb(f"wo_{s}", [P, OT, DIM], F32R) for s in ("hi", "lo")]
        w1 = [sb(f"w1_{s}", [P, KT, 2, HC * P], F32R) for s in ("hi", "lo")]
        w2 = [sb(f"w2_{s}", [P, HC, DIM], F32R) for s in ("hi", "lo")]
        u_in = sb("u_in", [P, QW, DIM])
        u_shift = sb("u_shift", [P, QW, P])
        rope_raw = sb("rope_raw", [P, QW, 2, 2, HD // 2])
        rope = sb("rope", [P, 2, 2, 2, HD])
        xT = [sb(f"xT_{s}", [P, DIM], F32R) for s in ("hi", "lo")]
        sq = sb("sq", [P, 2 * INNER])
        mask_f = sq[:, 0:3 * P].rearrange("p (m q) -> p m q", m=3)
        ss = sb("ss", [P, 2 * HEADS])
        ssc = sb("ssc", [P, 2 * HEADS])
        rn = sb("rn", [P, 2, 2 * HEADS])
        by_cos = sb("by_cos", [P, 2, HEADS, HD])
        by_sin = sb("by_sin", [P, 2, HEADS, HD])
        qk = sb("qk", [P, 2, HEADS, HD])
        qT = sb("qT", [P, OT, P])
        kT = sb("kT", [P, OT, QW, P])
        V = sb("V", [P, QW, INNER])
        nmraw = sb("nmraw", [P, HEADS])
        nm = sb("nm", [P, HEADS])
        probs = sb("probs", [P, 2, 2, 2 * P])
        rowsum = sb("rowsum", [P, HEADS])
        rinv = sb("rinv", [P, HEADS])
        pT = sb("pT", [P, 2, 4, P])
        o_sb = sb("o_sb", [P, HEADS, HD])
        oT = [sb(f"oT_{s}", [P, OT, P], F32R) for s in ("hi", "lo")]
        x1 = sb("x1", [P, QW, DIM])
        x1s = sb("x1s", [P, 2, 2, P])
        x1b = sb("x1b", [P, 2, DIM])
        stats = sb("stats", [P, 2, 2, 6])
        mv = sb("mv", [P, 2, 2])
        var_e = sb("var_e", [P, 2])
        rstd = sb("rstd", [P, 2])
        pT_flat = pT[:].rearrange("p s q t -> p s (q t)")
        probs_flat = probs[:].rearrange("p s h k -> p s (h k)")
        hn = pT_flat[:, 0].rearrange("p (t c) -> p t c", t=2)
        hTf = probs_flat[:, 0].rearrange("p (k t) -> p k t", k=KT)
        hT = [sb(f"hT_{s}", [P, KT, 2 * P], F32R) for s in ("hi", "lo")]
        gl = pT_flat[:, 1].rearrange("p (s t) -> p s t", s=2)
        gf = probs_flat[:, 1].rearrange("p (s t) -> p s t", s=2)
        gg = [sb(f"gg_{s}", [P, HC, 2 * P], F32R) for s in ("hi", "lo")]
        xres = sb("xres", [P, 2, 2, DIM])
        x2 = sb("x2", [P, 2, 2, DIM])
        ln_mv = sb("ln_mv", [P, QW, 2])
        ln_v = sb("ln_v", [P, QW])
        ln_r = sb("ln_r", [P, QW])
        QK = ps("QK", 1024)
        VB = ps("VB", 512)
        SC = [ps("SC0", 512), ps("SC1", 512)]
        TP = [ps("TP0", 512), ps("TP1", 512)]
        OB = ps("OB", 512)

        w_in_raw = wqkv_raw[:].rearrange("p k n -> p (k n)")[:, 0:KT * D_IN].rearrange("p (k n) -> p k n", k=KT)
        w_in = [a[:].rearrange("p k n -> p (k n)")[:, 0:KT * D_IN].rearrange("p (k n) -> p k n", k=KT) for a in wqkv]
        w_out_raw, w_out = wo_raw, wo
        tri, after, ones = u_shift[:, 0, :], u_shift[:, 1, :], u_shift[:, 2, :]
        mp = small[:, 0:MSMALL]
        xln = x1
        hm = x2[:].rearrange("p a t c -> p (a t) c")
        xsum = xres[:].rearrange("p a t c -> p (a t) c")
        u0 = w2_raw[:].rearrange("p k n -> p (k n)")[:, 0:QW * DIM].rearrange("p (t c) -> p t c", t=QW)
        kT_flat = kT[:].rearrange("p c s t -> p (c s t)")
        a_tri = kT_flat[:, 0:NH * P]
        decay = kT_flat[:, NH * P:2 * NH * P]
        V_flat = V[:].rearrange("p s c -> p (s c)")
        mT = V_flat[:, 0:NH * P]
        xc, xcd = V[:, 2, :], V[:, 3, :]
        x2h, z2h = by_cos[:, 0], by_cos[:, 1]
        ysum, dx = by_sin[:, 0], by_sin[:, 1]
        y2, yn = qk[:, 0], qk[:, 1]
        ysq = o_sb
        bcT = qT[:].rearrange("p c t -> p (c t)")[0:D_STATE, 0:2 * P]
        state = pT_flat[0:D_STATE, 0]
        scT = pT_flat[:, 1, 0:P]
        bcr = pT_flat[:, 1, P:P + 2 * D_STATE]
        bsin = pT_flat[:, 1, P + 64:P + 128]
        tbc = pT_flat[:, 1, 2 * P:2 * P + 64]
        bc2 = pT_flat[:, 1, 2 * P + 64:2 * P + 128]
        tiny = pT_flat[:, 1, 3 * P:4 * P]
        (v_, av_, e_, d_, r_, s_, s2_, p_, dt_, dth_, a_) = [tiny[:, k * NH:(k + 1) * NH] for k in range(11)]
        ex = tiny[:, 11 * NH:14 * NH]
        ssum, rms, rmsh = [tiny[:, 14 * NH + k:14 * NH + k + 1] for k in range(3)]
        s_tmp = probs_flat[0:D_STATE, 1]
        mmv = sb("mmv", [P, 2, QW, 2])
        mvar = sb("mvar", [P, 2, QW])
        mrs = sb("mrs", [P, 2, QW])

        names = """sp_steps const_loaded const_done zero_stored small_done u_loaded0 u_loaded1 u_loaded2 u_loaded3
            rope_loaded0 rope_loaded1 rope_loaded2 rope_loaded3 raw_qkv raw_o raw_1 raw_2
            wqkv_hi wqkv_ready rest_hi rest_ready 
            xT_psum xT_hi xT_lo q_proj k_proj v_proj qT_psum kT_psum qT_sb kT_sb scores probsT_psum attn_psum
            oT_psum oT_hi oT_lo wo_out x1_done sq_done ss_done rope_q rn_clip rn_done k_ready mulq mulk fold_done
            nmraw_done negmax exp_done ptA ptD v_sb rinv_done o_norm
            x1s_loaded0 x1s_loaded1 x1_stored0 x1_stored1 x1_stored2 x1_stored3
            stats_done mv_done var_done rstd_done hn_done hT_psum hT_f hT_hi hT_ready ga_psum gelu_done gf_done gg_hi gg_ready
            w2_out x1b_done x2_done xres_loaded0 xres_loaded1 out_done0 out_done1 u_stored0 u_stored1 out_stored0 out_stored1
            ln_loaded ln_stats ln_mv ln_var ln_rstd ln_done
            m_par m_par_done m_loaded m_tab m_stats m_mv m_var m_rstd m_xln m_hn m_xsum
            m_hT_psum m_hTf m_hT_hi m_hT m_b_proj m_x_proj m_z_proj m_tbc m_bmul m_bc m_v m_abs m_e m_dchain m_a
            m_tx m_tz m_x2h m_z2h m_atri m_bcT_psum m_bcT m_misc m_ex m_scT m_d m_L m_yo m_t1 m_MT m_xc m_xcd m_dx
            m_yd m_upd m_t2 m_t3 m_y2 m_sq m_rv m_rms m_yn m_stmp m_state m_yT_psum m_yT_hi m_yT m_mo m_out m_out_stored
            m_u0""".split()
        S = {}
        for nme in names:
            S[nme] = sem(nme)

        mix = (mamba and len(blocks) == 2) or blocks == ()
        LN0 = QUADS if blocks else 0
        block = ctx.enter_context(nc.Block())
        x_in, x_out = t["x_in"], t["x_out"]
        U, X1 = t["u_dram"], t["x1_dram"]

        def rows(T, row, count=P):
            return T[bass.ds(row, count), :]

        def rowtiles(T, row, tiles, c0=0, c1=DIM):
            return T[bass.ds(row, tiles * P), c0:c1].rearrange("(t p) c -> p t c", p=P)

        @block.sync
        def _(sp):
            for dst, src in ((ident[:], t["ident"]), (mask_f, t["mask"].rearrange("p (m q) -> p m q", m=3))):
                sp.dma_start(dst, src).then_inc(S["const_loaded"], 16)
            for l in range(LAYERS):
                sm = small_raw[:, l, :]
                for g, w in ((0, t["q_scale"]), (1, t["k_scale"])):
                    for cs in range(2):
                        o = FAC + (2 * g + cs) * HD
                        if cs == 0:
                            parts = ((0, 0, HD),)
                        else:
                            parts = ((0, HD // 2, HD // 2), (HD // 2, 0, HD // 2))
                        for d0, s0, n in parts:
                            sp.dma_start(sm[:, o + d0:o + d0 + n], w[l:l + 1, s0:s0 + n].to_broadcast([P, n])).then_inc(S["const_loaded"], 16)
                sp.dma_start(sm[:, B2:B2 + DIM], t["b2"][l:l + 1, :].to_broadcast([P, DIM])).then_inc(S["const_loaded"], 16)
                with nc.allow_non_contiguous_dma("parameters laid along partitions, once"):
                    for o, w in ((LG, t["ln_g"]), (LB, t["ln_b"])):
                        sp.dma_start(sm[:, o:o + KT], w[l, :].rearrange("(k p) -> p k", p=P)).then_inc(S["const_loaded"], 16)
                    for o, h in ((B1A, 0), (B1G, HID)):
                        sp.dma_start(sm[:, o:o + HC - 1], t["b1"][l, h:h + (HC - 1) * P].rearrange("(k p) -> p k", p=P)).then_inc(S["const_loaded"], 16)
            sp.wait_ge(S["const_done"], 1)
            with nc.allow_non_contiguous_dma("parameters laid along partitions, once"):
                for l in range(LAYERS):
                    for o, h in ((B1A, 0), (B1G, HID)):
                        sp.dma_start(small_raw[0:HTAIL, l, o + HC - 1:o + HC],
                                     t["b1"][l, h + (HC - 1) * P:h + HID].rearrange("(p k) -> p k", k=1)).then_inc(S["const_loaded"], 16)
            for T, n in ((U, LAYERS + 1), (X1, LAYERS)):
                for r in range(n):
                    sp.dma_start(T[r * REGION + QUAD - 1:r * REGION + QUAD, :], zrow[:]).then_inc(S["zero_stored"], 16)
            sp.wait_ge(S["zero_stored"], 16 * (2 * LAYERS + 1))

            def settle():
                sp.sem_inc(S["sp_steps"])

            def load_weights(l):
                sp.dma_start(wqkv_raw[:], t["wqkv"][l].rearrange("(k p) n -> p k n", p=P)).then_inc(S["raw_qkv"], 16)
                sp.dma_start(wo_raw[:], t["wo"][l].rearrange("(k p) n -> p k n", p=P)).then_inc(S["raw_o"], 16)
                for k in range(KT):
                    sp.dma_start(w1_raw[:, k, :, 0:HID], t["w1"][l, k * P:(k + 1) * P, :].rearrange("p (s n) -> p s n", s=2)).then_inc(S["raw_1"], 16)
                sp.dma_start(w2_raw[:, 0:HC - 1, :], t["w2"][l, 0:(HC - 1) * P, :].rearrange("(k p) n -> p k n", p=P)).then_inc(S["raw_2"], 16)
                sp.dma_start(w2_raw[0:HTAIL, HC - 1, :], t["w2"][l, (HC - 1) * P:HID, :]).then_inc(S["raw_2"], 16)

            def load_window(b, g, j):
                row = region_row(g) + j * P
                sp.dma_start(u_in[:, j, :], rows(U, row)).then_inc(S[f"u_loaded{j}"], 16)
                sp.dma_start(u_shift[:, j, :], U[bass.ds(row - 1, P), P:DIM]).then_inc(S[f"u_loaded{j}"], 16)
                sp.dma_start(rope_raw[:, j].rearrange("p a b c -> p (a b c)"),
                             t["rope"][bass.ds((g & 7) * QUAD + j * P, P), :]).then_inc(S[f"rope_loaded{j}"], 16)

            def stack(b):
                if b:
                    for name, per in (("wqkv_ready", 1), ("rest_ready", 3)):
                        sp.wait_ge(S[name], 2 * b * per)
                load_weights(0)
                src = x_in[b]
                base = 24 * b
                if b == 0:
                    with sp.Fori(0, QUADS) as g:
                        sp.wait_ge(S["ln_done"], 4 * g)
                        settle()
                        sp.dma_start(x1[:], rowtiles(src, g * QUAD, QW)).then_inc(S["ln_loaded"], 16)
                        sp.wait_ge(S["ln_done"], 4 * g + 4)
                        settle()
                        for h in range(2):
                            sp.wait_ge(S[f"u_stored{h}"], 16 * g)
                            sp.dma_start(rowtiles(U, region_row(g) + h * 2 * P, 2), u_in[:, 2 * h:2 * h + 2, :]).then_inc(S[f"u_stored{h}"], 16)
                for h in range(2):
                    sp.wait_ge(S[f"u_stored{h}"], 16 * (base + QUADS))
                for j in range(QW):
                    load_window(b, 0, j)
                for name, per in (("wqkv_ready", 1), ("rest_ready", 3)):
                    sp.wait_ge(S[name], (2 * b + 1) * per)
                load_weights(1)
                with sp.Fori(0, TRIPS) as i:
                    tokens = (i & (QUADS - 1)) * QUAD
                    for j in range(QW):
                        w = 64 * b + 4 * i + j
                        sp.wait_ge(S["x1_done"], w + 1)
                        sp.dma_start(rows(X1, region_row(i) + j * P), x1[:, j, :]).then_inc(S[f"x1_stored{j}"], 16)
                        sp.wait_ge(S[f"u_stored{j // 2}"], 16 * (base + i + 2))
                        settle()
                        sp.wait_ge(S["fold_done"], 65 * b + 4 * i + j + 1)
                        settle()
                        load_window(b, i + 1, j)
                        if j % 2:
                            h = j // 2
                            sp.wait_ge(S[f"out_stored{h}"], 16 * (16 * b + i))
                            settle()
                            sp.dma_start(xres[:, h], rowtiles(src, tokens + h * 2 * P, 2)).then_inc(S[f"xres_loaded{h}"], 16)
                            for k in (j - 1, j):
                                sp.wait_ge(S[f"x1_stored{k}"], 16 * (16 * b + i + 1))
                            sp.dma_start(x1s[:, h], rowtiles(X1, region_row(i) + h * 2 * P - 1, 2, P, DIM)).then_inc(S[f"x1s_loaded{h}"], 16)
                    for h in range(2):
                        f = 2 * (16 * b + i) + h
                        sp.wait_ge(S["x2_done"], f + 1)
                        sp.wait_ge(S[f"u_stored{h}"], 16 * (base + 8 + i))
                        settle()
                        sp.dma_start(rowtiles(U, region_row(i) + REGION + h * 2 * P, 2), x2[:, h]).then_inc(S[f"u_stored{h}"], 16)
                        sp.wait_ge(S[f"out_done{h}"], 16 * b + i + 1)
                        sp.dma_start(rowtiles(x_out[b], tokens + h * 2 * P, 2), xres[:, h]).then_inc(S[f"out_stored{h}"], 16)
                for h in range(2):
                    sp.wait_ge(S[f"out_stored{h}"], 16 * (16 * b + 16))
                    sp.wait_ge(S[f"u_stored{h}"], 16 * (base + 24))

            def state_space():
                src = t["m_in"]
                if blocks:
                    for name, per in (("wqkv_ready", 1), ("rest_ready", 3)):
                        sp.wait_ge(S[name], 2 * per)
                    sp.wait_ge(S["k_ready"], 65)
                    sp.wait_ge(S["xT_lo"], 65)
                    sp.wait_ge(S["v_proj"], 65)
                    sp.wait_ge(S["w2_out"], 32)
                    for h in range(2):
                        sp.wait_ge(S[f"out_stored{h}"], 16 * 16)
                    for j in range(QW):
                        sp.wait_ge(S[f"u_loaded{j}"], 32 * 17)
                        sp.wait_ge(S[f"rope_loaded{j}"], 16 * 17)
                sp.dma_start(w_in_raw, t["w_in"].rearrange("(k p) n -> p k n", p=P)).then_inc(S["m_par"], 16)
                sp.dma_start(w_out_raw[:], t["w_out"].rearrange("(k p) n -> p k n", p=P)).then_inc(S["m_par"], 16)
                for dst, name in ((tri, "tri"), (after, "after"), (ones, "ones")):
                    sp.dma_start(dst, t[name]).then_inc(S["m_par"], 16)
                for o, name in ((DTB, "dt_bias"), (NEGA, "A_log"), (DHALF, "D")):
                    sp.dma_start(small[:, o:o + NH], t[name].rearrange("(a n) -> a n", a=1).to_broadcast([P, NH])).then_inc(S["m_par"], 16)
                with nc.allow_non_contiguous_dma("parameters laid along partitions, once"):
                    for o, n, name in ((LNW, KT, "m_ln_w"), (LNBM, KT, "m_ln_b"), (RMSW, OT, "rms_w")):
                        sp.dma_start(small[:, o:o + n], t[name].rearrange("(k p) -> p k", p=P)).then_inc(S["m_par"], 16)

                def load_first():
                    sp.dma_start(u_in[:], rowtiles(src, 0, QW)).then_inc(S["m_loaded"], 16)
                    sp.dma_start(rope_raw[:].rearrange("p w a b c -> p w (a b c)")[:, :, 0:2 * D_STATE],
                                 t["m_rope"][0:QUAD, :].rearrange("(t p) c -> p t c", p=P)).then_inc(S["m_tab"], 16)

                load_first()
                with sp.Fori(0, QUADS) as q:
                    following = ((q + 1) & (QUADS - 1)) * QUAD
                    sp.wait_ge(S["m_xsum"], q + 1)
                    settle()
                    sp.dma_start(u_in[:], rowtiles(src, following, QW)).then_inc(S["m_loaded"], 16)
                    sp.wait_ge(S["m_bmul"], 4 * q + 4)
                    sp.dma_start(rope_raw[:].rearrange("p w a b c -> p w (a b c)")[:, :, 0:2 * D_STATE],
                                 t["m_rope"][bass.ds(following, QUAD), :].rearrange("(t p) c -> p t c", p=P)).then_inc(S["m_tab"], 16)
                    sp.wait_ge(S["m_out"], 4 * q + 4)
                    sp.dma_start(rowtiles(t["m_out"], q * QUAD, QW), xsum).then_inc(S["m_out_stored"], 16)
                    sp.wait_ge(S["m_u0"], q + 1)
                    for h in range(2):
                        sp.wait_ge(S[f"u_stored{h}"], 16 * (24 * len(blocks[:1]) + q))
                        settle()
                        sp.dma_start(rowtiles(U, region_row(q) + h * 2 * P, 2), u0[:, 2 * h:2 * h + 2, :]).then_inc(S[f"u_stored{h}"], 16)
                sp.wait_ge(S["m_out_stored"], 16 * QUADS)
                sp.wait_ge(S["m_loaded"], 16 * (QUADS + 1))
                sp.wait_ge(S["m_tab"], 16 * (QUADS + 1))
                sp.wait_ge(S["m_bmul"], 33)
                sp.wait_ge(S["m_z2h"], 33)
                sp.wait_ge(S["m_xsum"], QUADS + 1)

            for b in blocks:
                stack(b)
                if b == 0 and mix:
                    state_space()
            if not blocks:
                state_space()

        @block.tensor
        def _(pe):
            def split_product(out, left, right, first, last):
                ins = None
                for n, (a, c) in enumerate(((0, 0), (0, 1), (1, 0))):
                    ins = nc.tensor.matmul(out, left[a], right[c], start=(first and n == 0), stop=(last and n == 2))
                return ins

            def project(x, part, out, done):
                for k in range(KT):
                    ins = split_product(out, [a[:, k * P:(k + 1) * P] for a in xT],
                                        [a[:, k, part * INNER:(part + 1) * INNER] for a in wqkv], k == 0, k == KT - 1)
                ins.then_inc(S[done], 1)

            def transpose_o(w, v_count):
                pe.wait_ge(S["o_norm"], w + 1)
                pe.wait_ge(S["v_sb"], v_count)
                for c in range(OT):
                    ins = nc.tensor.transpose(VB[:, c * P:(c + 1) * P],
                                              o_sb[:, 2 * c:2 * c + 2, :].rearrange("p h d -> p (h d)"), ident[:])
                ins.then_inc(S["oT_psum"], 1)

            def out_project(w):
                pe.wait_ge(S["oT_lo"], w + 1)
                for c in range(OT):
                    ins = split_product(OB[:, 0:DIM], [a[:, c, :] for a in oT], [a[:, c, :] for a in wo],
                                        c == 0, c == OT - 1)
                ins.then_inc(S["wo_out"], 1)

            def stack(b):
                pe.wait_ge(S["wqkv_ready"], 2 * b + 1)
                x = 65 * b
                if b:
                    pe.wait_ge(S["x2_done"], 32 * b)
                pe.wait_ge(S["u_loaded0"], 32 * (17 * b + 1))
                nc.tensor.transpose(OB[:, DIM:DIM + P], u_in[:, 0, 0:P], ident[:])
                nc.tensor.transpose(OB[:, DIM + P:2 * DIM], u_shift[:, 0, :], ident[:]).then_inc(S["xT_psum"], 1)
                pe.wait_ge(S["xT_lo"], x + 1)
                project(x, 0, QK[:, 0:INNER], "q_proj")
                project(x, 1, QK[:, INNER:2 * INNER], "k_proj")
                project(x, 2, VB[:], "v_proj")
                with pe.Fori(0, TRIPS) as i:
                    for j in range(QW):
                        attention(b, i, j)
                    feed_forward(b, i)

            def attention(b, i, j):
                w = 64 * b + 4 * i + j
                x = 65 * b + 4 * i + j + 1
                nj = (j + 1) % QW
                pe.wait_ge(S["sq_done"], 2 * x)
                pe.wait_ge(S["rope_q"], x)
                for c in range(OT):
                    ins = nc.tensor.transpose(QK[:, c * P:(c + 1) * P],
                                              qk[:, 0, 2 * c:2 * c + 2, :].rearrange("p h d -> p (h d)"), ident[:])
                ins.then_inc(S["qT_psum"], 1)
                pe.wait_ge(S["k_ready"], x)
                for c in range(OT):
                    ins = nc.tensor.transpose(QK[:, INNER + c * P:INNER + (c + 1) * P],
                                              qk[:, 1, 2 * c:2 * c + 2, :].rearrange("p h d -> p (h d)"), ident[:])
                ins.then_inc(S["kT_psum"], 1)
                pe.wait_ge(S["qT_sb"], w + 1)
                pe.wait_ge(S["kT_sb"], w + 1)

                def score(hp):
                    bank = SC[hp % 2]
                    if j == 0:
                        first = ((i & 7) + 7) >> 3
                        m = mask[:, bass.ds(first * (4 * P), 4 * P)]
                        both = slice(0, QW, QW - 1)
                    else:
                        m = mask[:, 8 * P:12 * P]
                        both = slice(j - 1, j + 1)
                    nc.tensor.matmul(bank[:], ident_b[:], m, start=True, stop=False, skip_group_check=True)
                    for hh, h in enumerate(pair_heads(hp)):
                        r = slice((h % 2) * HD, (h % 2 + 1) * HD)
                        ins = nc.tensor.matmul(bank[:, hh * 2 * P:(hh + 1) * 2 * P], qT[r, h // 2, :], kT[r, h // 2, both, :],
                                               start=False, stop=True, skip_group_check=True)
                    ins.then_inc(S["scores"], 1)

                def probs_T(hp):
                    pe.wait_ge(S["exp_done"], 4 * w + hp + 1)
                    for q in range(4):
                        ins = nc.tensor.transpose(TP[hp % 2][:, q * P:(q + 1) * P],
                                                  probs[:, hp % 2, q // 2, (q % 2) * P:(q % 2 + 1) * P], ident[:])
                    ins.then_inc(S["probsT_psum"], 1)

                def weigh(hp):
                    if hp % 2:
                        pe.wait_ge(S["ptD"], 2 * w + hp // 2 + 1)
                    else:
                        pe.wait_ge(S["ptA"], 2 * w + hp // 2 + 1)
                    if hp == 0:
                        pe.wait_ge(S["v_sb"], x)
                        pe.wait_ge(S["x1_done"], w)
                    for hh, h in enumerate(pair_heads(hp)):
                        for s in range(2):
                            slot = (0, QW - 1)[s] if j == 0 else j - 1 + s
                            ins = nc.tensor.matmul(OB[:, h * HD:(h + 1) * HD], pT[:, hp % 2, 2 * hh + s, :],
                                                   V[:, slot, h * HD:(h + 1) * HD], start=(s == 0), stop=(s == 1))
                    if hp == OT - 1:
                        ins.then_inc(S["attn_psum"], 1)

                score(0)
                if j == 0:
                    pe.wait_ge(S["x2_done"], 2 * (16 * b + i))
                pe.wait_ge(S["o_norm"], w)
                u_count = 17 * b + i + (2 if nj == 0 else 1)
                pe.wait_ge(S[f"u_loaded{nj}"], 32 * u_count)
                nc.tensor.transpose(OB[:, DIM:DIM + P], u_in[:, nj, 0:P], ident[:])
                nc.tensor.transpose(OB[:, DIM + P:2 * DIM], u_shift[:, nj, :], ident[:]).then_inc(S["xT_psum"], 1)
                score(1)
                if j:
                    transpose_o(w - 1, x)
                pe.wait_ge(S["xT_lo"], x + 1)
                if j == QW - 1:
                    pe.wait_ge(S["wqkv_ready"], 2 * b + 1 + (((i + 1) >> 3) & 1))
                project(x, 0, QK[:, 0:INNER], "q_proj")
                if j:
                    if j == 1:
                        pe.wait_ge(S["rest_ready"], 3 * (2 * b + (i >> 3)) + 1)
                    out_project(w - 1)
                project(x, 1, QK[:, INNER:2 * INNER], "k_proj")
                probs_T(0)
                score(2)
                probs_T(1)
                weigh(0)
                score(3)
                project(x, 2, VB[:], "v_proj")
                probs_T(2)
                weigh(1)
                probs_T(3)
                weigh(2)
                weigh(3)

            def feed_forward(b, i):
                w3 = 64 * b + 4 * i + 3
                for h in range(2):
                    f = 2 * (16 * b + i) + h
                    pe.wait_ge(S["hn_done"], f + 1)
                    for k in range(KT):
                        for tt in range(2):
                            ins = nc.tensor.transpose(TP[0][:, (2 * k + tt) * P:(2 * k + tt + 1) * P],
                                                      hn[:, tt, k * P:(k + 1) * P], ident[:])
                    ins.then_inc(S["hT_psum"], 1)
                    ring = [SC[0], SC[1], TP[1]]
                    for c in range(HC):
                        if h == 0 and c == 0:
                            pe.wait_ge(S["rest_ready"], 3 * (2 * b + (i >> 3)) + 2)
                        if c == 0:
                            pe.wait_ge(S["hT_ready"], f + 1)
                        if c >= 3:
                            pe.wait_ge(S["gf_done"], 6 * f + c - 2)
                        for part, s in ((0, 1), (1, 0)):
                            for k in range(KT):
                                ins = split_product(ring[c % 3][:, part * 2 * P:(part + 1) * 2 * P],
                                                    [a[:, k, s, c * P:(c + 1) * P] for a in w1],
                                                    [a[:, k, :] for a in hT], k == 0, k == KT - 1)
                        ins.then_inc(S["ga_psum"], 1)
                        if h == 0 and c == 0:
                            transpose_o(w3, 65 * b + 4 * i + 5)
                        if h == 0 and c == 1:
                            if True:
                                out_project(w3)
                    if h == 0:
                        pe.wait_ge(S["x1_done"], w3 + 1)
                    else:
                        pe.wait_ge(S["x2_done"], f)
                    pe.wait_ge(S["rest_ready"], 3 * (2 * b + (i >> 3)) + 3)
                    for tt in range(2):
                        for c in range(HC):
                            pe.wait_ge(S["gg_ready"], 6 * f + c + 1)
                            ins = split_product(OB[:, tt * DIM:(tt + 1) * DIM],
                                                [a[:, c, tt * P:(tt + 1) * P] for a in gg],
                                                [a[:, c, :] for a in w2], c == 0, c == HC - 1)
                    ins.then_inc(S["w2_out"], 1)

            def state_space():
                def transpose_h(x, slot, quad):
                    pe.wait_ge(S["m_hn"], quad)
                    for k in range(KT):
                        ins = nc.tensor.transpose(TP[0][:, k * P:(k + 1) * P], hm[:, slot, k * P:(k + 1) * P], ident[:])
                    ins.then_inc(S["m_hT_psum"], 1)

                def in_project(x):
                    pe.wait_ge(S["m_hT"], x + 1)
                    for out, c0, n, done in ((VB[:, 0:BCDT], 2 * INNER, BCDT, "m_b_proj"),
                                             (QK[:, INNER:2 * INNER], INNER, INNER, "m_x_proj"),
                                             (QK[:, 0:INNER], 0, INNER, "m_z_proj")):
                        for k in range(KT):
                            ins = split_product(out, [a[:, k, 0:P] for a in hT], [a[:, k, c0:c0 + n] for a in w_in],
                                                k == 0, k == KT - 1)
                        ins.then_inc(S[done], 1)

                def transpose_y(m):
                    pe.wait_ge(S["m_yn"], m + 1)
                    for c in range(OT):
                        ins = nc.tensor.transpose(TP[0][:, c * P:(c + 1) * P],
                                                  yn[:, 2 * c:2 * c + 2, :].rearrange("p h d -> p (h d)"), ident[:])
                    ins.then_inc(S["m_yT_psum"], 1)

                def out_project(m):
                    pe.wait_ge(S["m_yT"], m + 1)
                    for c in range(OT):
                        ins = split_product(TP[0][:, 0:DIM], [a[:, c, :] for a in oT], [a[:, c, :] for a in w_out],
                                            c == 0, c == OT - 1)
                    ins.then_inc(S["m_mo"], 1)

                pe.wait_ge(S["m_par_done"], 2)
                transpose_h(0, 0, 1)
                in_project(0)
                with pe.Fori(0, QUADS) as q:
                    for j in range(QW):
                        m = 4 * q + j
                        x = m + 1
                        pe.wait_ge(S["m_bc"], m + 1)
                        pe.wait_ge(S["m_scT"], m)
                        nc.tensor.transpose(TP[1][0:D_STATE, 0:P], bcr[:, 0:D_STATE], ident[:])
                        nc.tensor.transpose(TP[1][0:D_STATE, P:2 * P], bcr[:, D_STATE:2 * D_STATE], ident[:]).then_inc(S["m_bcT_psum"], 1)
                        pe.wait_ge(S["m_bcT"], m + 1)
                        nc.tensor.matmul(TP[1][:, 2 * P:3 * P], bcT[:, 0:P], bcT[:, P:2 * P], start=True, stop=True)
                        pe.wait_ge(S["m_a"], m + 1)
                        for n, left in enumerate((tri, after, ones)):
                            ins = nc.tensor.matmul(TP[1][:, 3 * P + n * NH:3 * P + (n + 1) * NH], left, a_, start=True, stop=True)
                        ins.then_inc(S["m_misc"], 1)
                        pe.wait_ge(S["m_atri"], m + 1)
                        pe.wait_ge(S["m_t2"], m)
                        pe.wait_ge(S["m_state"], m + 1)
                        for n in range(2):
                            ins = nc.tensor.matmul(SC[n][:], after, a_tri[:, n * 4 * P:(n + 1) * 4 * P], start=True, stop=True)
                        ins.then_inc(S["m_d"], 1)
                        pe.wait_ge(S["m_t1"], m)
                        nc.tensor.matmul(OB[:], bcT[:, P:2 * P], state, start=True, stop=True).then_inc(S["m_yo"], 1)
                        pe.wait_ge(S["m_out"], m if j == 0 else m - 1)
                        transpose_h(x, (j + 1) % QW, q + (2 if j == QW - 1 else 1))
                        pe.wait_ge(S["m_x2h"], x)
                        pe.wait_ge(S["m_z2h"], x)
                        in_project(x)
                        if j:
                            transpose_y(m - 1)
                        pe.wait_ge(S["m_MT"], m + 1)
                        for h in range(NH):
                            ins = nc.tensor.matmul(SC[0][:, h * HD:(h + 1) * HD], mT[:, h * P:(h + 1) * P],
                                                   xc[:, h * HD:(h + 1) * HD], start=True, stop=True)
                        ins.then_inc(S["m_yd"], 1)
                        pe.wait_ge(S["m_xcd"], m + 1)
                        nc.tensor.matmul(SC[1][0:D_STATE, :], bcr[:, 0:D_STATE], xcd, start=True, stop=True).then_inc(S["m_upd"], 1)
                        if j:
                            out_project(m - 1)
                        if j == QW - 1:
                            pe.wait_ge(S["m_out"], m)
                            transpose_y(m)
                            out_project(m)

            pe.wait_ge(S["const_done"], 3)
            for b in blocks:
                stack(b)
                if b == 0 and mix:
                    state_space()
            if not blocks:
                state_space()

        @block.scalar
        def _(act):
            def split_hi(raw, hi, loaded, count, done):
                act.wait_ge(S[loaded], count)
                nc.scalar.activation(hi, raw, ACT.Copy).then_inc(S[done], 1)

            def hi_qkv(n):
                split_hi(wqkv_raw[:].rearrange("p k n -> p (k n)"), wqkv[0][:].rearrange("p k n -> p (k n)"), "raw_qkv", 16 * n, "wqkv_hi")

            def hi_rest(n):
                split_hi(wo_raw[:].rearrange("p k n -> p (k n)"), wo[0][:].rearrange("p k n -> p (k n)"), "raw_o", 16 * n, "rest_hi")
                split_hi(w1_raw[:].rearrange("p k s n -> p (k s n)"), w1[0][:].rearrange("p k s n -> p (k s n)"), "raw_1", 32 * n, "rest_hi")
                split_hi(w2_raw[:].rearrange("p k n -> p (k n)"), w2[0][:].rearrange("p k n -> p (k n)"), "raw_2", 32 * n, "rest_hi")

            def xT_high(x):
                act.wait_ge(S["xT_psum"], x + 1)
                nc.scalar.activation(xT[0][:], OB[:, DIM:2 * DIM], ACT.Copy).then_inc(S["xT_hi"], 1)

            def squares(x):
                act.wait_ge(S["q_proj"], x + 1)
                act.wait_ge(S["ss_done"], x)
                nc.scalar.activation(sq[:, 0:INNER], QK[:, 0:INNER], ACT.Square).then_inc(S["sq_done"], 1)
                act.wait_ge(S["k_proj"], x + 1)
                nc.scalar.activation(sq[:, INNER:2 * INNER], QK[:, INNER:2 * INNER], ACT.Square).then_inc(S["sq_done"], 1)

            def v_out(x, slot):
                act.wait_ge(S["v_proj"], x + 1)
                nc.scalar.activation(V[:, slot, :], VB[:], ACT.Copy).then_inc(S["v_sb"], 1)

            def oT_high(w):
                act.wait_ge(S["oT_psum"], w + 1)
                nc.scalar.activation(oT[0][:].rearrange("p c t -> p (c t)"), VB[:], ACT.Copy).then_inc(S["oT_hi"], 1)

            def attention(b, i, j):
                w = 64 * b + 4 * i + j
                x = 65 * b + 4 * i + j + 1

                def exps(hp):
                    act.wait_ge(S["negmax"], 4 * w + hp + 1)
                    for hh, h in enumerate(pair_heads(hp)):
                        ins = nc.scalar.activation(probs[:, hp % 2, hh, :], SC[hp % 2][:, hh * 2 * P:(hh + 1) * 2 * P],
                                                   ACT.Exp, bias=nm[:, h:h + 1], scale=rn[:, j % 2, h:h + 1],
                                                   accum_out=rowsum[:, h:h + 1])
                    ins.then_inc(S["exp_done"], 1)

                def pT_out(hp):
                    act.wait_ge(S["probsT_psum"], 4 * w + hp + 1)
                    nc.scalar.activation(pT[:, hp % 2].rearrange("p q t -> p (q t)"), TP[hp % 2][:], ACT.Copy).then_inc(S["ptA"], 1)

                act.wait_ge(S["qT_psum"], w + 1)
                nc.scalar.activation(qT[:].rearrange("p c t -> p (c t)"), QK[:, 0:INNER], ACT.Copy).then_inc(S["qT_sb"], 1)
                exps(0)
                xT_high(x)
                exps(1)
                if j:
                    oT_high(w - 1)
                squares(x)
                pT_out(0)
                exps(2)
                exps(3)
                v_out(x, (j + 1) % QW)
                pT_out(2)

            def feed_forward(b, i):
                for h in range(2):
                    f = 2 * (16 * b + i) + h
                    act.wait_ge(S["hT_psum"], f + 1)
                    for k in range(KT):
                        ins = nc.scalar.activation(hTf[:, k, :], TP[0][:, k * 2 * P:(k + 1) * 2 * P], ACT.Identity,
                                                   bias=small[:, LB + k:LB + k + 1], scale=small[:, LG + k:LG + k + 1])
                    ins.then_inc(S["hT_f"], 1)
                    for c in range(HC):
                        act.wait_ge(S["ga_psum"], 6 * f + c + 1)
                        if c < 2:
                            act.wait_ge(S["gf_done"], 6 * f)
                        else:
                            act.wait_ge(S["gf_done"], 6 * f + c - 1)
                        nc.scalar.activation(gl[:, c % 2, :], (SC[0], SC[1], TP[1])[c % 3][:, 0:2 * P], ACT.Gelu,
                                             bias=small[:, B1G + c:B1G + c + 1]).then_inc(S["gelu_done"], 1)
                        if h == 0 and c == 0:
                            oT_high(64 * b + 4 * i + 3)

            def stack(b):
                hi_qkv(2 * b + 1)
                hi_rest(2 * b + 1)
                xT_high(65 * b)
                squares(65 * b)
                v_out(65 * b, 0)
                with act.Fori(0, TRIPS) as i:
                    for j in range(QW):
                        if j == QW - 1:
                            with act.If(i == QUADS - 1):
                                act.wait_ge(S["v_proj"], 65 * b + 32)
                                hi_qkv(2 * b + 2)
                        attention(b, i, j)
                    feed_forward(b, i)
                    with act.If(i == QUADS - 1):
                        act.wait_ge(S["w2_out"], 32 * b + 16)
                        hi_rest(2 * b + 2)

            def state_space():
                A = nc.scalar.activation
                act.wait_ge(S["m_par"], 16 * 11)

                A(w_in[0], w_in_raw, ACT.Copy)
                for c in range(OT):
                    A(w_out[0][:, c, :], w_out_raw[:, c, :], ACT.Copy, scale=small[:, RMSW + c:RMSW + c + 1])
                A(small[:, NEGA:NEGA + NH], small[:, NEGA:NEGA + NH], ACT.Exp).then_inc(S["m_par_done"], 1)

                def h_out(x):
                    act.wait_ge(S["m_hT_psum"], x + 1)
                    for k in range(KT):
                        ins = A(hTf[:, k, 0:P], TP[0][:, k * P:(k + 1) * P], ACT.Identity,
                                bias=small[:, LNBM + k:LNBM + k + 1], scale=small[:, LNW + k:LNW + k + 1])
                    ins.then_inc(S["m_hTf"], 1)

                def gates(x):
                    act.wait_ge(S["m_b_proj"], x + 1)
                    A(tbc, VB[:, 0:2 * D_STATE], ACT.Tanh, scale=0.5).then_inc(S["m_tbc"], 1)
                    act.wait_ge(S["m_v"], x + 1)
                    A(av_, v_, ACT.Abs).then_inc(S["m_abs"], 1)
                    act.wait_ge(S["m_abs"], x + 1)
                    A(e_, av_, ACT.Exp, scale=-1.0).then_inc(S["m_e"], 1)
                    act.wait_ge(S["m_x_proj"], x + 1)
                    A(sq[:, INNER:2 * INNER], QK[:, INNER:2 * INNER], ACT.Tanh, scale=0.5).then_inc(S["m_tx"], 1)
                    act.wait_ge(S["m_z_proj"], x + 1)
                    A(sq[:, 0:INNER], QK[:, 0:INNER], ACT.Tanh, scale=0.5).then_inc(S["m_tz"], 1)

                def yT_high(m):
                    act.wait_ge(S["m_yT_psum"], m + 1)
                    A(oT[0][:].rearrange("p c t -> p (c t)"), TP[0][:], ACT.Copy).then_inc(S["m_yT_hi"], 1)

                h_out(0)
                gates(0)
                with act.Fori(0, QUADS) as q:
                    for j in range(QW):
                        m = 4 * q + j
                        act.wait_ge(S["m_misc"], m + 1)
                        A(ex, TP[1][:, 3 * P:3 * P + 3 * NH], ACT.Exp).then_inc(S["m_ex"], 1)
                        act.wait_ge(S["m_d"], m + 1)
                        for n in range(2):
                            ins = A(decay[:, n * 4 * P:(n + 1) * 4 * P], SC[n][:], ACT.Exp)
                        ins.then_inc(S["m_L"], 1)
                        h_out(m + 1)
                        if j:
                            yT_high(m - 1)
                        act.wait_ge(S["m_y2"], m + 1)
                        A(ysq[:], y2, ACT.Square, accum_out=ssum).then_inc(S["m_sq"], 1)
                        gates(m + 1)
                        if j == QW - 1:
                            yT_high(m)

            act.wait_ge(S["const_done"], 3)
            for b in blocks:
                stack(b)
                if b == 0 and mix:
                    state_space()
            if not blocks:
                state_space()

        @block.vector
        def _(dve):
            V_ = nc.vector

            def split_lo(raw, pair, hi_done, n, done):
                dve.wait_ge(S[hi_done], n)
                V_.tensor_tensor(pair[1], raw, pair[0].bitcast(F32), ALU.subtract).then_inc(S[done], 1)

            def lo_qkv(n):
                split_lo(wqkv_raw[:].rearrange("p k n -> p (k n)"), [a[:].rearrange("p k n -> p (k n)") for a in wqkv], "wqkv_hi", n, "wqkv_ready")

            def lo_rest(n):
                split_lo(wo_raw[:].rearrange("p k n -> p (k n)"), [a[:].rearrange("p k n -> p (k n)") for a in wo], "rest_hi", 3 * n - 2, "rest_ready")
                split_lo(w1_raw[:].rearrange("p k s n -> p (k s n)"), [a[:].rearrange("p k s n -> p (k s n)") for a in w1], "rest_hi", 3 * n - 1, "rest_ready")
                split_lo(w2_raw[:].rearrange("p k n -> p (k n)"), [a[:].rearrange("p k n -> p (k n)") for a in w2], "rest_hi", 3 * n - 0, "rest_ready")

            def xT_low(x):
                dve.wait_ge(S["xT_hi"], x + 1)
                V_.tensor_tensor(xT[1][:], OB[:, DIM:2 * DIM], xT[0][:].bitcast(F32), ALU.subtract).then_inc(S["xT_lo"], 1)

            def rope_products(x, xs, part, done):
                dve.wait_ge(S["sq_done"], 2 * x + part + 1)
                if part == 0:
                    dve.wait_ge(S["fold_done"], x + 1)
                    dve.wait_ge(S["k_ready"], x)
                src = QK[:, part * INNER:(part + 1) * INNER].rearrange("p (h d) -> p h d", d=HD)
                H2 = HD // 2
                cos = rope[:, xs, part, 0, :].unsqueeze(1).to_broadcast([P, HEADS, HD])
                V_.tensor_tensor(by_cos[:, part], src, cos, ALU.mult)
                for o, s in ((0, H2), (H2, 0)):
                    sin = rope[:, xs, part, 1, o:o + H2].unsqueeze(1).to_broadcast([P, HEADS, H2])
                    ins = V_.tensor_tensor(by_sin[:, part, :, o:o + H2], src[:, :, s:s + H2], sin, ALU.mult)
                ins.then_inc(S[done], 1)

            def sum_squares(x):
                dve.wait_ge(S["sq_done"], 2 * x + 2)
                V_.tensor_reduce(ss[:], sq[:].rearrange("p (h d) -> p h d", d=HD), AX.X, ALU.add).then_inc(S["ss_done"], 1)
                dve.wait_ge(S["ss_done"], x + 1)
                V_.tensor_scalar(ssc[:], ss[:], 1e-24, None, ALU.max).then_inc(S["rn_clip"], 1)

            def oT_low(w):
                dve.wait_ge(S["oT_hi"], w + 1)
                V_.tensor_tensor(oT[1][:].rearrange("p c t -> p (c t)"), VB[:],
                                 oT[0][:].rearrange("p c t -> p (c t)").bitcast(F32), ALU.subtract).then_inc(S["oT_lo"], 1)

            def residual1(w, b, i, j):
                dve.wait_ge(S["wo_out"], w + 1)
                dve.wait_ge(S[f"x1_stored{j}"], 16 * (16 * b + i))
                dve.wait_ge(S["x1b_done"], 2 * (16 * b + i))
                V_.tensor_tensor(x1[:, j, :], OB[:, 0:DIM], u_in[:, j, :], ALU.add).then_inc(S["x1_done"], 1)

            def attention(b, i, j):
                w = 64 * b + 4 * i + j
                x = 65 * b + 4 * i + j + 1

                def row_max(hp):
                    dve.wait_ge(S["scores"], 4 * w + hp + 1)
                    h0, h1 = pair_heads(hp)
                    V_.tensor_reduce(nmraw[:, h0:h1 + 1:2], SC[hp % 2][:].rearrange("p (h k) -> p h k", h=2),
                                     AX.X, ALU.max, negate=True).then_inc(S["nmraw_done"], 1)
                    dve.wait_ge(S["nmraw_done"], 4 * w + hp + 1)
                    V_.tensor_tensor(nm[:, h0:h1 + 1:2], nmraw[:, h0:h1 + 1:2],
                                     rn[:, j % 2, h0:h1 + 1:2], ALU.mult).then_inc(S["negmax"], 1)

                def pT_out(hp):
                    dve.wait_ge(S["probsT_psum"], 4 * w + hp + 1)
                    V_.tensor_copy(pT[:, hp % 2].rearrange("p q t -> p (q t)"), TP[hp % 2][:]).then_inc(S["ptD"], 1)

                dve.wait_ge(S["kT_psum"], w + 1)
                if j == 0:
                    with dve.If((i & (QUADS - 1)) == 0):
                        V_.memset(kT[:, :, QW - 1, :], 0.0)
                V_.tensor_copy(kT[:, :, j, :], QK[:, INNER:2 * INNER].rearrange("p (c t) -> p c t", c=OT)).then_inc(S["kT_sb"], 1)
                row_max(0)
                xT_low(x)
                row_max(1)
                if j:
                    oT_low(w - 1)
                rope_products(x, (j + 1) % 2, 0, "mulq")
                if j:
                    residual1(w - 1, b, i, j - 1)
                rope_products(x, (j + 1) % 2, 1, "mulk")
                sum_squares(x)
                row_max(2)
                pT_out(1)
                row_max(3)
                pT_out(3)
                dve.wait_ge(S["exp_done"], 4 * w + 4)
                V_.reciprocal(rinv[:], rowsum[:]).then_inc(S["rinv_done"], 1)
                dve.wait_ge(S["attn_psum"], w + 1)
                dve.wait_ge(S["rinv_done"], w + 1)
                V_.tensor_tensor(o_sb[:], OB[:].rearrange("p (h d) -> p h d", d=HD),
                                 rinv[:].unsqueeze(2).to_broadcast([P, HEADS, HD]), ALU.mult).then_inc(S["o_norm"], 1)

            def layer_norm(b, i, h):
                f = 2 * (16 * b + i) + h
                dve.wait_ge(S[f"x1s_loaded{h}"], 16 * (16 * b + i + 1))
                for tt in range(2):
                    V_.bn_stats(stats[:, tt, 0, :], x1[:, 2 * h + tt, 0:P])
                    ins = V_.bn_stats(stats[:, tt, 1, :], x1s[:, h, tt, :])
                ins.then_inc(S["stats_done"], 1)
                dve.wait_ge(S["stats_done"], f + 1)
                V_.memset(gap[:], 0.0)
                for tt in range(2):
                    ins = V_.bn_aggr(mv[:, tt, :], stats[:, tt].rearrange("p a s -> p (a s)"))
                ins.then_inc(S["mv_done"], 1)
                dve.wait_ge(S["rstd_done"], f + 1)
                for tt in range(2):
                    for k, src in ((0, x1[:, 2 * h + tt, 0:P]), (1, x1s[:, h, tt, :])):
                        ins = V_.tensor_scalar(hn[:, tt, k * P:(k + 1) * P], src, mv[:, tt, 0:1], rstd[:, tt:tt + 1],
                                               ALU.subtract, ALU.mult)
                ins.then_inc(S["hn_done"], 1)

            def feed_forward(b, i):
                w3 = 64 * b + 4 * i + 3
                for h in range(2):
                    f = 2 * (16 * b + i) + h
                    if h == 0:
                        layer_norm(b, i, 0)
                    dve.wait_ge(S["hT_f"], f + 1)
                    V_.tensor_copy(hT[0][:], hTf).then_inc(S["hT_hi"], 1)
                    dve.wait_ge(S["hT_hi"], f + 1)
                    V_.tensor_tensor(hT[1][:], hTf, hT[0][:].bitcast(F32), ALU.subtract).then_inc(S["hT_ready"], 1)
                    for c in range(HC):
                        dve.wait_ge(S["gelu_done"], 6 * f + c + 1)
                        if c < 2:
                            dve.wait_ge(S["gg_ready"], 6 * f)
                        else:
                            dve.wait_ge(S["gg_ready"], 6 * f + c - 1)
                        V_.scalar_tensor_tensor(gf[:, c % 2, :], (SC[0], SC[1], TP[1])[c % 3][:, 2 * P:4 * P],
                                                small[:, B1A + c:B1A + c + 1], gl[:, c % 2, :],
                                                ALU.add, ALU.mult).then_inc(S["gf_done"], 1)
                        dve.wait_ge(S["gf_done"], 6 * f + c + 1)
                        V_.tensor_copy(gg[0][:, c, :], gf[:, c % 2, :]).then_inc(S["gg_hi"], 1)
                        if h == 0 and c == 0:
                            oT_low(w3)
                        if h == 0 and c == 2:
                            residual1(w3, b, i, 3)
                    if h == 0:
                        layer_norm(b, i, 1)
                    dve.wait_ge(S["w2_out"], f + 1)
                    dve.wait_ge(S["x1b_done"], f + 1)
                    dve.wait_ge(S[f"u_stored{h}"], 16 * (24 * b + 8 + i))
                    V_.tensor_tensor(x2[:, h].rearrange("p t c -> p (t c)"), OB[:], x1b[:].rearrange("p t c -> p (t c)"),
                                     ALU.add).then_inc(S["x2_done"], 1)
                    dve.wait_ge(S["x2_done"], f + 1)
                    dve.wait_ge(S[f"xres_loaded{h}"], 16 * (16 * b + i + 1))
                    V_.scalar_tensor_tensor(xres[:, h].rearrange("p t c -> p (t c)"), x2[:, h].rearrange("p t c -> p (t c)"),
                                            0.5, xres[:, h].rearrange("p t c -> p (t c)"), ALU.mult, ALU.add).then_inc(S[f"out_done{h}"], 1)

            def input_norm(b):
                with dve.Fori(0, QUADS) as g:
                    n = 8 * b + g
                    dve.wait_ge(S["ln_loaded"], 16 * (n + 1))
                    for tt in range(QW):
                        ins = V_.bn_stats(stats[:, tt // 2, tt % 2, :], x1[:, tt, :])
                    ins.then_inc(S["ln_stats"], 1)
                    dve.wait_ge(S["ln_stats"], n + 1)
                    V_.memset(gap[:], 0.0)
                    for tt in range(QW):
                        ins = V_.bn_aggr(ln_mv[:, tt, :], stats[:, tt // 2, tt % 2, :])
                    ins.then_inc(S["ln_mv"], 1)
                    dve.wait_ge(S["ln_rstd"], n + 1)
                    for h in range(2):
                        dve.wait_ge(S[f"u_stored{h}"], 16 * g)
                    for tt in range(QW):
                        V_.tensor_scalar(u_in[:, tt, :], x1[:, tt, :], ln_mv[:, tt, 0:1], ln_r[:, tt:tt + 1],
                                         ALU.subtract, ALU.mult).then_inc(S["ln_done"], 1)

            def stack(b):
                if b == 0:
                    input_norm(b)
                V_.tensor_copy(small[:], small_raw[:, 0, :]).then_inc(S["small_done"], 1)
                lo_qkv(2 * b + 1)
                lo_rest(2 * b + 1)
                xT_low(65 * b)
                rope_products(65 * b, 0, 0, "mulq")
                rope_products(65 * b, 0, 1, "mulk")
                sum_squares(65 * b)
                with dve.Fori(0, TRIPS) as i:
                    for j in range(QW):
                        if j == QW - 1:
                            with dve.If(i == QUADS - 1):
                                lo_qkv(2 * b + 2)
                                dve.wait_ge(S["fold_done"], 65 * b + 32)
                                V_.tensor_copy(small[:, FAC:B2], small_raw[:, 1, FAC:B2]).then_inc(S["small_done"], 1)
                        attention(b, i, j)
                    feed_forward(b, i)
                    with dve.If(i == QUADS - 1):
                        lo_rest(2 * b + 2)
                        V_.tensor_copy(small[:, B2:SMALL], small_raw[:, 1, B2:SMALL])

            def state_space():
                T = V_.tensor_tensor

                def heads(a):
                    return a.unsqueeze(2).to_broadcast([a.shape[0], NH, HD])

                def chain(ins, n):
                    ins.then_inc(S["m_dchain"], 1)
                    dve.wait_ge(S["m_dchain"], n)

                def norm_stats(n, src, stat, mv_done, which, first, second):
                    for tt in range(QW):
                        ins = V_.bn_stats(stats[:, tt // 2, tt % 2, :], src[:, tt, :])
                    ins.then_inc(S[stat], 1)
                    dve.wait_ge(S[stat], first)
                    V_.memset(gap[:], 0.0)
                    for tt in range(QW):
                        ins = V_.bn_aggr(mmv[:, which, tt, :], stats[:, tt // 2, tt % 2, :])
                    ins.then_inc(S[mv_done], 1)
                    dve.wait_ge(S[second], n)

                def normalise(dst, src, which, done):
                    for tt in range(QW):
                        ins = V_.tensor_scalar(dst[:, tt, :], src[:, tt, :], mmv[:, which, tt, 0:1], mrs[:, which, tt:tt + 1],
                                               ALU.subtract, ALU.mult)
                    ins.then_inc(S[done], 1)

                def norms(g):
                    dve.wait_ge(S["m_loaded"], 16 * (g + 1))
                    norm_stats(2 * g + 1, u_in, "m_stats", "m_mv", 0, 2 * g + 1, "m_rstd")
                    dve.wait_ge(S["m_xsum"], g)
                    normalise(xln, u_in, 0, "m_xln")
                    dve.wait_ge(S["m_xln"], g + 1)
                    norm_stats(2 * g + 2, xln, "m_stats", "m_mv", 1, 2 * g + 2, "m_rstd")

                def h_split(x):
                    dve.wait_ge(S["m_hTf"], x + 1)
                    V_.tensor_copy(hT[0][:, :, 0:P], hTf[:, :, 0:P]).then_inc(S["m_hT_hi"], 1)
                    dve.wait_ge(S["m_hT_hi"], x + 1)
                    T(hT[1][:, :, 0:P], hTf[:, :, 0:P], hT[0][:, :, 0:P].bitcast(F32), ALU.subtract).then_inc(S["m_hT"], 1)

                STEPS = LOG1P_TERMS + 9

                def gates(x, slot, tabs):
                    c = STEPS * x
                    dve.wait_ge(S["m_tbc"], x + 1)
                    chain(T(v_, VB[:, 2 * D_STATE:BCDT], mp[:, DTB:DTB + NH], ALU.add), c + 1)
                    dve.wait_ge(S["m_upd"], x)
                    V_.scalar_tensor_tensor(bc2, tbc, 1.0, VB[:, 0:2 * D_STATE], ALU.add, ALU.mult).then_inc(S["m_v"], 1)
                    dve.wait_ge(S["m_v"], x + 1)
                    dve.wait_ge(S["m_tab"], 16 * tabs)
                    tab = rope_raw[:].rearrange("p w a b c -> p w (a b c)")[:, slot]
                    cos, sin = tab[:, 0:D_STATE], tab[:, D_STATE:2 * D_STATE]
                    b3 = bc2.rearrange("p (g d) -> p g d", g=2)
                    T(bcr.rearrange("p (g d) -> p g d", g=2), b3, cos.unsqueeze(1).to_broadcast([P, 2, D_STATE]), ALU.mult)
                    for o in range(2):
                        ins = T(bsin.rearrange("p (g d) -> p g d", g=2)[:, :, o:ROPE_DIM:2], b3[:, :, 1 - o:ROPE_DIM:2],
                                sin[:, o:ROPE_DIM:2].unsqueeze(1).to_broadcast([P, 2, ROPE_DIM // 2]), ALU.mult)
                    ins.then_inc(S["m_bmul"], 1)
                    dve.wait_ge(S["m_bmul"], x + 1)
                    b4 = bcr.rearrange("p (g d) -> p g d", g=2)[:, :, 0:ROPE_DIM]
                    T(b4, b4, bsin.rearrange("p (g d) -> p g d", g=2)[:, :, 0:ROPE_DIM], ALU.add).then_inc(S["m_bc"], 1)
                    dve.wait_ge(S["m_e"], x + 1)
                    chain(V_.tensor_scalar(d_, e_, 2.0, None, ALU.add), c + 2)
                    chain(V_.reciprocal(r_, d_), c + 3)
                    chain(T(s_, e_, r_, ALU.mult), c + 4)
                    chain(T(s2_, s_, s_, ALU.mult), c + 5)
                    chain(V_.tensor_scalar(p_, s2_, 1.0 / (2 * LOG1P_TERMS - 1), None, ALU.mult), c + 6)
                    for n in range(LOG1P_TERMS - 2, 0, -1):
                        chain(V_.scalar_tensor_tensor(p_, p_, 1.0 / (2 * n + 1), s2_, ALU.add, ALU.mult), c + 6 + LOG1P_TERMS - 1 - n)
                    chain(V_.scalar_tensor_tensor(p_, p_, 1.0, s_, ALU.add, ALU.mult), c + LOG1P_TERMS + 5)
                    chain(V_.tensor_scalar(d_, v_, 0.0, None, ALU.max), c + LOG1P_TERMS + 6)
                    chain(V_.scalar_tensor_tensor(dt_, p_, 2.0, d_, ALU.mult, ALU.add), c + LOG1P_TERMS + 7)
                    chain(V_.tensor_scalar(dth_, dt_, 0.5, None, ALU.mult), c + LOG1P_TERMS + 8)
                    T(a_, dt_, mp[:, NEGA:NEGA + NH], ALU.mult).then_inc(S["m_a"], 1)
                    chain(V_.tensor_copy(r_, dt_), c + STEPS)
                    dve.wait_ge(S["m_tx"], x + 1)
                    dve.wait_ge(S["m_dx"], x)
                    V_.scalar_tensor_tensor(x2h.rearrange("p h d -> p (h d)"), sq[:, INNER:2 * INNER], 1.0, QK[:, INNER:2 * INNER],
                                            ALU.add, ALU.mult).then_inc(S["m_x2h"], 1)
                    dve.wait_ge(S["m_tz"], x + 1)
                    V_.scalar_tensor_tensor(z2h.rearrange("p h d -> p (h d)"), sq[:, 0:INNER], 1.0, QK[:, 0:INNER],
                                            ALU.add, ALU.mult).then_inc(S["m_z2h"], 1)

                def y_norm(m):
                    dve.wait_ge(S["m_rms"], m + 1)
                    V_.tensor_scalar(yn, y2, rmsh, None, ALU.mult).then_inc(S["m_yn"], 1)

                def yT_low(m):
                    dve.wait_ge(S["m_yT_hi"], m + 1)
                    T(oT[1][:].rearrange("p c t -> p (c t)"), TP[0][:], oT[0][:].rearrange("p c t -> p (c t)").bitcast(F32),
                      ALU.subtract).then_inc(S["m_yT"], 1)

                def output(m, j):
                    dve.wait_ge(S["m_mo"], m + 1)
                    T(xsum[:, j, :], TP[0][:, 0:DIM], xsum[:, j, :], ALU.add).then_inc(S["m_out"], 1)

                dve.wait_ge(S["m_par_done"], 1)
                V_.tensor_scalar(small[:, NEGA:NEGA + NH], small[:, NEGA:NEGA + NH], -1.0, None, ALU.mult)
                V_.tensor_scalar(small[:, DHALF:DHALF + NH], small[:, DHALF:DHALF + NH], 0.5, None, ALU.mult)
                V_.memset(state, 0.0).then_inc(S["m_state"], 1)
                T(w_in[1], w_in_raw, w_in[0].bitcast(F32), ALU.subtract)
                for c in range(OT):
                    ins = V_.scalar_tensor_tensor(w_out[1][:, c, :], w_out_raw[:, c, :], small[:, RMSW + c:RMSW + c + 1],
                                                  w_out[0][:, c, :].bitcast(F32), ALU.mult, ALU.subtract)
                ins.then_inc(S["m_par_done"], 1)
                dve.wait_ge(S["m_par_done"], 2)
                norms(0)
                normalise(hm, xln, 1, "m_hn")
                h_split(0)
                gates(0, 0, 1)
                with dve.Fori(0, QUADS) as q:
                    for j in range(QW):
                        m = 4 * q + j
                        x = m + 1
                        dve.wait_ge(S["m_bcT_psum"], m + 1)
                        V_.tensor_copy(bcT, TP[1][0:D_STATE, 0:2 * P]).then_inc(S["m_bcT"], 1)
                        dve.wait_ge(S["m_x2h"], m + 1)
                        T(xc.rearrange("p (h d) -> p h d", h=NH), x2h, heads(dth_), ALU.mult).then_inc(S["m_xc"], 1)
                        dve.wait_ge(S["m_ex"], m + 1)
                        T(scT, TP[1][:, 2 * P:3 * P], tri, ALU.mult).then_inc(S["m_scT"], 1)
                        if j == QW - 1:
                            dve.wait_ge(S["m_hT_psum"], x)
                            normalise(hm, xln, 1, "m_hn")
                        dve.wait_ge(S["m_yo"], m + 1)
                        T(ysum, OB[:].rearrange("p (h d) -> p h d", h=NH), heads(ex[:, 0:NH]), ALU.mult).then_inc(S["m_t1"], 1)
                        h_split(x)
                        dve.wait_ge(S["m_L"], m + 1)
                        dve.wait_ge(S["m_scT"], m + 1)
                        T(mT.rearrange("p (h l) -> p h l", h=NH), decay.rearrange("p (h l) -> p h l", h=NH),
                          scT.unsqueeze(1).to_broadcast([P, NH, P]), ALU.mult).then_inc(S["m_MT"], 1)
                        if j:
                            yT_low(m - 1)
                        dve.wait_ge(S["m_yd"], m + 1)
                        dve.wait_ge(S["m_t1"], m + 1)
                        T(ysum, ysum, SC[0][:].rearrange("p (h d) -> p h d", h=NH), ALU.add).then_inc(S["m_t2"], 1)
                        dve.wait_ge(S["m_t2"], m + 1)
                        dve.wait_ge(S["m_dx"], m + 1)
                        T(ysum, ysum, dx, ALU.add).then_inc(S["m_t3"], 1)
                        dve.wait_ge(S["m_t3"], m + 1)
                        T(y2, ysum, z2h, ALU.mult).then_inc(S["m_y2"], 1)
                        T(s_tmp.rearrange("p (h d) -> p h d", h=NH), state.rearrange("p (h d) -> p h d", h=NH),
                          heads(ex[0:D_STATE, 2 * NH:3 * NH]), ALU.mult).then_inc(S["m_stmp"], 1)
                        dve.wait_ge(S["m_stmp"], m + 1)
                        dve.wait_ge(S["m_upd"], m + 1)
                        T(state, s_tmp, SC[1][0:D_STATE, :], ALU.add).then_inc(S["m_state"], 1)
                        if j:
                            output(m - 1, j - 1)
                        dve.wait_ge(S["m_sq"], m + 1)
                        V_.tensor_scalar(rms, ssum, 1.0 / INNER, 4 * EPS_SSM, ALU.mult, ALU.add).then_inc(S["m_rv"], 1)
                        gates(x, (j + 1) % QW, q + (2 if j == QW - 1 else 1))
                        y_norm(m)
                        if j == 1:
                            norms(q + 1)
                        if j == QW - 1:
                            yT_low(m)
                            output(m, j)
                            dve.wait_ge(S["m_out"], 4 * q + 4)
                            for tt in range(QW):
                                ins = V_.bn_stats(stats[:, tt // 2, tt % 2, :], xsum[:, tt, :])
                            ins.then_inc(S["ln_stats"], 1)
                            dve.wait_ge(S["ln_stats"], LN0 + q + 1)
                            V_.memset(gap[:], 0.0)
                            for tt in range(QW):
                                ins = V_.bn_aggr(ln_mv[:, tt, :], stats[:, tt // 2, tt % 2, :])
                            ins.then_inc(S["ln_mv"], 1)
                            dve.wait_ge(S["ln_rstd"], LN0 + q + 1)
                            for h in range(2):
                                dve.wait_ge(S[f"u_stored{h}"], 16 * (24 * len(blocks[:1]) + q))
                            for tt in range(QW):
                                ins = V_.tensor_scalar(u0[:, tt, :], xsum[:, tt, :], ln_mv[:, tt, 0:1], ln_r[:, tt:tt + 1],
                                                       ALU.subtract, ALU.mult)
                            ins.then_inc(S["m_u0"], 1)

            V_.memset(w1_raw[:, :, :, HID:HC * P], 0.0)
            V_.memset(w2_raw[:, HC - 1, :], 0.0)
            V_.memset(zrow[:], 0.0)
            V_.memset(kT[:, :, QW - 1, :], 0.0)
            V_.memset(V[:, QW - 1, :], 0.0)
            V_.memset(halfpow[:], -0.5)
            V_.memset(eps[:, 0, :], EPS_LN)
            V_.memset(eps[:, 1, :], EPS_SSM)
            for l in range(LAYERS):
                for o in (B1A, B1G):
                    ins = V_.memset(small_raw[:, l, o + HC - 1:o + HC], 0.0)
            ins.then_inc(S["const_done"], 1)
            dve.wait_ge(S["const_loaded"], 16 * (2 + LAYERS * (6 + 1 + 2 + 2 + 2)))
            V_.tensor_copy(ident_b[:], ident[:])
            for v, order in enumerate(((0, 2), (0, 1), (1, 0))):
                for hh in range(2):
                    for s, m in enumerate(order):
                        o = (4 * v + 2 * hh + s) * P
                        V_.tensor_copy(mask[:, o:o + P], mask_f[:, m, :])
            for l in range(LAYERS):
                V_.tensor_scalar(small_raw[:, l, FAC:FAC + HD], small_raw[:, l, FAC:FAC + HD], QK_SCALE, None, ALU.mult)
                V_.tensor_scalar(small_raw[:, l, FAC + HD:FAC + HD + HD // 2], small_raw[:, l, FAC + HD:FAC + HD + HD // 2], -QK_SCALE, None, ALU.mult)
                V_.tensor_scalar(small_raw[:, l, FAC + HD + HD // 2:FAC + 2 * HD], small_raw[:, l, FAC + HD + HD // 2:FAC + 2 * HD], QK_SCALE, None, ALU.mult)
                ins = V_.tensor_scalar(small_raw[:, l, FAC + 3 * HD:FAC + 3 * HD + HD // 2], small_raw[:, l, FAC + 3 * HD:FAC + 3 * HD + HD // 2], -1.0, None, ALU.mult)
            ins.then_inc(S["const_done"], 2)
            dve.wait_ge(S["const_done"], 3)
            for b in blocks:
                stack(b)
                if b == 0 and mix:
                    state_space()
            if not blocks:
                state_space()

        @block.gpsimd
        def _(pool):
            G = nc.gpsimd
            H2 = HD // 2

            def rope_window(b, x, xs, slot, loads, factors):
                pool.wait_ge(S["small_done"], factors)
                pool.wait_ge(S[f"rope_loaded{slot}"], 16 * loads)
                for g in range(2):
                    ins = G.tensor_tensor(rope[:, xs, g].rearrange("p c (e d) -> p c e d", e=2),
                                          rope_raw[:, slot, g].unsqueeze(2).to_broadcast([P, 2, 2, H2]),
                                          small[:, FAC + 2 * g * HD:FAC + 2 * (g + 1) * HD].rearrange("p (c e d) -> p c e d", c=2, e=2), ALU.mult)
                ins.then_inc(S["fold_done"], 1)
                pool.wait_ge(S["mulq"], x + 1)
                G.tensor_tensor(qk[:, 0], by_cos[:, 0], by_sin[:, 0], ALU.add).then_inc(S["rope_q"], 1)
                pool.wait_ge(S["mulk"], x + 1)
                G.tensor_tensor(by_cos[:, 1], by_cos[:, 1], by_sin[:, 1], ALU.add)
                pool.wait_ge(S["rn_clip"], x + 1)
                G.tensor_tensor(rn[:, xs], ssc[:], halfpow[:], ALU.pow).then_inc(S["rn_done"], 1)
                pool.wait_ge(S["rn_done"], x + 1)
                G.tensor_tensor(qk[:, 1], by_cos[:, 1], rn[:, xs, HEADS:2 * HEADS].unsqueeze(2).to_broadcast([P, HEADS, HD]),
                                ALU.mult).then_inc(S["k_ready"], 1)

            def norm_root(b, i, h):
                f = 2 * (16 * b + i) + h
                pool.wait_ge(S["mv_done"], f + 1)
                G.tensor_tensor(var_e[:], mv[:, :, 1], eps[:, 0, 0:2], ALU.add).then_inc(S["var_done"], 1)
                pool.wait_ge(S["var_done"], f + 1)
                G.tensor_tensor(rstd[:], var_e[:], halfpow[:, 0:2], ALU.pow).then_inc(S["rstd_done"], 1)

            def feed_forward(b, i):
                for h in range(2):
                    f = 2 * (16 * b + i) + h
                    if h == 0:
                        norm_root(b, i, 0)
                    for c in range(HC):
                        pool.wait_ge(S["gg_hi"], 6 * f + c + 1)
                        G.tensor_tensor(gg[1][:, c, :], gf[:, c % 2, :], gg[0][:, c, :].bitcast(F32), ALU.subtract).then_inc(S["gg_ready"], 1)
                    pool.wait_ge(S["x2_done"], f)
                    pool.wait_ge(S["x1_done"], 64 * b + 4 * i + 2 * h + 2)
                    for tt in range(2):
                        ins = G.tensor_tensor(x1b[:, tt, :], x1[:, 2 * h + tt, :], small[:, B2:B2 + DIM], ALU.add)
                    ins.then_inc(S["x1b_done"], 1)
                    if h == 0:
                        norm_root(b, i, 1)

            def input_norm(b):
                with pool.Fori(0, QUADS) as g:
                    n = 8 * b + g
                    pool.wait_ge(S["ln_mv"], n + 1)
                    G.tensor_tensor(ln_v[:], ln_mv[:, :, 1], eps[:, 0, :], ALU.add).then_inc(S["ln_var"], 1)
                    pool.wait_ge(S["ln_var"], n + 1)
                    G.tensor_tensor(ln_r[:], ln_v[:], halfpow[:, 0:4], ALU.pow).then_inc(S["ln_rstd"], 1)

            def stack(b):
                if b == 0:
                    input_norm(b)
                rope_window(b, 65 * b, 0, 0, 17 * b + 1, 2 * b + 1)
                with pool.Fori(0, TRIPS) as i:
                    for j in range(QW):
                        nj = (j + 1) % QW
                        loads = 17 * b + i + 2 if nj == 0 else 17 * b + i + 1
                        factors = 2 * b + 1 + ((((i + 1) >> 3) & 1) if j == QW - 1 else (i >> 3))
                        rope_window(b, 65 * b + 4 * i + j + 1, (j + 1) % 2, nj, loads, factors)
                    feed_forward(b, i)

            def state_space():
                T = G.tensor_tensor

                def heads(a):
                    return a.unsqueeze(2).to_broadcast([P, NH, HD])

                def root(n, which, mv_n):
                    pool.wait_ge(S["m_mv"], mv_n)
                    T(mvar[:, which], mmv[:, which, :, 1], eps[:, which, :], ALU.add).then_inc(S["m_var"], 1)
                    pool.wait_ge(S["m_var"], mv_n)
                    T(mrs[:, which], mvar[:, which], halfpow[:, 0:QW], ALU.pow).then_inc(S["m_rstd"], 1)

                def sum_input():
                    T(xsum, u_in[:], xln[:], ALU.add).then_inc(S["m_xsum"], 1)

                root(0, 0, 1)
                root(0, 1, 2)
                sum_input()
                with pool.Fori(0, QUADS) as q:
                    for j in range(QW):
                        m = 4 * q + j
                        pool.wait_ge(S["m_a"], m + 1)
                        pool.wait_ge(S["m_d"], m)
                        T(a_tri.rearrange("p (h l) -> p h l", h=NH), a_.unsqueeze(2).to_broadcast([P, NH, P]),
                          tri.unsqueeze(1).to_broadcast([P, NH, P]), ALU.mult).then_inc(S["m_atri"], 1)
                        pool.wait_ge(S["m_x2h"], m + 1)
                        pool.wait_ge(S["m_t3"], m)
                        T(dx, x2h, heads(mp[:, DHALF:DHALF + NH]), ALU.mult).then_inc(S["m_dx"], 1)
                        pool.wait_ge(S["m_xc"], m + 1)
                        pool.wait_ge(S["m_ex"], m + 1)
                        T(xcd.rearrange("p (h d) -> p h d", h=NH), xc.rearrange("p (h d) -> p h d", h=NH),
                          heads(ex[:, NH:2 * NH]), ALU.mult).then_inc(S["m_xcd"], 1)
                        pool.wait_ge(S["m_rv"], m + 1)
                        T(rmsh, rms, halfpow[:, 0:1], ALU.pow).then_inc(S["m_rms"], 1)
                        if j == 1:
                            root(q + 1, 0, 2 * q + 3)
                            root(q + 1, 1, 2 * q + 4)
                    pool.wait_ge(S["ln_mv"], LN0 + q + 1)
                    G.tensor_tensor(ln_v[:], ln_mv[:, :, 1], eps[:, 0, :], ALU.add).then_inc(S["ln_var"], 1)
                    pool.wait_ge(S["ln_var"], LN0 + q + 1)
                    T(ln_r[:], ln_v[:], halfpow[:, 0:QW], ALU.pow).then_inc(S["ln_rstd"], 1)
                    pool.wait_ge(S["m_u0"], q + 1)
                    pool.wait_ge(S["m_out_stored"], 16 * (q + 1))
                    sum_input()

            pool.wait_ge(S["const_done"], 3)
            for b in blocks:
                stack(b)
                if b == 0 and mix:
                    state_space()
            if not blocks:
                state_space()


def rope_table():
    f = np.float32
    half = np.arange(0, HD, 2, dtype=f)
    inv = (f(1.0) / np.power(f(10000.0), half / f(HD))).astype(f)
    pos = np.arange(N, dtype=f)
    ang = (pos[:, None] * inv[None, :]).astype(f)
    base = ((half + f(0.4 * HD)) / f(1.4 * HD)).astype(f)
    power = ((pos - f(N // 2)) / f(P // 2)).astype(f)
    scale = np.power(base[None, :], power[:, None]).astype(f)
    c, s = np.cos(ang).astype(f), np.sin(ang).astype(f)
    return np.ascontiguousarray(np.concatenate([c * scale, s * scale, c / scale, s / scale], axis=1).astype(f))


def state_rope_table():
    f = np.float32
    inv = (f(1.0) / np.power(f(10000.0), np.arange(0, ROPE_DIM, 2, dtype=f) / f(ROPE_DIM))).astype(f)
    ang = (np.arange(N, dtype=f)[:, None] * inv[None, :]).astype(f)
    c, s = np.cos(ang).astype(f), np.sin(ang).astype(f)
    own, partner = np.full((N, D_STATE), f(0.5)), np.zeros((N, D_STATE), f)
    own[:, 0:ROPE_DIM:2], own[:, 1:ROPE_DIM:2] = f(0.5) * c, f(0.5) * c
    partner[:, 0:ROPE_DIM:2], partner[:, 1:ROPE_DIM:2] = f(-0.5) * s, f(0.5) * s
    return np.ascontiguousarray(np.concatenate([own, partner], axis=1).astype(f))


def mask_table():
    q, k = np.arange(P)[:, None], np.arange(P)[None, :]
    m = [np.where(k > q, MASKED, 0.0), np.where(k < q, MASKED, 0.0), np.full((P, P), MASKED)]
    return np.concatenate(m, axis=1).astype(np.float32)


def build(nc, arrays, blocks=(0, 1)):
    t = {}
    for name, a in arrays.items():
        t[name] = nc.dram_tensor("in_" + name, a.shape, mybir.dt.from_np(a.dtype), kind="ExternalInput").ap()
    t["u_dram"] = nc.dram_tensor("u_dram", ((LAYERS + 2) * REGION, DIM), F32, kind="Internal").ap()
    t["x1_dram"] = nc.dram_tensor("x1_dram", ((LAYERS + 1) * REGION, DIM), F32, kind="Internal").ap()
    out = nc.dram_tensor("out", (N, DIM), F32, kind="ExternalOutput").ap()
    if blocks == (0, 1):
        mid = [nc.dram_tensor(f"mid_{n}", (N, DIM), F32, kind="Internal").ap() for n in range(2)]
        t["x_in"], t["x_out"] = (t["x"], mid[1]), (mid[0], out)
        t["m_in"], t["m_out"] = mid
    else:
        t["x_in"], t["x_out"] = (t["x"],), (out,)
        t["m_in"], t["m_out"] = t["x"], out
    macaron_program(nc, t, blocks)


def host_arrays(inp):
    a = {"x": np.ascontiguousarray(inp["L0_attn_x"]).reshape(N, DIM)}
    for k in ("wqkv", "wo", "w1", "w2", "q_scale", "k_scale", "ln_g", "ln_b", "b1", "b2"):
        a[k] = np.ascontiguousarray(inp["L0_ffn_" + k])
    for k, name in (("w_in", "W_in"), ("w_out", "W_out"), ("dt_bias", "dt_bias"), ("A_log", "A_log"), ("D", "D"),
                    ("m_ln_w", "ln_w"), ("m_ln_b", "ln_b"), ("rms_w", "rms_w")):
        a[k] = np.ascontiguousarray(inp["L0_attn_" + name])
    a["m_rope"] = state_rope_table()
    a["tri"] = np.triu(np.ones((P, P), np.float32))
    a["after"] = np.tril(np.ones((P, P), np.float32), -1)
    a["ones"] = np.ones((P, P), np.float32)
    a["rope"], a["mask"], a["ident"] = rope_table(), mask_table(), np.eye(P, dtype=np.float32)
    return a


def kernel(**inputs):
    import concourse.bacc as bacc
    from concourse.bass_utils import run_bass_kernel_spmd

    nc = bacc.Bacc("TRN2", target_bir_lowering=False, num_devices=1, dynamic_dma_scratch_size=1024)
    arrays = host_arrays({k: np.asarray(v) for k, v in inputs.items()})
    build(nc, arrays)
    r = run_bass_kernel_spmd(nc, [{"in_" + k: v for k, v in arrays.items()}], core_ids=[0])
    return r.results[0]["out"].reshape(1, N, DIM)
```

```python
import numpy as np
import concourse.bass as bass
from concourse import mybir
from contextlib import ExitStack

F32 = mybir.dt.float32
F32R = mybir.dt.float32r
BF16 = mybir.dt.bfloat16
ALU = mybir.AluOpType
ACT = mybir.ActivationFunctionType
AX = mybir.AxisListType

P = 128
N = 4096
DIM = 256
KT = DIM // P
HEADS, HD = 8, 64
INNER = HEADS * HD
OT = INNER // P
HID = 682
HC = -(-HID // P)
HTAIL = HID - (HC - 1) * P
LAYERS = 2
DOWN_LAG = 5
QW = 4
QUAD = QW * P
QUADS = N // QUAD
TRIPS = LAYERS * QUADS
REGION = (QUADS + 1) * QUAD
QK_SCALE = 8.0
MASKED = -1.0e30
EPS_LN = 1e-5

D_STATE = 32
ROPE_DIM = D_STATE // 2
NH = INNER // HD
D_IN = 2 * INNER + 2 * D_STATE + NH
BCDT = 2 * D_STATE + NH
EPS_SSM = 1e-6
LOG1P_TERMS = 8
DTB, NEGA, DHALF = 0, NH, 2 * NH
LNW = 3 * NH
LNBM = LNW + KT
RMSW = LNBM + KT
MSMALL = RMSW + OT

FAC = 0
B2 = FAC + 4 * HD
LG, LB = B2 + DIM, B2 + DIM + KT
B1A = LB + KT
B1G = B1A + HC
SMALL = B1G + HC


def pair_heads(hp):
    h = 4 * (hp // 2) + hp % 2
    return h, h + 2


def region_row(g):
    return (g + (g >> 3) + 1) * QUAD


def macaron_program(nc, t, blocks=(0, 1), mamba=True):
    ctx = ExitStack()
    with ctx:
        def sb(name, shape, dt=F32):
            return ctx.enter_context(nc.sbuf_tensor(name, shape, dt))

        def ps(name, cols):
            return ctx.enter_context(nc.psum_tensor(name, [P, cols], F32))

        def sem(name):
            return ctx.enter_context(nc.semaphore(name))

        ident = sb("ident", [P, P])
        ident_b = sb("ident_b", [P, P], BF16)
        mask = sb("mask", [P, 3 * 4 * P], BF16)
        halfpow = sb("halfpow", [P, 16])
        eps = sb("eps", [P, 2, QW])
        gap = sb("gap", [P, 1])
        zrow = sb("zrow", [1, DIM])
        small_raw = sb("small_raw", [P, LAYERS, SMALL])
        small = sb("small", [P, SMALL])
        wqkv_raw = sb("wqkv_raw", [P, KT, 3 * INNER])
        wo_raw = sb("wo_raw", [P, OT, DIM])
        w1_raw = sb("w1_raw", [P, KT, 2, HC * P])
        w2_raw = sb("w2_raw", [P, HC, DIM])
        wqkv = [sb(f"wqkv_{s}", [P, KT, 3 * INNER], F32R) for s in ("hi", "lo")]
        wo = [sb(f"wo_{s}", [P, OT, DIM], F32R) for s in ("hi", "lo")]
        w1 = [sb(f"w1_{s}", [P, KT, 2, HC * P], F32R) for s in ("hi", "lo")]
        w2 = [sb(f"w2_{s}", [P, HC, DIM], F32R) for s in ("hi", "lo")]
        u_in = sb("u_in", [P, QW, DIM])
        u_shift = sb("u_shift", [P, QW, P])
        rope_raw = sb("rope_raw", [P, QW, 2, 2, HD // 2])
        rope = sb("rope", [P, 2, 2, 2, HD])
        xT = [sb(f"xT_{s}", [P, DIM], F32R) for s in ("hi", "lo")]
        sq = sb("sq", [P, 2 * INNER])
        mask_f = sq[:, 0:3 * P].rearrange("p (m q) -> p m q", m=3)
        ss = sb("ss", [P, 2 * HEADS])
        ssc = sb("ssc", [P, 2 * HEADS])
        rn = sb("rn", [P, 2, 2 * HEADS])
        by_cos = sb("by_cos", [P, 2, HEADS, HD])
        by_sin = sb("by_sin", [P, 2, HEADS, HD])
        qk = sb("qk", [P, 2, HEADS, HD])
        qT = sb("qT", [P, OT, P])
        kT = sb("kT", [P, OT, QW, P])
        V = sb("V", [P, QW, INNER])
        nmraw = sb("nmraw", [P, HEADS])
        nm = sb("nm", [P, HEADS])
        probs = sb("probs", [P, 2, 2, 2 * P])
        rowsum = sb("rowsum", [P, HEADS])
        rinv = sb("rinv", [P, HEADS])
        pT = sb("pT", [P, 2, 4, P])
        o_sb = sb("o_sb", [P, HEADS, HD])
        oT = [sb(f"oT_{s}", [P, OT, P], F32R) for s in ("hi", "lo")]
        x1 = sb("x1", [P, QW, DIM])
        x1s = sb("x1s", [P, 2, 2, P])
        stats = sb("stats", [P, 2, 2, 6])
        mv = sb("mv", [P, 2, 2])
        var_e = sb("var_e", [P, 2])
        rstd = sb("rstd", [P, 2])
        pT_flat = pT[:].rearrange("p s q t -> p s (q t)")
        probs_flat = probs[:].rearrange("p s h k -> p s (h k)")
        gl = pT_flat[:, 1].rearrange("p (s t) -> p s t", s=2)
        gf = probs_flat[:, 1].rearrange("p (s t) -> p s t", s=2)
        gg = [sb(f"gg_{s}", [P, HC, 2 * P], F32R) for s in ("hi", "lo")]
        hn_tile = sb("hn_tile", [P, 2 * DIM])
        hn = [hn_tile[:].rearrange("p (t c) -> p t c", t=2), pT_flat[:, 0].rearrange("p (t c) -> p t c", t=2)]
        hTf = [hn_tile[:].rearrange("p (k t) -> p k t", k=KT), pT_flat[:, 0].rearrange("p (k t) -> p k t", k=KT)]
        hT = [[sb(f"hT_{s}", [P, KT, 2 * P], F32R)[:] for s in ("hi", "lo")],
              [a[:].rearrange("p c t -> p (c t)").rearrange("p (k t) -> p k t", k=KT) for a in oT]]
        xres = sb("xres", [P, 2, 2, DIM])
        x2 = sb("x2", [P, 2, 2, DIM])
        ln_mv = sb("ln_mv", [P, QW, 2])
        ln_v = sb("ln_v", [P, QW])
        ln_r = sb("ln_r", [P, QW])
        QK = ps("QK", 1024)
        VB = ps("VB", 512)
        SC = [ps("SC0", 512), ps("SC1", 512)]
        TP = [ps("TP0", 512), ps("TP1", 512)]
        OB = ps("OB", 512)

        w_in_raw = wqkv_raw[:].rearrange("p k n -> p (k n)")[:, 0:KT * D_IN].rearrange("p (k n) -> p k n", k=KT)
        w_in = [a[:].rearrange("p k n -> p (k n)")[:, 0:KT * D_IN].rearrange("p (k n) -> p k n", k=KT) for a in wqkv]
        w_out_raw, w_out = wo_raw, wo
        tri, after, ones = u_shift[:, 0, :], u_shift[:, 1, :], u_shift[:, 2, :]
        mp = small[:, 0:MSMALL]
        mh, mhf = hT[0], hTf[0]
        xln = x1
        hm = x2[:].rearrange("p a t c -> p (a t) c")
        xsum = xres[:].rearrange("p a t c -> p (a t) c")
        u0 = w2_raw[:].rearrange("p k n -> p (k n)")[:, 0:QW * DIM].rearrange("p (t c) -> p t c", t=QW)
        kT_flat = kT[:].rearrange("p c s t -> p (c s t)")
        a_tri = kT_flat[:, 0:NH * P]
        decay = kT_flat[:, NH * P:2 * NH * P]
        V_flat = V[:].rearrange("p s c -> p (s c)")
        mT = V_flat[:, 0:NH * P]
        xc, xcd = V[:, 2, :], V[:, 3, :]
        x2h, z2h = by_cos[:, 0], by_cos[:, 1]
        ysum, dx = by_sin[:, 0], by_sin[:, 1]
        y2, yn = qk[:, 0], qk[:, 1]
        ysq = o_sb
        bcT = qT[:].rearrange("p c t -> p (c t)")[0:D_STATE, 0:2 * P]
        state = pT_flat[0:D_STATE, 0]
        scT = pT_flat[:, 1, 0:P]
        bcr = [pT_flat[:, 1, P:P + 2 * D_STATE], probs_flat[:, 0, 2 * D_STATE:4 * D_STATE]]
        bsin = pT_flat[:, 1, P + 64:P + 128]
        tbc = pT_flat[:, 1, 2 * P:2 * P + 64]
        bc2 = pT_flat[:, 1, 2 * P + 64:2 * P + 128]
        tiny = pT_flat[:, 1, 3 * P:4 * P]
        (v_, av_, e_, d_, r_, s_, s2_, p_, dt_, dth_, a_) = [tiny[:, k * NH:(k + 1) * NH] for k in range(11)]
        ex = [probs_flat[:, 0, k * 3 * NH:(k + 1) * 3 * NH] for k in range(2)]
        ssum, rms, rmsh = [tiny[:, 14 * NH + k:14 * NH + k + 1] for k in range(3)]
        s_tmp = probs_flat[0:D_STATE, 1]
        mmv = sb("mmv", [P, 2, QW, 2])
        mvar = sb("mvar", [P, 2, QW])
        mrs = sb("mrs", [P, 2, QW])

        names = """sp_steps const_loaded const_done zero_stored small_done u_loaded0 u_loaded1 u_loaded2 u_loaded3
            rope_loaded0 rope_loaded1 rope_loaded2 rope_loaded3 raw_qkv raw_o raw_1 raw_2
            wqkv_hi wqkv_ready rest_hi rest_ready 
            xT_psum xT_hi xT_lo q_proj k_proj v_proj qT_psum kT_psum qT_sb kT_sb scores probsT_psum attn_psum
            oT_psum oT_hi oT_lo wo_out x1_done sq_done ss_done rope_q rn_clip rn_done k_ready mulq mulk fold_done
            k_sum nmraw_done negmax exp_done ptA ptD v_sb rinv_done o_norm
            x1s_loaded0 x1s_loaded1
            stats_done mv_done var_done rstd_done hn_done hT_psum hT_f hT_hi hT_ready ga_psum gelu_done gf_done gg_hi gg_ready
            w2_out x1b_done x2_done xres_loaded0 xres_loaded1 out_done0 out_done1 u_stored0 u_stored1 out_stored0 out_stored1
            ln_loaded ln_stats ln_mv ln_var ln_rstd ln_done
            m_par m_par_done m_loaded m_tab m_stats m_mv m_var m_rstd m_xln m_hn m_xsum
            m_hT_psum m_hTf m_hT_hi m_hT m_b_proj m_x_proj m_z_proj m_tbc m_bmul m_bc m_v m_abs m_e m_dchain m_a
            m_tx m_tz m_x2h m_z2h m_atri m_bcT_psum m_bcT m_misc m_ex m_scT m_d m_L m_yo m_t1 m_MT m_xc m_xcd m_dx
            m_yd m_upd m_t2 m_t3 m_y2 m_sq m_rv m_rms m_yn m_stmp m_state m_yT_psum m_yT_hi m_yT m_mo m_out m_out_stored
            m_u0""".split()
        S = {}
        for nme in names:
            S[nme] = sem(nme)

        mix = (mamba and len(blocks) == 2) or blocks == ()
        LN0 = QUADS if blocks else 0
        block = ctx.enter_context(nc.Block())
        x_in, x_out = t["x_in"], t["x_out"]
        U = t["u_dram"]

        def rows(T, row, count=P):
            return T[bass.ds(row, count), :]

        def rowtiles(T, row, tiles, c0=0, c1=DIM):
            return T[bass.ds(row, tiles * P), c0:c1].rearrange("(t p) c -> p t c", p=P)

        @block.sync
        def _(sp):
            for dst, src in ((ident[:], t["ident"]), (mask_f, t["mask"].rearrange("p (m q) -> p m q", m=3))):
                sp.dma_start(dst, src).then_inc(S["const_loaded"], 16)
            for l in range(LAYERS):
                sm = small_raw[:, l, :]
                for g, w in ((0, t["q_scale"]), (1, t["k_scale"])):
                    for cs in range(2):
                        o = FAC + (2 * g + cs) * HD
                        if cs == 0:
                            parts = ((0, 0, HD),)
                        else:
                            parts = ((0, HD // 2, HD // 2), (HD // 2, 0, HD // 2))
                        for d0, s0, n in parts:
                            sp.dma_start(sm[:, o + d0:o + d0 + n], w[l:l + 1, s0:s0 + n].to_broadcast([P, n])).then_inc(S["const_loaded"], 16)
                sp.dma_start(sm[:, B2:B2 + DIM], t["b2"][l:l + 1, :].to_broadcast([P, DIM])).then_inc(S["const_loaded"], 16)
                with nc.allow_non_contiguous_dma("parameters laid along partitions, once"):
                    for o, w in ((LG, t["ln_g"]), (LB, t["ln_b"])):
                        sp.dma_start(sm[:, o:o + KT], w[l, :].rearrange("(k p) -> p k", p=P)).then_inc(S["const_loaded"], 16)
                    for o, h in ((B1A, 0), (B1G, HID)):
                        sp.dma_start(sm[:, o:o + HC - 1], t["b1"][l, h:h + (HC - 1) * P].rearrange("(k p) -> p k", p=P)).then_inc(S["const_loaded"], 16)
            sp.wait_ge(S["const_done"], 1)
            with nc.allow_non_contiguous_dma("parameters laid along partitions, once"):
                for l in range(LAYERS):
                    for o, h in ((B1A, 0), (B1G, HID)):
                        sp.dma_start(small_raw[0:HTAIL, l, o + HC - 1:o + HC],
                                     t["b1"][l, h + (HC - 1) * P:h + HID].rearrange("(p k) -> p k", k=1)).then_inc(S["const_loaded"], 16)
            for r in range(LAYERS + 1):
                sp.dma_start(U[r * REGION + QUAD - 1:r * REGION + QUAD, :], zrow[:]).then_inc(S["zero_stored"], 16)
            sp.wait_ge(S["zero_stored"], 16 * (LAYERS + 1))

            def settle():
                sp.sem_inc(S["sp_steps"])

            def load_weights(l):
                sp.dma_start(wqkv_raw[:], t["wqkv"][l].rearrange("(k p) n -> p k n", p=P)).then_inc(S["raw_qkv"], 16)
                sp.dma_start(wo_raw[:], t["wo"][l].rearrange("(k p) n -> p k n", p=P)).then_inc(S["raw_o"], 16)
                for k in range(KT):
                    sp.dma_start(w1_raw[:, k, :, 0:HID], t["w1"][l, k * P:(k + 1) * P, :].rearrange("p (s n) -> p s n", s=2)).then_inc(S["raw_1"], 16)
                sp.dma_start(w2_raw[:, 0:HC - 1, :], t["w2"][l, 0:(HC - 1) * P, :].rearrange("(k p) n -> p k n", p=P)).then_inc(S["raw_2"], 16)
                sp.dma_start(w2_raw[0:HTAIL, HC - 1, :], t["w2"][l, (HC - 1) * P:HID, :]).then_inc(S["raw_2"], 16)

            def load_window(b, g, j):
                row = region_row(g) + j * P
                sp.dma_start(u_in[:, j, :], rows(U, row)).then_inc(S[f"u_loaded{j}"], 16)
                sp.dma_start(u_shift[:, j, :], U[bass.ds(row - 1, P), P:DIM]).then_inc(S[f"u_loaded{j}"], 16)
                sp.dma_start(rope_raw[:, j].rearrange("p a b c -> p (a b c)"),
                             t["rope"][bass.ds((g & 7) * QUAD + j * P, P), :]).then_inc(S[f"rope_loaded{j}"], 16)

            def shift_x1(i, h):
                done = S[f"x1s_loaded{h}"]
                sp.dma_start(x1s[1:P, h], x1[0:P - 1, 2 * h:2 * h + 2, P:DIM]).then_inc(done, 16)
                if h:
                    sp.dma_start(x1s[0:1, h], x1[P - 1:P, 1:3, P:DIM]).then_inc(done, 16)
                else:
                    sp.dma_start(x1s[0:1, h, 1], x1[P - 1:P, 0, P:DIM]).then_inc(done, 16)
                    with sp.If((i & (QUADS - 1)) == 0):
                        sp.dma_start(x1s[0:1, h, 0], zrow[0:1, 0:P]).then_inc(done, 16)
                    with sp.Else():
                        sp.dma_start(x1s[0:1, h, 0], x1[P - 1:P, QW - 1, P:DIM]).then_inc(done, 16)

            def stack(b):
                if b:
                    for name, per in (("wqkv_ready", 1), ("rest_ready", 3)):
                        sp.wait_ge(S[name], 2 * b * per)
                load_weights(0)
                src = x_in[b]
                base = 24 * b
                if b == 0:
                    with sp.Fori(0, QUADS) as g:
                        sp.wait_ge(S["ln_done"], 4 * g)
                        settle()
                        sp.dma_start(x1[:], rowtiles(src, g * QUAD, QW)).then_inc(S["ln_loaded"], 16)
                        sp.wait_ge(S["ln_done"], 4 * g + 4)
                        settle()
                        for h in range(2):
                            sp.wait_ge(S[f"u_stored{h}"], 16 * g)
                            sp.dma_start(rowtiles(U, region_row(g) + h * 2 * P, 2), u_in[:, 2 * h:2 * h + 2, :]).then_inc(S[f"u_stored{h}"], 16)
                for h in range(2):
                    sp.wait_ge(S[f"u_stored{h}"], 16 * (base + QUADS))
                for j in range(QW):
                    load_window(b, 0, j)
                for name, per in (("wqkv_ready", 1), ("rest_ready", 3)):
                    sp.wait_ge(S[name], (2 * b + 1) * per)
                load_weights(1)
                with sp.Fori(0, TRIPS) as i:
                    tokens = (i & (QUADS - 1)) * QUAD
                    for j in range(QW):
                        w = 64 * b + 4 * i + j
                        sp.wait_ge(S["x1_done"], w + 1)
                        if j % 2:
                            shift_x1(i, j // 2)
                        sp.wait_ge(S[f"u_stored{j // 2}"], 16 * (base + i + 2))
                        settle()
                        sp.wait_ge(S["fold_done"], 65 * b + 4 * i + j + 1)
                        settle()
                        load_window(b, i + 1, j)
                        if j % 2:
                            h = j // 2
                            sp.wait_ge(S[f"out_stored{h}"], 16 * (16 * b + i))
                            settle()
                            sp.dma_start(xres[:, h], rowtiles(src, tokens + h * 2 * P, 2)).then_inc(S[f"xres_loaded{h}"], 16)
                    for h in range(2):
                        f = 2 * (16 * b + i) + h
                        sp.wait_ge(S["x2_done"], f + 1)
                        sp.wait_ge(S[f"u_stored{h}"], 16 * (base + 8 + i))
                        settle()
                        sp.dma_start(rowtiles(U, region_row(i) + REGION + h * 2 * P, 2), x2[:, h]).then_inc(S[f"u_stored{h}"], 16)
                        sp.wait_ge(S[f"out_done{h}"], 16 * b + i + 1)
                        sp.dma_start(rowtiles(x_out[b], tokens + h * 2 * P, 2), xres[:, h]).then_inc(S[f"out_stored{h}"], 16)
                for h in range(2):
                    sp.wait_ge(S[f"out_stored{h}"], 16 * (16 * b + 16))
                    sp.wait_ge(S[f"u_stored{h}"], 16 * (base + 24))

            def state_space():
                src = t["m_in"]
                if blocks:
                    for name, per in (("wqkv_ready", 1), ("rest_ready", 3)):
                        sp.wait_ge(S[name], 2 * per)
                    sp.wait_ge(S["k_ready"], 65)
                    sp.wait_ge(S["xT_lo"], 65)
                    sp.wait_ge(S["v_proj"], 65)
                    sp.wait_ge(S["w2_out"], 32)
                    for h in range(2):
                        sp.wait_ge(S[f"out_stored{h}"], 16 * 16)
                    for j in range(QW):
                        sp.wait_ge(S[f"u_loaded{j}"], 32 * 17)
                        sp.wait_ge(S[f"rope_loaded{j}"], 16 * 17)
                sp.dma_start(w_in_raw, t["w_in"].rearrange("(k p) n -> p k n", p=P)).then_inc(S["m_par"], 16)
                sp.dma_start(w_out_raw[:], t["w_out"].rearrange("(k p) n -> p k n", p=P)).then_inc(S["m_par"], 16)
                for dst, name in ((tri, "tri"), (after, "after"), (ones, "ones")):
                    sp.dma_start(dst, t[name]).then_inc(S["m_par"], 16)
                for o, name in ((DTB, "dt_bias"), (NEGA, "A_log"), (DHALF, "D")):
                    sp.dma_start(small[:, o:o + NH], t[name].rearrange("(a n) -> a n", a=1).to_broadcast([P, NH])).then_inc(S["m_par"], 16)
                with nc.allow_non_contiguous_dma("parameters laid along partitions, once"):
                    for o, n, name in ((LNW, KT, "m_ln_w"), (LNBM, KT, "m_ln_b"), (RMSW, OT, "rms_w")):
                        sp.dma_start(small[:, o:o + n], t[name].rearrange("(k p) -> p k", p=P)).then_inc(S["m_par"], 16)

                def load_first():
                    sp.dma_start(u_in[:], rowtiles(src, 0, QW)).then_inc(S["m_loaded"], 16)
                    sp.dma_start(rope_raw[:].rearrange("p w a b c -> p w (a b c)")[:, :, 0:2 * D_STATE],
                                 t["m_rope"][0:QUAD, :].rearrange("(t p) c -> p t c", p=P)).then_inc(S["m_tab"], 16)

                load_first()
                with sp.Fori(0, QUADS) as q:
                    following = ((q + 1) & (QUADS - 1)) * QUAD
                    sp.wait_ge(S["m_xsum"], q + 1)
                    settle()
                    sp.dma_start(u_in[:], rowtiles(src, following, QW)).then_inc(S["m_loaded"], 16)
                    sp.wait_ge(S["m_bmul"], 4 * q + 4)
                    sp.dma_start(rope_raw[:].rearrange("p w a b c -> p w (a b c)")[:, :, 0:2 * D_STATE],
                                 t["m_rope"][bass.ds(following, QUAD), :].rearrange("(t p) c -> p t c", p=P)).then_inc(S["m_tab"], 16)
                    sp.wait_ge(S["m_out"], 4 * q + 4)
                    sp.dma_start(rowtiles(t["m_out"], q * QUAD, QW), xsum).then_inc(S["m_out_stored"], 16)
                    sp.wait_ge(S["m_u0"], q + 1)
                    for h in range(2):
                        sp.wait_ge(S[f"u_stored{h}"], 16 * (24 * len(blocks[:1]) + q))
                        settle()
                        sp.dma_start(rowtiles(U, region_row(q) + h * 2 * P, 2), u0[:, 2 * h:2 * h + 2, :]).then_inc(S[f"u_stored{h}"], 16)
                sp.wait_ge(S["m_out_stored"], 16 * QUADS)
                sp.wait_ge(S["m_loaded"], 16 * (QUADS + 1))
                sp.wait_ge(S["m_tab"], 16 * (QUADS + 1))
                sp.wait_ge(S["m_bmul"], 33)
                sp.wait_ge(S["m_z2h"], 33)
                sp.wait_ge(S["m_xsum"], QUADS + 1)

            for b in blocks:
                stack(b)
                if b == 0 and mix:
                    state_space()
            if not blocks:
                state_space()

        @block.tensor
        def _(pe):
            def split_product(out, left, right, first, last):
                ins = None
                for n, (a, c) in enumerate(((0, 0), (0, 1), (1, 0))):
                    ins = nc.tensor.matmul(out, left[a], right[c], start=(first and n == 0), stop=(last and n == 2))
                return ins

            def project(x, part, out, done):
                for k in range(KT):
                    ins = split_product(out, [a[:, k * P:(k + 1) * P] for a in xT],
                                        [a[:, k, part * INNER:(part + 1) * INNER] for a in wqkv], k == 0, k == KT - 1)
                ins.then_inc(S[done], 1)

            def transpose_qk(x, part):
                pe.wait_ge(S["k_ready" if part else "rope_q"], x + 1)
                for c in range(OT):
                    o = part * INNER + c * P
                    ins = nc.tensor.transpose(QK[:, o:o + P], qk[:, part, 2 * c:2 * c + 2, :].rearrange("p h d -> p (h d)"), ident[:])
                ins.then_inc(S["kT_psum" if part else "qT_psum"], 1)

            def transpose_hidden(f, hn, bank):
                pe.wait_ge(S["hn_done"], f + 1)
                for k in range(KT):
                    for tt in range(2):
                        ins = nc.tensor.transpose(bank[:, (2 * k + tt) * P:(2 * k + tt + 1) * P], hn[:, tt, k * P:(k + 1) * P], ident[:])
                ins.then_inc(S["hT_psum"], 1)

            def transpose_o(w, v_count):
                pe.wait_ge(S["o_norm"], w + 1)
                pe.wait_ge(S["v_sb"], v_count)
                for c in range(OT):
                    ins = nc.tensor.transpose(VB[:, c * P:(c + 1) * P],
                                              o_sb[:, 2 * c:2 * c + 2, :].rearrange("p h d -> p (h d)"), ident[:])
                ins.then_inc(S["oT_psum"], 1)

            def out_project(w):
                pe.wait_ge(S["oT_lo"], w + 1)
                for c in range(OT):
                    ins = split_product(OB[:, 0:DIM], [a[:, c, :] for a in oT], [a[:, c, :] for a in wo],
                                        c == 0, c == OT - 1)
                ins.then_inc(S["wo_out"], 1)

            def stack(b):
                pe.wait_ge(S["wqkv_ready"], 2 * b + 1)
                x = 65 * b
                if b:
                    pe.wait_ge(S["x2_done"], 32 * b)
                pe.wait_ge(S["u_loaded0"], 32 * (17 * b + 1))
                nc.tensor.transpose(OB[:, DIM:DIM + P], u_in[:, 0, 0:P], ident[:])
                nc.tensor.transpose(OB[:, DIM + P:2 * DIM], u_shift[:, 0, :], ident[:]).then_inc(S["xT_psum"], 1)
                pe.wait_ge(S["xT_lo"], x + 1)
                project(x, 1, QK[:, INNER:2 * INNER], "k_proj")
                project(x, 0, QK[:, 0:INNER], "q_proj")
                project(x, 2, VB[:], "v_proj")
                transpose_qk(x, 1)
                transpose_qk(x, 0)
                with pe.Fori(0, TRIPS) as i:
                    for j in range(QW):
                        attention(b, i, j)
                    feed_forward(b, i)

            def attention(b, i, j):
                w = 64 * b + 4 * i + j
                x = 65 * b + 4 * i + j + 1
                nj = (j + 1) % QW
                def score(hp):
                    bank = SC[hp % 2]
                    if j == 0:
                        first = ((i & 7) + 7) >> 3
                        m = mask[:, bass.ds(first * (4 * P), 4 * P)]
                        both = slice(0, QW, QW - 1)
                    else:
                        m = mask[:, 8 * P:12 * P]
                        both = slice(j - 1, j + 1)
                    nc.tensor.matmul(bank[:], ident_b[:], m, start=True, stop=False, skip_group_check=True)
                    for hh, h in enumerate(pair_heads(hp)):
                        r = slice((h % 2) * HD, (h % 2 + 1) * HD)
                        ins = nc.tensor.matmul(bank[:, hh * 2 * P:(hh + 1) * 2 * P], qT[r, h // 2, :], kT[r, h // 2, both, :],
                                               start=False, stop=True, skip_group_check=True)
                    ins.then_inc(S["scores"], 1)

                def probs_T(hp):
                    pe.wait_ge(S["exp_done"], 4 * w + hp + 1)
                    for q in range(4):
                        ins = nc.tensor.transpose(TP[hp % 2][:, q * P:(q + 1) * P],
                                                  probs[:, hp % 2, q // 2, (q % 2) * P:(q % 2 + 1) * P], ident[:])
                    ins.then_inc(S["probsT_psum"], 1)

                def weigh(hp):
                    if hp % 2:
                        pe.wait_ge(S["ptD"], 2 * w + hp // 2 + 1)
                    else:
                        pe.wait_ge(S["ptA"], 2 * w + hp // 2 + 1)
                    if hp == 0:
                        pe.wait_ge(S["v_sb"], x)
                        pe.wait_ge(S["x1_done"], w)
                    for hh, h in enumerate(pair_heads(hp)):
                        for s in range(2):
                            slot = (0, QW - 1)[s] if j == 0 else j - 1 + s
                            ins = nc.tensor.matmul(OB[:, h * HD:(h + 1) * HD], pT[:, hp % 2, 2 * hh + s, :],
                                                   V[:, slot, h * HD:(h + 1) * HD], start=(s == 0), stop=(s == 1))
                    if hp == OT - 1:
                        ins.then_inc(S["attn_psum"], 1)

                def transpose_x():
                    if j == 0:
                        pe.wait_ge(S["x2_done"], 2 * (16 * b + i))
                    pe.wait_ge(S["o_norm"], w)
                    u_count = 17 * b + i + (2 if nj == 0 else 1)
                    pe.wait_ge(S[f"u_loaded{nj}"], 32 * u_count)
                    nc.tensor.transpose(OB[:, DIM:DIM + P], u_in[:, nj, 0:P], ident[:])
                    nc.tensor.transpose(OB[:, DIM + P:2 * DIM], u_shift[:, nj, :], ident[:]).then_inc(S["xT_psum"], 1)

                pe.wait_ge(S["kT_sb"], x)
                pe.wait_ge(S["qT_sb"], x)
                score(0)
                transpose_x()
                if j:
                    transpose_o(w - 1, x)
                score(1)
                pe.wait_ge(S["xT_lo"], x + 1)
                if j == QW - 1:
                    pe.wait_ge(S["wqkv_ready"], 2 * b + 1 + (((i + 1) >> 3) & 1))
                project(x, 1, QK[:, INNER:2 * INNER], "k_proj")
                if j:
                    if j == 1:
                        pe.wait_ge(S["rest_ready"], 3 * (2 * b + (i >> 3)) + 1)
                    out_project(w - 1)
                project(x, 0, QK[:, 0:INNER], "q_proj")
                probs_T(0)
                if j == QW - 1:
                    project(x, 2, VB[:], "v_proj")
                score(2)
                probs_T(1)
                weigh(0)
                score(3)
                if j == QW - 1:
                    pe.wait_ge(S["v_sb"], x + 1)
                    transpose_hidden(2 * (16 * b + i), hn[0], VB)
                else:
                    project(x, 2, VB[:], "v_proj")
                probs_T(2)
                weigh(1)
                probs_T(3)
                transpose_qk(x, 1)
                if j < QW - 1:
                    transpose_qk(x, 0)
                weigh(2)
                weigh(3)
                if j == QW - 1:
                    transpose_qk(x, 0)

            def feed_forward(b, i):
                w3 = 64 * b + 4 * i + 3
                ring = [SC[0], SC[1], TP[1]]
                for h in range(2):
                    f = 2 * (16 * b + i) + h

                    def down(tt, c):
                        if tt == 0 and c == 0:
                            if h == 0:
                                pe.wait_ge(S["x1_done"], w3 + 1)
                                pe.wait_ge(S["rest_ready"], 3 * (2 * b + (i >> 3)) + 3)
                            else:
                                pe.wait_ge(S["x2_done"], f)
                        if tt == 0:
                            pe.wait_ge(S["gg_ready"], 6 * f + c + 1)
                        return split_product(OB[:, tt * DIM:(tt + 1) * DIM],
                                             [a[:, c, tt * P:(tt + 1) * P] for a in gg],
                                             [a[:, c, :] for a in w2], c == 0, c == HC - 1)

                    pe.wait_ge(S["hT_ready"], f + 1)
                    for c in range(HC):
                        if h == 0 and c == 0:
                            pe.wait_ge(S["rest_ready"], 3 * (2 * b + (i >> 3)) + 2)
                        if c >= 3:
                            pe.wait_ge(S["gf_done"], 6 * f + c - 2)
                        for part, s in ((0, 1), (1, 0)):
                            for k in range(KT):
                                ins = split_product(ring[c % 3][:, part * 2 * P:(part + 1) * 2 * P],
                                                    [a[:, k, s, c * P:(c + 1) * P] for a in w1],
                                                    [a[:, k, :] for a in hT[h]], k == 0, k == KT - 1)
                            if h == 0 and c == 0 and part == 0:
                                pe.wait_ge(S["hT_f"], f + 1)
                                transpose_o(w3, 65 * b + 4 * i + 5)
                        ins.then_inc(S["ga_psum"], 1)
                        if h == 0 and c == 1:
                            out_project(w3)
                        if c >= DOWN_LAG:
                            down(0, c - DOWN_LAG)
                    for c in range(HC - DOWN_LAG, HC):
                        down(0, c)
                    if h == 0:
                        transpose_hidden(f + 1, hn[1], TP[0])
                    for c in range(HC):
                        ins = down(1, c)
                    ins.then_inc(S["w2_out"], 1)

            def state_space():
                def transpose_h(slot, quad):
                    pe.wait_ge(S["m_hn"], quad)
                    for k in range(KT):
                        ins = nc.tensor.transpose(TP[0][:, k * P:(k + 1) * P], hm[:, slot, k * P:(k + 1) * P], ident[:])
                    ins.then_inc(S["m_hT_psum"], 1)

                def in_project(out, c0, n, done):
                    for k in range(KT):
                        ins = split_product(out, [a[:, k, 0:P] for a in mh], [a[:, k, c0:c0 + n] for a in w_in],
                                            k == 0, k == KT - 1)
                    ins.then_inc(S[done], 1)

                def project_bcdt(x):
                    pe.wait_ge(S["m_hT"], x + 1)
                    in_project(VB[:, 0:BCDT], 2 * INNER, BCDT, "m_b_proj")

                def transpose_bc(x, s):
                    pe.wait_ge(S["m_bc"], x + 1)
                    pe.wait_ge(S["m_scT"], x)
                    pe.wait_ge(S["m_ex"], x)
                    nc.tensor.transpose(TP[1][0:D_STATE, 0:P], bcr[s][:, 0:D_STATE], ident[:])
                    nc.tensor.transpose(TP[1][0:D_STATE, P:2 * P], bcr[s][:, D_STATE:2 * D_STATE], ident[:]).then_inc(S["m_bcT_psum"], 1)

                def sums(x):
                    pe.wait_ge(S["m_bcT"], x + 1)
                    nc.tensor.matmul(TP[1][:, 2 * P:3 * P], bcT[:, 0:P], bcT[:, P:2 * P], start=True, stop=True)
                    pe.wait_ge(S["m_a"], x + 1)
                    for n, left in enumerate((tri, after, ones)):
                        ins = nc.tensor.matmul(TP[1][:, 3 * P + n * NH:3 * P + (n + 1) * NH], left, a_, start=True, stop=True)
                    ins.then_inc(S["m_misc"], 1)

                def segment_sums(x):
                    pe.wait_ge(S["m_atri"], x + 1)
                    pe.wait_ge(S["m_L"], x)
                    for n in range(2):
                        ins = nc.tensor.matmul(SC[n][:], after, a_tri[:, n * 4 * P:(n + 1) * 4 * P], start=True, stop=True)
                    ins.then_inc(S["m_d"], 1)

                def transpose_y(m):
                    pe.wait_ge(S["m_yn"], m + 1)
                    for c in range(OT):
                        ins = nc.tensor.transpose(TP[0][:, c * P:(c + 1) * P],
                                                  yn[:, 2 * c:2 * c + 2, :].rearrange("p h d -> p (h d)"), ident[:])
                    ins.then_inc(S["m_yT_psum"], 1)

                def out_project(m):
                    pe.wait_ge(S["m_yT"], m + 1)
                    for c in range(OT):
                        ins = split_product(TP[0][:, 0:DIM], [a[:, c, :] for a in oT], [a[:, c, :] for a in w_out],
                                            c == 0, c == OT - 1)
                    ins.then_inc(S["m_mo"], 1)

                pe.wait_ge(S["m_par_done"], 2)
                transpose_h(0, 1)
                project_bcdt(0)
                in_project(QK[:, INNER:2 * INNER], INNER, INNER, "m_x_proj")
                in_project(QK[:, 0:INNER], 0, INNER, "m_z_proj")
                transpose_bc(0, 0)
                sums(0)
                segment_sums(0)
                transpose_h(1, 1)
                with pe.Fori(0, QUADS) as q:
                    for j in range(QW):
                        m = 4 * q + j
                        x = m + 1
                        pe.wait_ge(S["m_t2"], m)
                        project_bcdt(x)
                        pe.wait_ge(S["m_x2h"], x)
                        in_project(QK[:, INNER:2 * INNER], INNER, INNER, "m_x_proj")
                        pe.wait_ge(S["m_out"], m if j == 0 else m - 1)
                        if j:
                            transpose_y(m - 1)
                        pe.wait_ge(S["m_z2h"], x)
                        in_project(QK[:, 0:INNER], 0, INNER, "m_z_proj")
                        pe.wait_ge(S["m_state"], m + 1)
                        nc.tensor.matmul(OB[:], bcT[:, P:2 * P], state, start=True, stop=True).then_inc(S["m_yo"], 1)
                        pe.wait_ge(S["m_v"], x + 1)
                        pe.wait_ge(S["m_MT"], m + 1)
                        pe.wait_ge(S["m_xc"], m + 1)
                        for h in range(NH):
                            ins = nc.tensor.matmul(VB[:, h * HD:(h + 1) * HD], mT[:, h * P:(h + 1) * P],
                                                   xc[:, h * HD:(h + 1) * HD], start=True, stop=True)
                        ins.then_inc(S["m_yd"], 1)
                        transpose_bc(x, (j + 1) % 2)
                        if j:
                            out_project(m - 1)
                        sums(x)
                        pe.wait_ge(S["m_t1"], m + 1)
                        pe.wait_ge(S["m_xcd"], m + 1)
                        nc.tensor.matmul(OB[0:D_STATE, :], bcr[j % 2][:, 0:D_STATE], xcd, start=True, stop=True).then_inc(S["m_upd"], 1)
                        segment_sums(x)
                        pe.wait_ge(S["m_out"], m)
                        transpose_h((j + 2) % QW, q + (2 if j >= QW - 2 else 1))
                        if j == QW - 1:
                            pe.wait_ge(S["m_hTf"], m + 3)
                            transpose_y(m)
                            out_project(m)

            pe.wait_ge(S["const_done"], 3)
            for b in blocks:
                stack(b)
                if b == 0 and mix:
                    state_space()
            if not blocks:
                state_space()

        @block.scalar
        def _(act):
            def split_hi(raw, hi, loaded, count, done):
                act.wait_ge(S[loaded], count)
                nc.scalar.activation(hi, raw, ACT.Copy).then_inc(S[done], 1)

            def hi_qkv(n):
                split_hi(wqkv_raw[:].rearrange("p k n -> p (k n)"), wqkv[0][:].rearrange("p k n -> p (k n)"), "raw_qkv", 16 * n, "wqkv_hi")

            def hi_rest(n):
                split_hi(wo_raw[:].rearrange("p k n -> p (k n)"), wo[0][:].rearrange("p k n -> p (k n)"), "raw_o", 16 * n, "rest_hi")
                split_hi(w1_raw[:].rearrange("p k s n -> p (k s n)"), w1[0][:].rearrange("p k s n -> p (k s n)"), "raw_1", 32 * n, "rest_hi")
                split_hi(w2_raw[:].rearrange("p k n -> p (k n)"), w2[0][:].rearrange("p k n -> p (k n)"), "raw_2", 32 * n, "rest_hi")

            def xT_high(x):
                act.wait_ge(S["xT_psum"], x + 1)
                nc.scalar.activation(xT[0][:], OB[:, DIM:2 * DIM], ACT.Copy).then_inc(S["xT_hi"], 1)

            def squares(x):
                act.wait_ge(S["k_proj"], x + 1)
                act.wait_ge(S["ss_done"], 2 * x)
                nc.scalar.activation(sq[:, INNER:2 * INNER], QK[:, INNER:2 * INNER], ACT.Square).then_inc(S["sq_done"], 1)
                act.wait_ge(S["q_proj"], x + 1)
                nc.scalar.activation(sq[:, 0:INNER], QK[:, 0:INNER], ACT.Square).then_inc(S["sq_done"], 1)

            def qT_out(x):
                act.wait_ge(S["qT_psum"], x + 1)
                nc.scalar.activation(qT[:].rearrange("p c t -> p (c t)"), QK[:, 0:INNER], ACT.Copy).then_inc(S["qT_sb"], 1)

            def v_out(x, slot):
                act.wait_ge(S["v_proj"], x + 1)
                nc.scalar.activation(V[:, slot, :], VB[:], ACT.Copy).then_inc(S["v_sb"], 1)

            def oT_high(w):
                act.wait_ge(S["oT_psum"], w + 1)
                nc.scalar.activation(oT[0][:].rearrange("p c t -> p (c t)"), VB[:], ACT.Copy).then_inc(S["oT_hi"], 1)

            def attention(b, i, j):
                w = 64 * b + 4 * i + j
                x = 65 * b + 4 * i + j + 1

                def exps(hp):
                    act.wait_ge(S["negmax"], 4 * w + hp + 1)
                    for hh, h in enumerate(pair_heads(hp)):
                        ins = nc.scalar.activation(probs[:, hp % 2, hh, :], SC[hp % 2][:, hh * 2 * P:(hh + 1) * 2 * P],
                                                   ACT.Exp, bias=nm[:, h:h + 1], scale=rn[:, j % 2, h:h + 1],
                                                   accum_out=rowsum[:, h:h + 1])
                    ins.then_inc(S["exp_done"], 1)

                def pT_out(hp):
                    act.wait_ge(S["probsT_psum"], 4 * w + hp + 1)
                    nc.scalar.activation(pT[:, hp % 2].rearrange("p q t -> p (q t)"), TP[hp % 2][:], ACT.Copy).then_inc(S["ptA"], 1)

                xT_high(x)
                if j:
                    oT_high(w - 1)
                exps(0)
                exps(1)
                squares(x)
                pT_out(0)
                if j == QW - 1:
                    v_out(x, (j + 1) % QW)
                exps(2)
                exps(3)
                pT_out(2)
                if j == QW - 1:
                    hidden_in(2 * (16 * b + i), hTf[0], VB)
                else:
                    v_out(x, (j + 1) % QW)
                qT_out(x)

            def hidden_in(f, hTf, bank):
                act.wait_ge(S["hT_psum"], f + 1)
                for k in range(KT):
                    ins = nc.scalar.activation(hTf[:, k, :], bank[:, k * 2 * P:(k + 1) * 2 * P], ACT.Identity,
                                               bias=small[:, LB + k:LB + k + 1], scale=small[:, LG + k:LG + k + 1])
                ins.then_inc(S["hT_f"], 1)

            def feed_forward(b, i):
                for h in range(2):
                    f = 2 * (16 * b + i) + h
                    if h == 0:
                        oT_high(64 * b + 4 * i + 3)
                    for c in range(HC):
                        act.wait_ge(S["ga_psum"], 6 * f + c + 1)
                        if c < 2:
                            act.wait_ge(S["gf_done"], 6 * f)
                        else:
                            act.wait_ge(S["gf_done"], 6 * f + c - 1)
                        nc.scalar.activation(gl[:, c % 2, :], (SC[0], SC[1], TP[1])[c % 3][:, 0:2 * P], ACT.Gelu,
                                             bias=small[:, B1G + c:B1G + c + 1]).then_inc(S["gelu_done"], 1)
                    if h == 0:
                        hidden_in(f + 1, hTf[1], TP[0])

            def stack(b):
                hi_qkv(2 * b + 1)
                hi_rest(2 * b + 1)
                xT_high(65 * b)
                squares(65 * b)
                v_out(65 * b, 0)
                qT_out(65 * b)
                with act.Fori(0, TRIPS) as i:
                    for j in range(QW):
                        if j == QW - 1:
                            with act.If(i == QUADS - 1):
                                act.wait_ge(S["v_proj"], 65 * b + 32)
                                hi_qkv(2 * b + 2)
                        attention(b, i, j)
                    feed_forward(b, i)
                    with act.If(i == QUADS - 1):
                        act.wait_ge(S["w2_out"], 32 * b + 16)
                        hi_rest(2 * b + 2)

            def state_space():
                A = nc.scalar.activation
                act.wait_ge(S["m_par"], 16 * 11)

                A(w_in[0], w_in_raw, ACT.Copy)
                for c in range(OT):
                    A(w_out[0][:, c, :], w_out_raw[:, c, :], ACT.Copy, scale=small[:, RMSW + c:RMSW + c + 1])
                A(small[:, NEGA:NEGA + NH], small[:, NEGA:NEGA + NH], ACT.Exp).then_inc(S["m_par_done"], 1)

                def h_out(x):
                    act.wait_ge(S["m_hT_psum"], x + 1)
                    for k in range(KT):
                        ins = A(mhf[:, k, 0:P], TP[0][:, k * P:(k + 1) * P], ACT.Identity,
                                bias=small[:, LNBM + k:LNBM + k + 1], scale=small[:, LNW + k:LNW + k + 1])
                    ins.then_inc(S["m_hTf"], 1)

                def gates_bcdt(x):
                    act.wait_ge(S["m_b_proj"], x + 1)
                    A(tbc, VB[:, 0:2 * D_STATE], ACT.Tanh, scale=0.5).then_inc(S["m_tbc"], 1)
                    act.wait_ge(S["m_v"], x + 1)
                    A(av_, v_, ACT.Abs).then_inc(S["m_abs"], 1)
                    act.wait_ge(S["m_abs"], x + 1)
                    A(e_, av_, ACT.Exp, scale=-1.0).then_inc(S["m_e"], 1)

                def gates_xz(x):
                    act.wait_ge(S["m_x_proj"], x + 1)
                    A(sq[:, INNER:2 * INNER], QK[:, INNER:2 * INNER], ACT.Tanh, scale=0.5).then_inc(S["m_tx"], 1)
                    act.wait_ge(S["m_z_proj"], x + 1)
                    A(sq[:, 0:INNER], QK[:, 0:INNER], ACT.Tanh, scale=0.5).then_inc(S["m_tz"], 1)

                def yT_high(m):
                    act.wait_ge(S["m_yT_psum"], m + 1)
                    A(oT[0][:].rearrange("p c t -> p (c t)"), TP[0][:], ACT.Copy).then_inc(S["m_yT_hi"], 1)

                def decays(x, s):
                    act.wait_ge(S["m_misc"], x + 1)
                    A(ex[s], TP[1][:, 3 * P:3 * P + 3 * NH], ACT.Exp).then_inc(S["m_ex"], 1)
                    act.wait_ge(S["m_MT"], x)
                    act.wait_ge(S["m_d"], x + 1)
                    for n in range(2):
                        ins = A(decay[:, n * 4 * P:(n + 1) * 4 * P], SC[n][:], ACT.Exp)
                    ins.then_inc(S["m_L"], 1)

                h_out(0)
                gates_bcdt(0)
                gates_xz(0)
                decays(0, 0)
                h_out(1)
                with act.Fori(0, QUADS) as q:
                    for j in range(QW):
                        m = 4 * q + j
                        x = m + 1
                        gates_bcdt(x)
                        if j:
                            yT_high(m - 1)
                        gates_xz(x)
                        act.wait_ge(S["m_y2"], m + 1)
                        A(ysq[:], y2, ACT.Square, accum_out=ssum).then_inc(S["m_sq"], 1)
                        decays(x, (j + 1) % 2)
                        h_out(m + 2)
                        if j == QW - 1:
                            yT_high(m)

            act.wait_ge(S["const_done"], 3)
            for b in blocks:
                stack(b)
                if b == 0 and mix:
                    state_space()
            if not blocks:
                state_space()

        @block.vector
        def _(dve):
            V_ = nc.vector

            def split_lo(raw, pair, hi_done, n, done):
                dve.wait_ge(S[hi_done], n)
                V_.tensor_tensor(pair[1], raw, pair[0].bitcast(F32), ALU.subtract).then_inc(S[done], 1)

            def lo_qkv(n):
                split_lo(wqkv_raw[:].rearrange("p k n -> p (k n)"), [a[:].rearrange("p k n -> p (k n)") for a in wqkv], "wqkv_hi", n, "wqkv_ready")

            def lo_rest(n):
                split_lo(wo_raw[:].rearrange("p k n -> p (k n)"), [a[:].rearrange("p k n -> p (k n)") for a in wo], "rest_hi", 3 * n - 2, "rest_ready")
                split_lo(w1_raw[:].rearrange("p k s n -> p (k s n)"), [a[:].rearrange("p k s n -> p (k s n)") for a in w1], "rest_hi", 3 * n - 1, "rest_ready")
                split_lo(w2_raw[:].rearrange("p k n -> p (k n)"), [a[:].rearrange("p k n -> p (k n)") for a in w2], "rest_hi", 3 * n - 0, "rest_ready")

            def xT_low(x):
                dve.wait_ge(S["xT_hi"], x + 1)
                V_.tensor_tensor(xT[1][:], OB[:, DIM:2 * DIM], xT[0][:].bitcast(F32), ALU.subtract).then_inc(S["xT_lo"], 1)

            def rope_products(x, xs, part, done):
                dve.wait_ge(S["sq_done"], 2 * x + 2 - part)
                if part:
                    dve.wait_ge(S["fold_done"], x + 1)
                    dve.wait_ge(S["k_ready"], x)
                else:
                    dve.wait_ge(S["rope_q"], x)
                src = QK[:, part * INNER:(part + 1) * INNER].rearrange("p (h d) -> p h d", d=HD)
                H2 = HD // 2
                cos = rope[:, xs, part, 0, :].unsqueeze(1).to_broadcast([P, HEADS, HD])
                V_.tensor_tensor(by_cos[:, part], src, cos, ALU.mult)
                for o, s in ((0, H2), (H2, 0)):
                    sin = rope[:, xs, part, 1, o:o + H2].unsqueeze(1).to_broadcast([P, HEADS, H2])
                    ins = V_.tensor_tensor(by_sin[:, part, :, o:o + H2], src[:, :, s:s + H2], sin, ALU.mult)
                ins.then_inc(S[done], 1)

            def kT_out(x, slot):
                dve.wait_ge(S["kT_psum"], x + 1)
                V_.tensor_copy(kT[:, :, slot, :], QK[:, INNER:2 * INNER].rearrange("p (c t) -> p c t", c=OT)).then_inc(S["kT_sb"], 1)

            def sum_squares(x, part):
                n = 2 * x + 2 - part
                o = part * HEADS
                dve.wait_ge(S["sq_done"], n)
                V_.tensor_reduce(ss[:, o:o + HEADS], sq[:, part * INNER:(part + 1) * INNER].rearrange("p (h d) -> p h d", d=HD),
                                 AX.X, ALU.add).then_inc(S["ss_done"], 1)
                dve.wait_ge(S["ss_done"], n)
                V_.tensor_scalar(ssc[:, o:o + HEADS], ss[:, o:o + HEADS], 1e-24, None, ALU.max).then_inc(S["rn_clip"], 1)

            def oT_low(w):
                dve.wait_ge(S["oT_hi"], w + 1)
                V_.tensor_tensor(oT[1][:].rearrange("p c t -> p (c t)"), VB[:],
                                 oT[0][:].rearrange("p c t -> p (c t)").bitcast(F32), ALU.subtract).then_inc(S["oT_lo"], 1)

            def residual1(w, b, i, j):
                dve.wait_ge(S["wo_out"], w + 1)
                dve.wait_ge(S["x1b_done"], 2 * (16 * b + i))
                V_.tensor_tensor(x1[:, j, :], OB[:, 0:DIM], u_in[:, j, :], ALU.add).then_inc(S["x1_done"], 1)

            def attention(b, i, j):
                w = 64 * b + 4 * i + j
                x = 65 * b + 4 * i + j + 1
                f0 = 2 * (16 * b + i)

                def row_max(hp):
                    dve.wait_ge(S["scores"], 4 * w + hp + 1)
                    h0, h1 = pair_heads(hp)
                    V_.tensor_reduce(nmraw[:, h0:h1 + 1:2], SC[hp % 2][:].rearrange("p (h k) -> p h k", h=2),
                                     AX.X, ALU.max, negate=True).then_inc(S["nmraw_done"], 1)
                    dve.wait_ge(S["nmraw_done"], 4 * w + hp + 1)
                    if hp == 0:
                        dve.wait_ge(S["rn_done"], 2 * x)
                    V_.tensor_tensor(nm[:, h0:h1 + 1:2], nmraw[:, h0:h1 + 1:2],
                                     rn[:, j % 2, h0:h1 + 1:2], ALU.mult).then_inc(S["negmax"], 1)

                def pT_out(hp):
                    dve.wait_ge(S["probsT_psum"], 4 * w + hp + 1)
                    V_.tensor_copy(pT[:, hp % 2].rearrange("p q t -> p (q t)"), TP[hp % 2][:]).then_inc(S["ptD"], 1)

                row_max(0)
                xT_low(x)
                if j:
                    oT_low(w - 1)
                row_max(1)
                if j == QW - 1:
                    norm_stats(f0, 48 * (16 * b + i + 1), 0)
                sum_squares(x, 1)
                rope_products(x, (j + 1) % 2, 1, "mulk")
                if j:
                    residual1(w - 1, b, i, j - 1)
                if j == QW - 1:
                    normalise(f0, 0)
                rope_products(x, (j + 1) % 2, 0, "mulq")
                row_max(2)
                pT_out(1)
                row_max(3)
                sum_squares(x, 0)
                pT_out(3)
                if j == QW - 1:
                    with dve.If(((i + 1) & (QUADS - 1)) == 0):
                        dve.wait_ge(S["kT_psum"], x + 1)
                        V_.memset(kT[:, :, QW - 1, :], 0.0)
                kT_out(x, (j + 1) % QW)
                if j == QW - 1:
                    hidden_split(f0, 0)
                dve.wait_ge(S["exp_done"], 4 * w + 4)
                V_.reciprocal(rinv[:], rowsum[:]).then_inc(S["rinv_done"], 1)
                dve.wait_ge(S["attn_psum"], w + 1)
                dve.wait_ge(S["rinv_done"], w + 1)
                V_.tensor_tensor(o_sb[:], OB[:].rearrange("p (h d) -> p h d", d=HD),
                                 rinv[:].unsqueeze(2).to_broadcast([P, HEADS, HD]), ALU.mult).then_inc(S["o_norm"], 1)

            def norm_stats(f, loaded, h):
                dve.wait_ge(S[f"x1s_loaded{h}"], loaded)
                for tt in range(2):
                    V_.bn_stats(stats[:, tt, 0, :], x1[:, 2 * h + tt, 0:P])
                    ins = V_.bn_stats(stats[:, tt, 1, :], x1s[:, h, tt, :])
                ins.then_inc(S["stats_done"], 1)
                dve.wait_ge(S["stats_done"], f + 1)
                V_.memset(gap[:], 0.0)
                for tt in range(2):
                    ins = V_.bn_aggr(mv[:, tt, :], stats[:, tt].rearrange("p a s -> p (a s)"))
                ins.then_inc(S["mv_done"], 1)

            def normalise(f, h):
                dve.wait_ge(S["rstd_done"], f + 1)
                for tt in range(2):
                    for k, src in ((0, x1[:, 2 * h + tt, 0:P]), (1, x1s[:, h, tt, :])):
                        ins = V_.tensor_scalar(hn[h][:, tt, k * P:(k + 1) * P], src, mv[:, tt, 0:1], rstd[:, tt:tt + 1],
                                               ALU.subtract, ALU.mult)
                ins.then_inc(S["hn_done"], 1)

            def hidden_split(f, h):
                dve.wait_ge(S["hT_f"], f + 1)
                V_.tensor_copy(hT[h][0], hTf[h]).then_inc(S["hT_hi"], 1)
                dve.wait_ge(S["hT_hi"], f + 1)
                V_.tensor_tensor(hT[h][1], hTf[h], hT[h][0].bitcast(F32), ALU.subtract).then_inc(S["hT_ready"], 1)

            def feed_forward(b, i):
                w3 = 64 * b + 4 * i + 3
                for h in range(2):
                    f = 2 * (16 * b + i) + h
                    if h == 0:
                        oT_low(w3)
                    for c in range(HC):
                        dve.wait_ge(S["gelu_done"], 6 * f + c + 1)
                        if c < 2:
                            dve.wait_ge(S["gg_ready"], 6 * f)
                        else:
                            dve.wait_ge(S["gg_ready"], 6 * f + c - 1)
                        V_.scalar_tensor_tensor(gf[:, c % 2, :], (SC[0], SC[1], TP[1])[c % 3][:, 2 * P:4 * P],
                                                small[:, B1A + c:B1A + c + 1], gl[:, c % 2, :],
                                                ALU.add, ALU.mult).then_inc(S["gf_done"], 1)
                        dve.wait_ge(S["gf_done"], 6 * f + c + 1)
                        V_.tensor_copy(gg[0][:, c, :], gf[:, c % 2, :]).then_inc(S["gg_hi"], 1)
                        if c == HC - 1:
                            dve.wait_ge(S["gg_hi"], 6 * f + 6)
                            dve.wait_ge(S["gg_ready"], 6 * f + 5)
                            V_.tensor_tensor(gg[1][:, c, :], gf[:, c % 2, :], gg[0][:, c, :].bitcast(F32),
                                             ALU.subtract).then_inc(S["gg_ready"], 1)
                        if h == 0 and c == 1:
                            residual1(w3, b, i, 3)
                        if h == 0 and c == 4:
                            norm_stats(f + 1, 32 * (16 * b + i + 1), 1)
                    if h == 0:
                        normalise(f + 1, 1)
                        hidden_split(f + 1, 1)
                    dve.wait_ge(S["w2_out"], f + 1)
                    dve.wait_ge(S["x1b_done"], f + 1)
                    x2h_ = x2[:, h].rearrange("p t c -> p (t c)")
                    V_.tensor_tensor(x2h_, OB[:], x2h_, ALU.add).then_inc(S["x2_done"], 1)
                    dve.wait_ge(S["x2_done"], f + 1)
                    dve.wait_ge(S[f"xres_loaded{h}"], 16 * (16 * b + i + 1))
                    V_.scalar_tensor_tensor(xres[:, h].rearrange("p t c -> p (t c)"), x2h_,
                                            0.5, xres[:, h].rearrange("p t c -> p (t c)"), ALU.mult, ALU.add).then_inc(S[f"out_done{h}"], 1)

            def input_norm(b):
                with dve.Fori(0, QUADS) as g:
                    n = 8 * b + g
                    dve.wait_ge(S["ln_loaded"], 16 * (n + 1))
                    for tt in range(QW):
                        ins = V_.bn_stats(stats[:, tt // 2, tt % 2, :], x1[:, tt, :])
                    ins.then_inc(S["ln_stats"], 1)
                    dve.wait_ge(S["ln_stats"], n + 1)
                    V_.memset(gap[:], 0.0)
                    for tt in range(QW):
                        ins = V_.bn_aggr(ln_mv[:, tt, :], stats[:, tt // 2, tt % 2, :])
                    ins.then_inc(S["ln_mv"], 1)
                    dve.wait_ge(S["ln_rstd"], n + 1)
                    for h in range(2):
                        dve.wait_ge(S[f"u_stored{h}"], 16 * g)
                    for tt in range(QW):
                        V_.tensor_scalar(u_in[:, tt, :], x1[:, tt, :], ln_mv[:, tt, 0:1], ln_r[:, tt:tt + 1],
                                         ALU.subtract, ALU.mult).then_inc(S["ln_done"], 1)

            def stack(b):
                if b == 0:
                    input_norm(b)
                V_.tensor_copy(small[:], small_raw[:, 0, :]).then_inc(S["small_done"], 1)
                lo_qkv(2 * b + 1)
                lo_rest(2 * b + 1)
                xT_low(65 * b)
                sum_squares(65 * b, 1)
                rope_products(65 * b, 0, 1, "mulk")
                rope_products(65 * b, 0, 0, "mulq")
                sum_squares(65 * b, 0)
                V_.memset(kT[:, :, QW - 1, :], 0.0)
                kT_out(65 * b, 0)
                with dve.Fori(0, TRIPS) as i:
                    for j in range(QW):
                        if j == QW - 1:
                            with dve.If(i == QUADS - 1):
                                lo_qkv(2 * b + 2)
                                dve.wait_ge(S["fold_done"], 65 * b + 32)
                                V_.tensor_copy(small[:, FAC:B2], small_raw[:, 1, FAC:B2]).then_inc(S["small_done"], 1)
                        attention(b, i, j)
                    feed_forward(b, i)
                    with dve.If(i == QUADS - 1):
                        lo_rest(2 * b + 2)
                        V_.tensor_copy(small[:, B2:SMALL], small_raw[:, 1, B2:SMALL])

            def state_space():
                T = V_.tensor_tensor

                def heads(a):
                    return a.unsqueeze(2).to_broadcast([a.shape[0], NH, HD])

                def chain(ins, n):
                    ins.then_inc(S["m_dchain"], 1)
                    dve.wait_ge(S["m_dchain"], n)

                def norm_stats(n, src, stat, mv_done, which, first, second):
                    for tt in range(QW):
                        ins = V_.bn_stats(stats[:, tt // 2, tt % 2, :], src[:, tt, :])
                    ins.then_inc(S[stat], 1)
                    dve.wait_ge(S[stat], first)
                    V_.memset(gap[:], 0.0)
                    for tt in range(QW):
                        ins = V_.bn_aggr(mmv[:, which, tt, :], stats[:, tt // 2, tt % 2, :])
                    ins.then_inc(S[mv_done], 1)
                    dve.wait_ge(S[second], n)

                def normalise(dst, src, which, done):
                    for tt in range(QW):
                        ins = V_.tensor_scalar(dst[:, tt, :], src[:, tt, :], mmv[:, which, tt, 0:1], mrs[:, which, tt:tt + 1],
                                               ALU.subtract, ALU.mult)
                    ins.then_inc(S[done], 1)

                def norms(g):
                    dve.wait_ge(S["m_loaded"], 16 * (g + 1))
                    norm_stats(2 * g + 1, u_in, "m_stats", "m_mv", 0, 2 * g + 1, "m_rstd")
                    dve.wait_ge(S["m_xsum"], g)
                    normalise(xln, u_in, 0, "m_xln")
                    dve.wait_ge(S["m_xln"], g + 1)
                    norm_stats(2 * g + 2, xln, "m_stats", "m_mv", 1, 2 * g + 2, "m_rstd")

                def h_split(x):
                    dve.wait_ge(S["m_hTf"], x + 1)
                    V_.tensor_copy(mh[0][:, :, 0:P], mhf[:, :, 0:P]).then_inc(S["m_hT_hi"], 1)
                    dve.wait_ge(S["m_hT_hi"], x + 1)
                    T(mh[1][:, :, 0:P], mhf[:, :, 0:P], mh[0][:, :, 0:P].bitcast(F32), ALU.subtract).then_inc(S["m_hT"], 1)

                STEPS = LOG1P_TERMS + 8

                def gates_bcdt(x, slot, tabs):
                    bcr_ = bcr[slot % 2]
                    c = STEPS * x
                    dve.wait_ge(S["m_tbc"], x + 1)
                    chain(T(v_, VB[:, 2 * D_STATE:BCDT], mp[:, DTB:DTB + NH], ALU.add), c + 1)
                    V_.scalar_tensor_tensor(bc2, tbc, 1.0, VB[:, 0:2 * D_STATE], ALU.add, ALU.mult).then_inc(S["m_v"], 1)
                    dve.wait_ge(S["m_v"], x + 1)
                    dve.wait_ge(S["m_tab"], 16 * tabs)
                    tab = rope_raw[:].rearrange("p w a b c -> p w (a b c)")[:, slot]
                    cos, sin = tab[:, 0:D_STATE], tab[:, D_STATE:2 * D_STATE]
                    b3 = bc2.rearrange("p (g d) -> p g d", g=2)
                    T(bcr_.rearrange("p (g d) -> p g d", g=2), b3, cos.unsqueeze(1).to_broadcast([P, 2, D_STATE]), ALU.mult)
                    for o in range(2):
                        ins = T(bsin.rearrange("p (g d) -> p g d", g=2)[:, :, o:ROPE_DIM:2], b3[:, :, 1 - o:ROPE_DIM:2],
                                sin[:, o:ROPE_DIM:2].unsqueeze(1).to_broadcast([P, 2, ROPE_DIM // 2]), ALU.mult)
                    ins.then_inc(S["m_bmul"], 1)
                    dve.wait_ge(S["m_bmul"], x + 1)
                    b4 = bcr_.rearrange("p (g d) -> p g d", g=2)[:, :, 0:ROPE_DIM]
                    T(b4, b4, bsin.rearrange("p (g d) -> p g d", g=2)[:, :, 0:ROPE_DIM], ALU.add).then_inc(S["m_bc"], 1)
                    dve.wait_ge(S["m_e"], x + 1)
                    chain(V_.tensor_scalar(d_, e_, 2.0, None, ALU.add), c + 2)
                    chain(V_.reciprocal(r_, d_), c + 3)
                    chain(T(s_, e_, r_, ALU.mult), c + 4)
                    chain(T(s2_, s_, s_, ALU.mult), c + 5)
                    chain(V_.tensor_scalar(p_, s2_, 1.0 / (2 * LOG1P_TERMS - 1), None, ALU.mult), c + 6)
                    for n in range(LOG1P_TERMS - 2, 0, -1):
                        chain(V_.scalar_tensor_tensor(p_, p_, 1.0 / (2 * n + 1), s2_, ALU.add, ALU.mult), c + 6 + LOG1P_TERMS - 1 - n)
                    chain(V_.scalar_tensor_tensor(p_, p_, 1.0, s_, ALU.add, ALU.mult), c + LOG1P_TERMS + 5)
                    chain(V_.tensor_scalar(d_, v_, 0.0, None, ALU.max), c + LOG1P_TERMS + 6)
                    chain(V_.scalar_tensor_tensor(dt_, p_, 2.0, d_, ALU.mult, ALU.add), c + LOG1P_TERMS + 7)
                    chain(V_.tensor_scalar(dth_, dt_, 0.5, None, ALU.mult), c + LOG1P_TERMS + 8)
                    T(a_, dt_, mp[:, NEGA:NEGA + NH], ALU.mult).then_inc(S["m_a"], 1)

                def gate_x(x):
                    dve.wait_ge(S["m_tx"], x + 1)
                    dve.wait_ge(S["m_dx"], x)
                    V_.scalar_tensor_tensor(x2h.rearrange("p h d -> p (h d)"), sq[:, INNER:2 * INNER], 1.0, QK[:, INNER:2 * INNER],
                                            ALU.add, ALU.mult).then_inc(S["m_x2h"], 1)
                    dve.wait_ge(S["m_x2h"], x + 1)
                    dve.wait_ge(S["m_xcd"], x)
                    T(xc.rearrange("p (h d) -> p h d", h=NH), x2h, heads(dth_), ALU.mult).then_inc(S["m_xc"], 1)

                def gate_z(x):
                    dve.wait_ge(S["m_y2"], x)
                    dve.wait_ge(S["m_tz"], x + 1)
                    V_.scalar_tensor_tensor(z2h.rearrange("p h d -> p (h d)"), sq[:, 0:INNER], 1.0, QK[:, 0:INNER],
                                            ALU.add, ALU.mult).then_inc(S["m_z2h"], 1)

                def y_norm(m):
                    dve.wait_ge(S["m_rms"], m + 1)
                    V_.tensor_scalar(yn, y2, rmsh, None, ALU.mult).then_inc(S["m_yn"], 1)

                def yT_low(m):
                    dve.wait_ge(S["m_yT_hi"], m + 1)
                    T(oT[1][:].rearrange("p c t -> p (c t)"), TP[0][:], oT[0][:].rearrange("p c t -> p (c t)").bitcast(F32),
                      ALU.subtract).then_inc(S["m_yT"], 1)

                def output(m, j):
                    dve.wait_ge(S["m_mo"], m + 1)
                    T(xsum[:, j, :], TP[0][:, 0:DIM], xsum[:, j, :], ALU.add).then_inc(S["m_out"], 1)

                def bcT_out(x):
                    dve.wait_ge(S["m_bcT_psum"], x + 1)
                    V_.tensor_copy(bcT, TP[1][0:D_STATE, 0:2 * P]).then_inc(S["m_bcT"], 1)

                def cb_out(x):
                    dve.wait_ge(S["m_ex"], x + 1)
                    dve.wait_ge(S["m_MT"], x)
                    T(scT, TP[1][:, 2 * P:3 * P], tri, ALU.mult).then_inc(S["m_scT"], 1)

                def weights(x):
                    dve.wait_ge(S["m_L"], x + 1)
                    dve.wait_ge(S["m_scT"], x + 1)
                    T(mT.rearrange("p (h l) -> p h l", h=NH), decay.rearrange("p (h l) -> p h l", h=NH),
                      scT.unsqueeze(1).to_broadcast([P, NH, P]), ALU.mult).then_inc(S["m_MT"], 1)

                dve.wait_ge(S["m_par_done"], 1)
                V_.tensor_scalar(small[:, NEGA:NEGA + NH], small[:, NEGA:NEGA + NH], -1.0, None, ALU.mult)
                V_.tensor_scalar(small[:, DHALF:DHALF + NH], small[:, DHALF:DHALF + NH], 0.5, None, ALU.mult)
                V_.memset(state, 0.0).then_inc(S["m_state"], 1)
                T(w_in[1], w_in_raw, w_in[0].bitcast(F32), ALU.subtract)
                for c in range(OT):
                    ins = V_.scalar_tensor_tensor(w_out[1][:, c, :], w_out_raw[:, c, :], small[:, RMSW + c:RMSW + c + 1],
                                                  w_out[0][:, c, :].bitcast(F32), ALU.mult, ALU.subtract)
                ins.then_inc(S["m_par_done"], 1)
                dve.wait_ge(S["m_par_done"], 2)
                norms(0)
                normalise(hm, xln, 1, "m_hn")
                h_split(0)
                gates_bcdt(0, 0, 1)
                bcT_out(0)
                gate_x(0)
                gate_z(0)
                cb_out(0)
                weights(0)
                h_split(1)
                with dve.Fori(0, QUADS) as q:
                    for j in range(QW):
                        m = 4 * q + j
                        x = m + 1
                        gates_bcdt(x, (j + 1) % QW, q + (2 if j == QW - 1 else 1))
                        if j:
                            yT_low(m - 1)
                        dve.wait_ge(S["m_yo"], m + 1)
                        T(ysum, OB[:].rearrange("p (h d) -> p h d", h=NH), heads(ex[j % 2][:, 0:NH]), ALU.mult).then_inc(S["m_t1"], 1)
                        dve.wait_ge(S["m_yd"], m + 1)
                        dve.wait_ge(S["m_t1"], m + 1)
                        T(ysum, ysum, VB[:].rearrange("p (h d) -> p h d", h=NH), ALU.add).then_inc(S["m_t2"], 1)
                        bcT_out(x)
                        gate_x(x)
                        dve.wait_ge(S["m_t3"], m + 1)
                        dve.wait_ge(S["m_yn"], m)
                        T(y2, ysum, z2h, ALU.mult).then_inc(S["m_y2"], 1)
                        cb_out(x)
                        gate_z(x)
                        dve.wait_ge(S["m_stmp"], m + 1)
                        dve.wait_ge(S["m_upd"], m + 1)
                        T(state, s_tmp, OB[0:D_STATE, :], ALU.add).then_inc(S["m_state"], 1)
                        if j:
                            output(m - 1, j - 1)
                        dve.wait_ge(S["m_sq"], m + 1)
                        V_.tensor_scalar(rms, ssum, 1.0 / INNER, 4 * EPS_SSM, ALU.mult, ALU.add).then_inc(S["m_rv"], 1)
                        if j == 2:
                            dve.wait_ge(S["m_hT_psum"], m + 2)
                            normalise(hm, xln, 1, "m_hn")
                        weights(x)
                        y_norm(m)
                        h_split(m + 2)
                        if j == 1:
                            norms(q + 1)
                        if j == QW - 1:
                            yT_low(m)
                            output(m, j)
                            dve.wait_ge(S["m_out"], 4 * q + 4)
                            for tt in range(QW):
                                ins = V_.bn_stats(stats[:, tt // 2, tt % 2, :], xsum[:, tt, :])
                            ins.then_inc(S["ln_stats"], 1)
                            dve.wait_ge(S["ln_stats"], LN0 + q + 1)
                            V_.memset(gap[:], 0.0)
                            for tt in range(QW):
                                ins = V_.bn_aggr(ln_mv[:, tt, :], stats[:, tt // 2, tt % 2, :])
                            ins.then_inc(S["ln_mv"], 1)
                            dve.wait_ge(S["ln_rstd"], LN0 + q + 1)
                            for h in range(2):
                                dve.wait_ge(S[f"u_stored{h}"], 16 * (24 * len(blocks[:1]) + q))
                            for tt in range(QW):
                                ins = V_.tensor_scalar(u0[:, tt, :], xsum[:, tt, :], ln_mv[:, tt, 0:1], ln_r[:, tt:tt + 1],
                                                       ALU.subtract, ALU.mult)
                            ins.then_inc(S["m_u0"], 1)

            V_.memset(w1_raw[:, :, :, HID:HC * P], 0.0)
            V_.memset(w2_raw[:, HC - 1, :], 0.0)
            V_.memset(zrow[:], 0.0)
            V_.memset(V[:, QW - 1, :], 0.0)
            V_.memset(halfpow[:], -0.5)
            V_.memset(eps[:, 0, :], EPS_LN)
            V_.memset(eps[:, 1, :], EPS_SSM)
            for l in range(LAYERS):
                for o in (B1A, B1G):
                    ins = V_.memset(small_raw[:, l, o + HC - 1:o + HC], 0.0)
            ins.then_inc(S["const_done"], 1)
            dve.wait_ge(S["const_loaded"], 16 * (2 + LAYERS * (6 + 1 + 2 + 2 + 2)))
            V_.tensor_copy(ident_b[:], ident[:])
            for v, order in enumerate(((0, 2), (0, 1), (1, 0))):
                for hh in range(2):
                    for s, m in enumerate(order):
                        o = (4 * v + 2 * hh + s) * P
                        V_.tensor_copy(mask[:, o:o + P], mask_f[:, m, :])
            for l in range(LAYERS):
                V_.tensor_scalar(small_raw[:, l, FAC:FAC + HD], small_raw[:, l, FAC:FAC + HD], QK_SCALE, None, ALU.mult)
                V_.tensor_scalar(small_raw[:, l, FAC + HD:FAC + HD + HD // 2], small_raw[:, l, FAC + HD:FAC + HD + HD // 2], -QK_SCALE, None, ALU.mult)
                V_.tensor_scalar(small_raw[:, l, FAC + HD + HD // 2:FAC + 2 * HD], small_raw[:, l, FAC + HD + HD // 2:FAC + 2 * HD], QK_SCALE, None, ALU.mult)
                ins = V_.tensor_scalar(small_raw[:, l, FAC + 3 * HD:FAC + 3 * HD + HD // 2], small_raw[:, l, FAC + 3 * HD:FAC + 3 * HD + HD // 2], -1.0, None, ALU.mult)
            ins.then_inc(S["const_done"], 2)
            dve.wait_ge(S["const_done"], 3)
            for b in blocks:
                stack(b)
                if b == 0 and mix:
                    state_space()
            if not blocks:
                state_space()

        @block.gpsimd
        def _(pool):
            G = nc.gpsimd
            H2 = HD // 2

            def rope_window(b, x, xs, slot, loads, factors):
                pool.wait_ge(S["small_done"], factors)
                pool.wait_ge(S[f"rope_loaded{slot}"], 16 * loads)
                for g in range(2):
                    ins = G.tensor_tensor(rope[:, xs, g].rearrange("p c (e d) -> p c e d", e=2),
                                          rope_raw[:, slot, g].unsqueeze(2).to_broadcast([P, 2, 2, H2]),
                                          small[:, FAC + 2 * g * HD:FAC + 2 * (g + 1) * HD].rearrange("p (c e d) -> p c e d", c=2, e=2), ALU.mult)
                ins.then_inc(S["fold_done"], 1)
                pool.wait_ge(S["rn_clip"], 2 * x + 1)
                G.tensor_tensor(rn[:, xs, HEADS:2 * HEADS], ssc[:, HEADS:2 * HEADS], halfpow[:, 0:HEADS], ALU.pow).then_inc(S["rn_done"], 1)
                pool.wait_ge(S["mulk"], x + 1)
                G.tensor_tensor(by_cos[:, 1], by_cos[:, 1], by_sin[:, 1], ALU.add).then_inc(S["k_sum"], 1)
                pool.wait_ge(S["rn_done"], 2 * x + 1)
                pool.wait_ge(S["k_sum"], x + 1)
                G.tensor_tensor(qk[:, 1], by_cos[:, 1], rn[:, xs, HEADS:2 * HEADS].unsqueeze(2).to_broadcast([P, HEADS, HD]),
                                ALU.mult).then_inc(S["k_ready"], 1)
                pool.wait_ge(S["mulq"], x + 1)
                G.tensor_tensor(qk[:, 0], by_cos[:, 0], by_sin[:, 0], ALU.add).then_inc(S["rope_q"], 1)
                pool.wait_ge(S["rn_clip"], 2 * x + 2)
                G.tensor_tensor(rn[:, xs, 0:HEADS], ssc[:, 0:HEADS], halfpow[:, 0:HEADS], ALU.pow).then_inc(S["rn_done"], 1)

            def norm_root(b, i, h):
                f = 2 * (16 * b + i) + h
                pool.wait_ge(S["mv_done"], f + 1)
                G.tensor_tensor(var_e[:], mv[:, :, 1], eps[:, 0, 0:2], ALU.add).then_inc(S["var_done"], 1)
                pool.wait_ge(S["var_done"], f + 1)
                G.tensor_tensor(rstd[:], var_e[:], halfpow[:, 0:2], ALU.pow).then_inc(S["rstd_done"], 1)

            def add_bias(b, i, h):
                pool.wait_ge(S[f"u_stored{h}"], 16 * (24 * b + 8 + i))
                pool.wait_ge(S["x1_done"], 64 * b + 4 * i + 2 * h + 2)
                for tt in range(2):
                    ins = G.tensor_tensor(x2[:, h, tt, :], x1[:, 2 * h + tt, :], small[:, B2:B2 + DIM], ALU.add)
                ins.then_inc(S["x1b_done"], 1)

            def feed_forward(b, i):
                add_bias(b, i, 0)
                for h in range(2):
                    f = 2 * (16 * b + i) + h
                    for c in range(HC - 1):
                        pool.wait_ge(S["gg_hi"], 6 * f + c + 1)
                        G.tensor_tensor(gg[1][:, c, :], gf[:, c % 2, :], gg[0][:, c, :].bitcast(F32), ALU.subtract).then_inc(S["gg_ready"], 1)
                        if h == 0 and c == 4:
                            norm_root(b, i, 1)
                    if h == 0:
                        add_bias(b, i, 1)

            def input_norm(b):
                with pool.Fori(0, QUADS) as g:
                    n = 8 * b + g
                    pool.wait_ge(S["ln_mv"], n + 1)
                    G.tensor_tensor(ln_v[:], ln_mv[:, :, 1], eps[:, 0, :], ALU.add).then_inc(S["ln_var"], 1)
                    pool.wait_ge(S["ln_var"], n + 1)
                    G.tensor_tensor(ln_r[:], ln_v[:], halfpow[:, 0:4], ALU.pow).then_inc(S["ln_rstd"], 1)

            def stack(b):
                if b == 0:
                    input_norm(b)
                rope_window(b, 65 * b, 0, 0, 17 * b + 1, 2 * b + 1)
                with pool.Fori(0, TRIPS) as i:
                    for j in range(QW):
                        nj = (j + 1) % QW
                        loads = 17 * b + i + 2 if nj == 0 else 17 * b + i + 1
                        factors = 2 * b + 1 + ((((i + 1) >> 3) & 1) if j == QW - 1 else (i >> 3))
                        if j == QW - 1:
                            norm_root(b, i, 0)
                        rope_window(b, 65 * b + 4 * i + j + 1, (j + 1) % 2, nj, loads, factors)
                    feed_forward(b, i)

            def state_space():
                T = G.tensor_tensor

                def heads(a):
                    return a.unsqueeze(2).to_broadcast([P, NH, HD])

                def root(n, which, mv_n):
                    pool.wait_ge(S["m_mv"], mv_n)
                    T(mvar[:, which], mmv[:, which, :, 1], eps[:, which, :], ALU.add).then_inc(S["m_var"], 1)
                    pool.wait_ge(S["m_var"], mv_n)
                    T(mrs[:, which], mvar[:, which], halfpow[:, 0:QW], ALU.pow).then_inc(S["m_rstd"], 1)

                def sum_input():
                    T(xsum, u_in[:], xln[:], ALU.add).then_inc(S["m_xsum"], 1)

                def a_masked(x):
                    pool.wait_ge(S["m_a"], x + 1)
                    pool.wait_ge(S["m_d"], x)
                    T(a_tri.rearrange("p (h l) -> p h l", h=NH), a_.unsqueeze(2).to_broadcast([P, NH, P]),
                      tri.unsqueeze(1).to_broadcast([P, NH, P]), ALU.mult).then_inc(S["m_atri"], 1)

                def inputs(x, s):
                    pool.wait_ge(S["m_x2h"], x + 1)
                    pool.wait_ge(S["m_t3"], x)
                    T(dx, x2h, heads(mp[:, DHALF:DHALF + NH]), ALU.mult).then_inc(S["m_dx"], 1)
                    pool.wait_ge(S["m_xc"], x + 1)
                    pool.wait_ge(S["m_ex"], x + 1)
                    pool.wait_ge(S["m_upd"], x)
                    T(xcd.rearrange("p (h d) -> p h d", h=NH), xc.rearrange("p (h d) -> p h d", h=NH),
                      heads(ex[s][:, NH:2 * NH]), ALU.mult).then_inc(S["m_xcd"], 1)

                root(0, 0, 1)
                root(0, 1, 2)
                sum_input()
                a_masked(0)
                inputs(0, 0)
                with pool.Fori(0, QUADS) as q:
                    for j in range(QW):
                        m = 4 * q + j
                        pool.wait_ge(S["m_state"], m + 1)
                        T(s_tmp.rearrange("p (h d) -> p h d", h=NH), state.rearrange("p (h d) -> p h d", h=NH),
                          ex[j % 2][0:D_STATE, 2 * NH:3 * NH].unsqueeze(2).to_broadcast([D_STATE, NH, HD]), ALU.mult).then_inc(S["m_stmp"], 1)
                        a_masked(m + 1)
                        pool.wait_ge(S["m_t2"], m + 1)
                        pool.wait_ge(S["m_dx"], m + 1)
                        T(ysum, ysum, dx, ALU.add).then_inc(S["m_t3"], 1)
                        inputs(m + 1, (j + 1) % 2)
                        pool.wait_ge(S["m_rv"], m + 1)
                        T(rmsh, rms, halfpow[:, 0:1], ALU.pow).then_inc(S["m_rms"], 1)
                        if j == 1:
                            root(q + 1, 0, 2 * q + 3)
                            root(q + 1, 1, 2 * q + 4)
                    pool.wait_ge(S["ln_mv"], LN0 + q + 1)
                    G.tensor_tensor(ln_v[:], ln_mv[:, :, 1], eps[:, 0, :], ALU.add).then_inc(S["ln_var"], 1)
                    pool.wait_ge(S["ln_var"], LN0 + q + 1)
                    T(ln_r[:], ln_v[:], halfpow[:, 0:QW], ALU.pow).then_inc(S["ln_rstd"], 1)
                    pool.wait_ge(S["m_u0"], q + 1)
                    pool.wait_ge(S["m_out_stored"], 16 * (q + 1))
                    sum_input()

            pool.wait_ge(S["const_done"], 3)
            for b in blocks:
                stack(b)
                if b == 0 and mix:
                    state_space()
            if not blocks:
                state_space()


def rope_table():
    f = np.float32
    half = np.arange(0, HD, 2, dtype=f)
    inv = (f(1.0) / np.power(f(10000.0), half / f(HD))).astype(f)
    pos = np.arange(N, dtype=f)
    ang = (pos[:, None] * inv[None, :]).astype(f)
    base = ((half + f(0.4 * HD)) / f(1.4 * HD)).astype(f)
    power = ((pos - f(N // 2)) / f(P // 2)).astype(f)
    scale = np.power(base[None, :], power[:, None]).astype(f)
    c, s = np.cos(ang).astype(f), np.sin(ang).astype(f)
    return np.ascontiguousarray(np.concatenate([c * scale, s * scale, c / scale, s / scale], axis=1).astype(f))


def state_rope_table():
    f = np.float32
    inv = (f(1.0) / np.power(f(10000.0), np.arange(0, ROPE_DIM, 2, dtype=f) / f(ROPE_DIM))).astype(f)
    ang = (np.arange(N, dtype=f)[:, None] * inv[None, :]).astype(f)
    c, s = np.cos(ang).astype(f), np.sin(ang).astype(f)
    own, partner = np.full((N, D_STATE), f(0.5)), np.zeros((N, D_STATE), f)
    own[:, 0:ROPE_DIM:2], own[:, 1:ROPE_DIM:2] = f(0.5) * c, f(0.5) * c
    partner[:, 0:ROPE_DIM:2], partner[:, 1:ROPE_DIM:2] = f(-0.5) * s, f(0.5) * s
    return np.ascontiguousarray(np.concatenate([own, partner], axis=1).astype(f))


def mask_table():
    q, k = np.arange(P)[:, None], np.arange(P)[None, :]
    m = [np.where(k > q, MASKED, 0.0), np.where(k < q, MASKED, 0.0), np.full((P, P), MASKED)]
    return np.concatenate(m, axis=1).astype(np.float32)


def build(nc, arrays, blocks=(0, 1)):
    t = {}
    for name, a in arrays.items():
        t[name] = nc.dram_tensor("in_" + name, a.shape, mybir.dt.from_np(a.dtype), kind="ExternalInput").ap()
    t["u_dram"] = nc.dram_tensor("u_dram", ((LAYERS + 2) * REGION, DIM), F32, kind="Internal").ap()
    out = nc.dram_tensor("out", (N, DIM), F32, kind="ExternalOutput").ap()
    if blocks == (0, 1):
        mid = [nc.dram_tensor(f"mid_{n}", (N, DIM), F32, kind="Internal").ap() for n in range(2)]
        t["x_in"], t["x_out"] = (t["x"], mid[1]), (mid[0], out)
        t["m_in"], t["m_out"] = mid
    else:
        t["x_in"], t["x_out"] = (t["x"],), (out,)
        t["m_in"], t["m_out"] = t["x"], out
    macaron_program(nc, t, blocks)


def host_arrays(inp):
    a = {"x": np.ascontiguousarray(inp["L0_attn_x"]).reshape(N, DIM)}
    for k in ("wqkv", "wo", "w1", "w2", "q_scale", "k_scale", "ln_g", "ln_b", "b1", "b2"):
        a[k] = np.ascontiguousarray(inp["L0_ffn_" + k])
    for k, name in (("w_in", "W_in"), ("w_out", "W_out"), ("dt_bias", "dt_bias"), ("A_log", "A_log"), ("D", "D"),
                    ("m_ln_w", "ln_w"), ("m_ln_b", "ln_b"), ("rms_w", "rms_w")):
        a[k] = np.ascontiguousarray(inp["L0_attn_" + name])
    a["m_rope"] = state_rope_table()
    a["tri"] = np.triu(np.ones((P, P), np.float32))
    a["after"] = np.tril(np.ones((P, P), np.float32), -1)
    a["ones"] = np.ones((P, P), np.float32)
    a["rope"], a["mask"], a["ident"] = rope_table(), mask_table(), np.eye(P, dtype=np.float32)
    return a


def kernel(**inputs):
    import concourse.bacc as bacc
    from concourse.bass_utils import run_bass_kernel_spmd

    nc = bacc.Bacc("TRN2", target_bir_lowering=False, num_devices=1, dynamic_dma_scratch_size=1024)
    arrays = host_arrays({k: np.asarray(v) for k, v in inputs.items()})
    build(nc, arrays)
    r = run_bass_kernel_spmd(nc, [{"in_" + k: v for k, v in arrays.items()}], core_ids=[0])
    return r.results[0]["out"].reshape(1, N, DIM)
```

```python
import numpy as np
import concourse.bass as bass
from concourse import mybir
from contextlib import ExitStack


F32 = mybir.dt.float32
F32R = mybir.dt.float32r
BF16 = mybir.dt.bfloat16
ALU = mybir.AluOpType
ACT = mybir.ActivationFunctionType
AX = mybir.AxisListType

P = 128
N = 4096
DIM = 256
KT = DIM // P
HEADS, HD = 8, 64
INNER = HEADS * HD
OT = INNER // P
HID = 682
HC = -(-HID // P)
HTAIL = HID - (HC - 1) * P
LAYERS = 2
DOWN_LAG = 5
QW = 4
QUAD = QW * P
QUADS = N // QUAD
TRIPS = LAYERS * QUADS
REGION = (QUADS + 1) * QUAD
QK_SCALE = 8.0
MASKED = -1.0e30
START = 1
LOWEST = -3.0e38
EPS_LN = 1e-5

D_STATE = 32
ROPE_DIM = D_STATE // 2
NH = INNER // HD
D_IN = 2 * INNER + 2 * D_STATE + NH
BCDT = 2 * D_STATE + NH
EPS_SSM = 1e-6
LOG1P_TERMS = 8
DTB, NEGA, DHALF = 0, NH, 2 * NH
LNW = 3 * NH
LNBM = LNW + KT
RMSW = LNBM + KT
MSMALL = RMSW + OT

FAC = 0
B2 = FAC + 4 * HD
LG, LB = B2 + DIM, B2 + DIM + KT
B1A = LB + KT
B1G = B1A + HC
SMALL = B1G + HC


def pair_heads(hp):
    h = 4 * (hp // 2) + hp % 2
    return h, h + 2


def region_row(g):
    return (g + (g >> 3) + 1) * QUAD


def macaron_program(nc, t, blocks=(0, 1), mamba=True):
    ctx = ExitStack()
    with ctx:
        def sb(name, shape, dt=F32):
            return ctx.enter_context(nc.sbuf_tensor(name, shape, dt))

        def ps(name, cols):
            return ctx.enter_context(nc.psum_tensor(name, [P, cols], F32))

        def sem(name):
            return ctx.enter_context(nc.semaphore(name))

        ident = sb("ident", [P, P])
        mask_first = sb("mask_first", [P, 2 * P])
        mask_rest = sb("mask_rest", [P, 2 * P])
        halfpow = sb("halfpow", [P, 16])
        eps = sb("eps", [P, 2, QW])
        gap = sb("gap", [P, 1])
        half = sb("half", [P, 1])
        zrow = sb("zrow", [1, DIM])
        small_raw = sb("small_raw", [P, LAYERS, SMALL])
        small = sb("small", [P, SMALL])
        wqkv_raw = sb("wqkv_raw", [P, KT, 3 * INNER])
        wo_raw = sb("wo_raw", [P, OT, DIM])
        w1_raw = sb("w1_raw", [P, KT, 2, HC * P])
        w2_raw = sb("w2_raw", [P, HC, DIM])
        wqkv = [sb(f"wqkv_{s}", [P, KT, 3 * INNER], F32R) for s in ("hi", "lo")]
        wo = [sb(f"wo_{s}", [P, OT, DIM], F32R) for s in ("hi", "lo")]
        w1 = [sb(f"w1_{s}", [P, KT, 2, HC * P], F32R) for s in ("hi", "lo")]
        w2 = [sb(f"w2_{s}", [P, HC, DIM], F32R) for s in ("hi", "lo")]
        u_in = sb("u_in", [P, QW, DIM])
        u_shift = sb("u_shift", [P, QW, P])
        rope_raw = sb("rope_raw", [P, QW, 2, 2, HD // 2])
        rope = sb("rope", [P, 2, 2, 2, HD])
        xT = [sb(f"xT_{s}", [P, DIM], F32R) for s in ("hi", "lo")]
        sq = sb("sq", [P, 2 * INNER])
        sq_sums = sb("sq_sums", [P, 2 * HEADS])
        sq_sums_clipped = sb("sq_sums_clipped", [P, 2 * HEADS])
        inv_norm = sb("inv_norm", [P, 2, 2 * HEADS])
        by_cos = sb("by_cos", [P, 2, HEADS, HD])
        by_sin = sb("by_sin", [P, 2, HEADS, HD])
        qk = sb("qk", [P, 2, HEADS, HD])
        qT = sb("qT", [P, OT, P])
        kT = sb("kT", [P, OT, QW, P])
        V = sb("V", [P, QW, INNER])
        row_maxima = sb("row_maxima", [P, HEADS])
        neg_maxima = sb("neg_maxima", [P, HEADS])
        probs = sb("probs", [P, 2, 2, 2 * P])
        rowsum = sb("rowsum", [P, HEADS])
        rinv = sb("rinv", [P, HEADS])
        pT = sb("pT", [P, 2, 4, P])
        o_sb = sb("o_sb", [P, HEADS, HD])
        oT = [sb(f"oT_{s}", [P, OT, P], F32R) for s in ("hi", "lo")]
        x1 = sb("x1", [P, QW, DIM])
        x1s = sb("x1s", [P, 2, 2, P])
        stats = sb("stats", [P, 2, 2, 6])
        mv = sb("mv", [P, 2, 2])
        var_e = sb("var_e", [P, 2])
        rstd = sb("rstd", [P, 2])
        pT_flat = pT[:].rearrange("p s q t -> p s (q t)")
        probs_flat = probs[:].rearrange("p s h k -> p s (h k)")
        gl = pT_flat[:, 1].rearrange("p (s t) -> p s t", s=2)
        gf = probs_flat[:, 1].rearrange("p (s t) -> p s t", s=2)
        gg = [sb(f"gg_{s}", [P, HC, 2 * P], F32R) for s in ("hi", "lo")]
        hn_tile = sb("hn_tile", [P, 2 * DIM])
        hn = [hn_tile[:].rearrange("p (t c) -> p t c", t=2), pT_flat[:, 0].rearrange("p (t c) -> p t c", t=2)]
        hTf = [hn_tile[:].rearrange("p (k t) -> p k t", k=KT), pT_flat[:, 0].rearrange("p (k t) -> p k t", k=KT)]
        hT = [[sb(f"hT_{s}", [P, KT, 2 * P], F32R)[:] for s in ("hi", "lo")],
              [a[:].rearrange("p c t -> p (c t)").rearrange("p (k t) -> p k t", k=KT) for a in oT]]
        xres = sb("xres", [P, 2, 2, DIM])
        x2 = sb("x2", [P, 2, 2, DIM])
        ln_mv = sb("ln_mv", [P, QW, 2])
        ln_v = sb("ln_v", [P, QW])
        ln_r = sb("ln_r", [P, QW])
        QK = ps("QK", 1024)
        VB = ps("VB", 512)
        SC = [ps("SC0", 512), ps("SC1", 512)]
        TP = [ps("TP0", 512), ps("TP1", 512)]
        OB = ps("OB", 512)

        w_in_raw = wqkv_raw[:].rearrange("p k n -> p (k n)")[:, 0:KT * D_IN].rearrange("p (k n) -> p k n", k=KT)
        w_in = [a[:].rearrange("p k n -> p (k n)")[:, 0:KT * D_IN].rearrange("p (k n) -> p k n", k=KT) for a in wqkv]
        w_out_raw, w_out = wo_raw, wo
        tri, after, ones = u_shift[:, 0, :], u_shift[:, 1, :], u_shift[:, 2, :]
        mp = small[:, 0:MSMALL]
        mh, mhf = hT[0], hTf[0]
        xln = x1
        hm = x2[:].rearrange("p a t c -> p (a t) c")
        xsum = xres[:].rearrange("p a t c -> p (a t) c")
        u0 = w2_raw[:].rearrange("p k n -> p (k n)")[:, 0:QW * DIM].rearrange("p (t c) -> p t c", t=QW)
        kT_flat = kT[:].rearrange("p c s t -> p (c s t)")
        a_tri = kT_flat[:, 0:NH * P]
        decay = kT_flat[:, NH * P:2 * NH * P]
        V_flat = V[:].rearrange("p s c -> p (s c)")
        mT = V_flat[:, 0:NH * P]
        xc, xcd = V[:, 2, :], V[:, 3, :]
        x2h, z2h = by_cos[:, 0], by_cos[:, 1]
        ysum, dx = by_sin[:, 0], by_sin[:, 1]
        y2, yn = qk[:, 0], qk[:, 1]
        ysq = o_sb
        bcT = qT[:].rearrange("p c t -> p (c t)")[0:D_STATE, 0:2 * P]
        state = pT_flat[0:D_STATE, 0]
        scT = pT_flat[:, 1, 0:P]
        bcr = [pT_flat[:, 1, P:P + 2 * D_STATE], probs_flat[:, 0, 2 * D_STATE:4 * D_STATE]]
        bsin = pT_flat[:, 1, P + 64:P + 128]
        tbc = pT_flat[:, 1, 2 * P:2 * P + 64]
        bc2 = pT_flat[:, 1, 2 * P + 64:2 * P + 128]
        tiny = pT_flat[:, 1, 3 * P:4 * P]
        (v_, av_, e_, d_, r_, s_, s2_, p_, dt_, dth_, a_) = [tiny[:, k * NH:(k + 1) * NH] for k in range(11)]
        ex = [probs_flat[:, 0, k * 3 * NH:(k + 1) * 3 * NH] for k in range(2)]
        ssum, rms, rmsh = [tiny[:, 14 * NH + k:14 * NH + k + 1] for k in range(3)]
        s_tmp = probs_flat[0:D_STATE, 1]
        ln_in = [x1[:], x2[:].rearrange("p a t c -> p (a t) c")]
        ln_out = [u_in[:], xres[:].rearrange("p a t c -> p (a t) c")]
        mmv = sb("mmv", [P, 2, QW, 2])
        mvar = sb("mvar", [P, 2, QW])
        mrs = sb("mrs", [P, 2, QW])

        names = """sp_steps const_loaded const_done zero_stored small_done u_loaded0 u_loaded1 u_loaded2 u_loaded3
            rope_loaded0 rope_loaded1 rope_loaded2 rope_loaded3 raw_qkv raw_o raw_1 raw_2
            wqkv_hi wqkv_ready rest_hi rest_ready 
            xT_psum xT_hi xT_lo q_proj k_proj v_proj qT_psum kT_psum qT_sb kT_sb scores probsT_psum attn_psum
            oT_psum oT_hi oT_lo wo_out x1_done sq_done ss_done rope_q rn_clip rn_done k_ready mulq mulk fold_done
            k_sum max_done negmax exp_done ptA ptD v_sb rinv_done o_norm
            x1s_loaded0 x1s_loaded1
            stats_done mv_done var_done rstd_done hn_done hT_psum hT_f hT_hi hT_ready ga_psum gelu_done gf_done gg_hi gg_ready
            w2_out x2_half bias_added x2_done xres_loaded0 xres_loaded1 out_done0 out_done1 u_stored0 u_stored1 out_stored0 out_stored1
            ln_loaded0 ln_loaded1 ln_stats ln_done ln_mv ln_var ln_rstd
            m_par m_par_done m_loaded m_tab m_stats m_mv m_var m_rstd m_xln m_hn m_xsum
            m_hT_psum m_hTf m_hT_hi m_hT m_b_proj m_x_proj m_z_proj m_tbc m_bmul m_bc m_v m_abs m_e m_dchain m_a
            m_tx m_tz m_x2h m_z2h m_atri m_bcT_psum m_bcT m_misc m_ex m_scT m_d m_L m_yo m_t1 m_MT m_xc m_xcd m_dx
            m_yd m_upd m_t2 m_t3 m_y2 m_sq m_rv m_rms m_yn m_stmp m_state m_yT_psum m_yT_hi m_yT m_mo m_out m_out_stored
            m_u0""".split()
        S = {}
        for nme in names:
            S[nme] = sem(nme)
        started = sem("started")

        mix = (mamba and len(blocks) == 2) or blocks == ()
        LN0 = QUADS if blocks else 0
        block = ctx.enter_context(nc.Block())
        x_in, x_out = t["x_in"], t["x_out"]
        U = t["u_dram"]

        def start_counts(engine, part):
            for nme in names[part::5]:
                engine.sem_inc(S[nme], START)
            engine.sem_inc(started, 1)
            engine.wait_ge(started, 5)

        def rows(T, row, count=P):
            return T[bass.ds(row, count), :]

        def rowtiles(T, row, tiles, c0=0, c1=DIM):
            return T[bass.ds(row, tiles * P), c0:c1].rearrange("(t p) c -> p t c", p=P)

        @block.sync
        def _(sp):
            start_counts(sp, 0)
            def settle():
                sp.sem_inc(S["sp_steps"])

            def load_weights(l):
                sp.dma_start(wqkv_raw[:], t["wqkv"][l].rearrange("(k p) n -> p k n", p=P)).then_inc(S["raw_qkv"], 16)
                sp.dma_start(wo_raw[:], t["wo"][l].rearrange("(k p) n -> p k n", p=P)).then_inc(S["raw_o"], 16)
                for k in range(KT):
                    sp.dma_start(w1_raw[:, k, :, 0:HID], t["w1"][l, k * P:(k + 1) * P, :].rearrange("p (s n) -> p s n", s=2)).then_inc(S["raw_1"], 16)
                sp.dma_start(w2_raw[:, 0:HC - 1, :], t["w2"][l, 0:(HC - 1) * P, :].rearrange("(k p) n -> p k n", p=P)).then_inc(S["raw_2"], 16)
                sp.dma_start(w2_raw[0:HTAIL, HC - 1, :], t["w2"][l, (HC - 1) * P:HID, :]).then_inc(S["raw_2"], 16)

            def load_window(b, g, j):
                row = region_row(g) + j * P
                sp.dma_start(u_in[:, j, :], rows(U, row)).then_inc(S[f"u_loaded{j}"], 16)
                sp.dma_start(u_shift[:, j, :], U[bass.ds(row - 1, P), P:DIM]).then_inc(S[f"u_loaded{j}"], 16)
                sp.dma_start(rope_raw[:, j].rearrange("p a b c -> p (a b c)"),
                             t["rope"][bass.ds((g & 7) * QUAD + j * P, P), :]).then_inc(S[f"rope_loaded{j}"], 16)

            def shift_x1(i, h):
                done = S[f"x1s_loaded{h}"]
                sp.dma_start(x1s[1:P, h], x1[0:P - 1, 2 * h:2 * h + 2, P:DIM]).then_inc(done, 16)
                if h:
                    sp.dma_start(x1s[0:1, h], x1[P - 1:P, 1:3, P:DIM]).then_inc(done, 16)
                else:
                    sp.dma_start(x1s[0:1, h, 1], x1[P - 1:P, 0, P:DIM]).then_inc(done, 16)
                    with sp.If((i & (QUADS - 1)) == 0):
                        sp.dma_start(x1s[0:1, h, 0], zrow[0:1, 0:P]).then_inc(done, 16)
                    with sp.Else():
                        sp.dma_start(x1s[0:1, h, 0], x1[P - 1:P, QW - 1, P:DIM]).then_inc(done, 16)

            def stack(b):
                if b:
                    for name, per in (("wqkv_ready", 1), ("rest_ready", 3)):
                        sp.wait_ge(S[name], START + 2 * b * per)
                base = 24 * b
                if b == 0:
                    def load_quad(s, row):
                        sp.dma_start(ln_in[s], rowtiles(x_in[0], row, QW)).then_inc(S[f"ln_loaded{s}"], 16)

                    for s in range(2):
                        load_quad(s, s * QUAD)
                    sp.wait_ge(S["const_done"], START + 1)
                load_weights(0)
                if b == 0:
                    with sp.Fori(0, QUADS // 2) as n:
                        for s in range(2):
                            sp.wait_ge(S["ln_done"], START + 2 * n + s + 1)
                            settle()
                            for h in range(2):
                                sp.dma_start(rowtiles(U, (2 * n + s + 1) * QUAD + h * 2 * P, 2),
                                             ln_out[s][:, 2 * h:2 * h + 2, :]).then_inc(S[f"u_stored{h}"], 16)
                            load_quad(s, ((2 * n + 2 + s) & (QUADS - 1)) * QUAD)
                    for s in range(2):
                        sp.wait_ge(S[f"ln_loaded{s}"], START + 16 * (QUADS // 2 + 1))
                    sp.wait_ge(S["zero_stored"], START + 16 * (LAYERS + 1))
                for h in range(2):
                    sp.wait_ge(S[f"u_stored{h}"], START + 16 * (base + QUADS))
                for j in range(QW):
                    load_window(b, 0, j)
                for name, per in (("wqkv_ready", 1), ("rest_ready", 3)):
                    sp.wait_ge(S[name], START + (2 * b + 1) * per)
                load_weights(1)
                with sp.Fori(0, TRIPS) as i:
                    tokens = (i & (QUADS - 1)) * QUAD
                    for j in range(QW):
                        w = 64 * b + 4 * i + j
                        sp.wait_ge(S["x1_done"], START + w + 1)
                        if j % 2:
                            shift_x1(i, j // 2)
                        sp.wait_ge(S[f"u_stored{j // 2}"], START + 16 * (base + i + 2))
                        settle()
                        sp.wait_ge(S["fold_done"], START + 65 * b + 4 * i + j + 1)
                        settle()
                        load_window(b, i + 1, j)
                        if j % 2:
                            h = j // 2
                            sp.wait_ge(S[f"out_stored{h}"], START + 16 * (16 * b + i))
                            settle()
                            sp.dma_start(xres[:, h], rowtiles(x_in[b], tokens + h * 2 * P, 2)).then_inc(S[f"xres_loaded{h}"], 16)
                    for h in range(2):
                        f = 2 * (16 * b + i) + h
                        sp.wait_ge(S["x2_done"], START + f + 1)
                        sp.wait_ge(S[f"u_stored{h}"], START + 16 * (base + 8 + i))
                        settle()
                        sp.dma_start(rowtiles(U, region_row(i) + REGION + h * 2 * P, 2), x2[:, h]).then_inc(S[f"u_stored{h}"], 16)
                        sp.wait_ge(S[f"out_done{h}"], START + 16 * b + i + 1)
                        sp.dma_start(rowtiles(x_out[b], tokens + h * 2 * P, 2), xres[:, h]).then_inc(S[f"out_stored{h}"], 16)
                for h in range(2):
                    sp.wait_ge(S[f"out_stored{h}"], START + 16 * (16 * b + 16))
                    sp.wait_ge(S[f"u_stored{h}"], START + 16 * (base + 24))

            def state_space():
                src = t["m_in"]
                if blocks:
                    for name, per in (("wqkv_ready", 1), ("rest_ready", 3)):
                        sp.wait_ge(S[name], START + 2 * per)
                    sp.wait_ge(S["k_ready"], START + 65)
                    sp.wait_ge(S["xT_lo"], START + 65)
                    sp.wait_ge(S["v_proj"], START + 65)
                    sp.wait_ge(S["w2_out"], START + 32)
                    for h in range(2):
                        sp.wait_ge(S[f"out_stored{h}"], START + 16 * 16)
                    for j in range(QW):
                        sp.wait_ge(S[f"u_loaded{j}"], START + 32 * 17)
                        sp.wait_ge(S[f"rope_loaded{j}"], START + 16 * 17)
                sp.dma_start(w_in_raw, t["w_in"].rearrange("(k p) n -> p k n", p=P)).then_inc(S["m_par"], 16)
                sp.dma_start(w_out_raw[:], t["w_out"].rearrange("(k p) n -> p k n", p=P)).then_inc(S["m_par"], 16)
                for dst, name in ((tri, "tri"), (after, "after"), (ones, "ones")):
                    sp.dma_start(dst, t[name]).then_inc(S["m_par"], 16)
                for o, name in ((DTB, "dt_bias"), (NEGA, "A_log"), (DHALF, "D")):
                    sp.dma_start(small[:, o:o + NH], t[name].rearrange("(a n) -> a n", a=1).to_broadcast([P, NH])).then_inc(S["m_par"], 16)
                with nc.allow_non_contiguous_dma("parameters laid along partitions, once"):
                    for o, n, name in ((LNW, KT, "m_ln_w"), (LNBM, KT, "m_ln_b"), (RMSW, OT, "rms_w")):
                        sp.dma_start(small[:, o:o + n], t[name].rearrange("(k p) -> p k", p=P)).then_inc(S["m_par"], 16)

                def load_first():
                    sp.dma_start(u_in[:], rowtiles(src, 0, QW)).then_inc(S["m_loaded"], 16)
                    sp.dma_start(rope_raw[:].rearrange("p w a b c -> p w (a b c)")[:, :, 0:2 * D_STATE],
                                 t["m_rope"][0:QUAD, :].rearrange("(t p) c -> p t c", p=P)).then_inc(S["m_tab"], 16)

                load_first()
                with sp.Fori(0, QUADS) as q:
                    following = ((q + 1) & (QUADS - 1)) * QUAD
                    sp.wait_ge(S["m_xsum"], START + q + 1)
                    settle()
                    sp.dma_start(u_in[:], rowtiles(src, following, QW)).then_inc(S["m_loaded"], 16)
                    sp.wait_ge(S["m_bmul"], START + 4 * q + 4)
                    sp.dma_start(rope_raw[:].rearrange("p w a b c -> p w (a b c)")[:, :, 0:2 * D_STATE],
                                 t["m_rope"][bass.ds(following, QUAD), :].rearrange("(t p) c -> p t c", p=P)).then_inc(S["m_tab"], 16)
                    sp.wait_ge(S["m_out"], START + 4 * q + 4)
                    sp.dma_start(rowtiles(t["m_out"], q * QUAD, QW), xsum).then_inc(S["m_out_stored"], 16)
                    sp.wait_ge(S["m_u0"], START + q + 1)
                    for h in range(2):
                        sp.wait_ge(S[f"u_stored{h}"], START + 16 * (24 * len(blocks[:1]) + q))
                        settle()
                        sp.dma_start(rowtiles(U, region_row(q) + h * 2 * P, 2), u0[:, 2 * h:2 * h + 2, :]).then_inc(S[f"u_stored{h}"], 16)
                sp.wait_ge(S["m_out_stored"], START + 16 * QUADS)
                sp.wait_ge(S["m_loaded"], START + 16 * (QUADS + 1))
                sp.wait_ge(S["m_tab"], START + 16 * (QUADS + 1))
                sp.wait_ge(S["m_bmul"], START + 34)
                sp.wait_ge(S["m_z2h"], START + 33)
                sp.wait_ge(S["m_xsum"], START + QUADS + 1)

            for b in blocks:
                stack(b)
                if b == 0 and mix:
                    state_space()
            if not blocks:
                state_space()

        @block.tensor
        def _(pe):
            start_counts(pe, 1)
            def split_product(out, left, right, first, last):
                ins = None
                for n, (a, c) in enumerate(((0, 0), (0, 1), (1, 0))):
                    ins = nc.tensor.matmul(out, left[a], right[c], start=(first and n == 0), stop=(last and n == 2))
                return ins

            def project(x, part, out, done):
                for k in range(KT):
                    ins = split_product(out, [a[:, k * P:(k + 1) * P] for a in xT],
                                        [a[:, k, part * INNER:(part + 1) * INNER] for a in wqkv], k == 0, k == KT - 1)
                ins.then_inc(S[done], 1)

            def transpose_qk(x, part):
                pe.wait_ge(S["k_ready" if part else "rope_q"], START + x + 1)
                for c in range(OT):
                    o = part * INNER + c * P
                    ins = nc.tensor.transpose(QK[:, o:o + P], qk[:, part, 2 * c:2 * c + 2, :].rearrange("p h d -> p (h d)"), ident[:])
                ins.then_inc(S["kT_psum" if part else "qT_psum"], 1)

            def transpose_hidden(f, hn, bank):
                pe.wait_ge(S["hn_done"], START + f + 1)
                for k in range(KT):
                    for tt in range(2):
                        ins = nc.tensor.transpose(bank[:, (2 * k + tt) * P:(2 * k + tt + 1) * P], hn[:, tt, k * P:(k + 1) * P], ident[:])
                ins.then_inc(S["hT_psum"], 1)

            def transpose_o(w, v_count):
                pe.wait_ge(S["o_norm"], START + w + 1)
                pe.wait_ge(S["v_sb"], START + v_count)
                for c in range(OT):
                    ins = nc.tensor.transpose(VB[:, c * P:(c + 1) * P],
                                              o_sb[:, 2 * c:2 * c + 2, :].rearrange("p h d -> p (h d)"), ident[:])
                ins.then_inc(S["oT_psum"], 1)

            def out_project(w):
                pe.wait_ge(S["oT_lo"], START + w + 1)
                for c in range(OT):
                    ins = split_product(OB[:, 0:DIM], [a[:, c, :] for a in oT], [a[:, c, :] for a in wo],
                                        c == 0, c == OT - 1)
                ins.then_inc(S["wo_out"], 1)

            def stack(b):
                pe.wait_ge(S["wqkv_ready"], START + 2 * b + 1)
                x = 65 * b
                if b:
                    pe.wait_ge(S["x2_done"], START + 32 * b)
                pe.wait_ge(S["u_loaded0"], START + 32 * (17 * b + 1))
                nc.tensor.transpose(TP[0][:, 0:P], u_in[:, 0, 0:P], ident[:])
                nc.tensor.transpose(TP[0][:, P:2 * P], u_shift[:, 0, :], ident[:]).then_inc(S["xT_psum"], 1)
                pe.wait_ge(S["xT_lo"], START + x + 1)
                project(x, 1, QK[:, INNER:2 * INNER], "k_proj")
                project(x, 0, QK[:, 0:INNER], "q_proj")
                project(x, 2, VB[:], "v_proj")
                transpose_qk(x, 1)
                transpose_qk(x, 0)
                with pe.Fori(0, TRIPS) as i:
                    for j in range(QW):
                        attention(b, i, j)
                    feed_forward(b, i)

            def attention(b, i, j):
                w = 64 * b + 4 * i + j
                x = 65 * b + 4 * i + j + 1
                nj = (j + 1) % QW
                def score(hp):
                    bank = SC[hp % 2]
                    both = slice(0, QW, QW - 1) if j == 0 else slice(j - 1, j + 1)
                    for hh, h in enumerate(pair_heads(hp)):
                        r = slice((h % 2) * HD, (h % 2 + 1) * HD)
                        ins = nc.tensor.matmul(bank[:, hh * 2 * P:(hh + 1) * 2 * P], qT[r, h // 2, :], kT[r, h // 2, both, :],
                                               start=True, stop=True)
                    ins.then_inc(S["scores"], 1)

                def probs_T(hp):
                    pe.wait_ge(S["exp_done"], START + 4 * w + hp + 1)
                    for q in range(4):
                        ins = nc.tensor.transpose(TP[hp % 2][:, q * P:(q + 1) * P],
                                                  probs[:, hp % 2, q // 2, (q % 2) * P:(q % 2 + 1) * P], ident[:])
                    ins.then_inc(S["probsT_psum"], 1)

                def weigh(hp):
                    if hp == OT - 1:
                        pe.wait_ge(S["ptD"], START + w + 1)
                    else:
                        pe.wait_ge(S["ptA"], START + 3 * w + hp + 1)
                    if hp == 0:
                        pe.wait_ge(S["v_sb"], START + x)
                        pe.wait_ge(S["x1_done"], START + w)
                        if j == 0:
                            pe.wait_ge(S["x2_done"], START + 2 * (16 * b + i))
                    for hh, h in enumerate(pair_heads(hp)):
                        for s in range(2):
                            slot = (0, QW - 1)[s] if j == 0 else j - 1 + s
                            ins = nc.tensor.matmul(OB[:, h * HD:(h + 1) * HD], pT[:, hp % 2, 2 * hh + s, :],
                                                   V[:, slot, h * HD:(h + 1) * HD], start=(s == 0), stop=(s == 1))
                    if hp == OT - 1:
                        ins.then_inc(S["attn_psum"], 1)

                u_count = 17 * b + i + (2 if nj == 0 else 1)
                pe.wait_ge(S[f"u_loaded{nj}"], START + 32 * u_count)
                nc.tensor.transpose(TP[0][:, 0:P], u_in[:, nj, 0:P], ident[:])
                nc.tensor.transpose(TP[0][:, P:2 * P], u_shift[:, nj, :], ident[:]).then_inc(S["xT_psum"], 1)
                pe.wait_ge(S["kT_sb"], START + x)
                pe.wait_ge(S["qT_sb"], START + x)
                score(0)
                if j:
                    transpose_o(w - 1, x)
                score(1)
                pe.wait_ge(S["xT_lo"], START + x + 1)
                if j == QW - 1:
                    pe.wait_ge(S["wqkv_ready"], START + 2 * b + 1 + (((i + 1) >> 3) & 1))
                project(x, 1, QK[:, INNER:2 * INNER], "k_proj")
                if j:
                    if j == 1:
                        pe.wait_ge(S["rest_ready"], START + 3 * (2 * b + (i >> 3)) + 1)
                    out_project(w - 1)
                project(x, 0, QK[:, 0:INNER], "q_proj")
                probs_T(0)
                if j == QW - 1:
                    project(x, 2, VB[:], "v_proj")
                score(2)
                probs_T(1)
                weigh(0)
                score(3)
                if j == QW - 1:
                    pe.wait_ge(S["v_sb"], START + x + 1)
                    transpose_hidden(2 * (16 * b + i), hn[0], VB)
                else:
                    project(x, 2, VB[:], "v_proj")
                probs_T(2)
                weigh(1)
                probs_T(3)
                transpose_qk(x, 1)
                if j < QW - 1:
                    transpose_qk(x, 0)
                weigh(2)
                weigh(3)
                if j == QW - 1:
                    transpose_qk(x, 0)

            def feed_forward(b, i):
                w3 = 64 * b + 4 * i + 3
                ring = [SC[0], SC[1], TP[1]]
                for h in range(2):
                    f = 2 * (16 * b + i) + h

                    def down(tt, c):
                        if tt == 0 and c == 0:
                            if h == 0:
                                pe.wait_ge(S["x1_done"], START + w3 + 1)
                                pe.wait_ge(S["rest_ready"], START + 3 * (2 * b + (i >> 3)) + 3)
                            else:
                                pe.wait_ge(S["x2_done"], START + f)
                        if tt == 0:
                            pe.wait_ge(S["gg_ready"], START + 6 * f + c + 1)
                        return split_product(OB[:, tt * DIM:(tt + 1) * DIM],
                                             [a[:, c, tt * P:(tt + 1) * P] for a in gg],
                                             [a[:, c, :] for a in w2], c == 0, c == HC - 1)

                    pe.wait_ge(S["hT_ready"], START + f + 1)
                    for c in range(HC):
                        if h == 0 and c == 0:
                            pe.wait_ge(S["rest_ready"], START + 3 * (2 * b + (i >> 3)) + 2)
                        if c >= 3:
                            pe.wait_ge(S["gf_done"], START + 6 * f + c - 2)
                        for part, s in ((0, 1), (1, 0)):
                            for k in range(KT):
                                ins = split_product(ring[c % 3][:, part * 2 * P:(part + 1) * 2 * P],
                                                    [a[:, k, s, c * P:(c + 1) * P] for a in w1],
                                                    [a[:, k, :] for a in hT[h]], k == 0, k == KT - 1)
                            if h == 0 and c == 0 and part == 0:
                                pe.wait_ge(S["hT_f"], START + f + 1)
                                transpose_o(w3, 65 * b + 4 * i + 5)
                        ins.then_inc(S["ga_psum"], 1)
                        if h == 0 and c == 1:
                            out_project(w3)
                        if c >= DOWN_LAG:
                            down(0, c - DOWN_LAG)
                    for c in range(HC - DOWN_LAG, HC):
                        down(0, c)
                    if h == 0:
                        transpose_hidden(f + 1, hn[1], TP[0])
                    for c in range(HC):
                        ins = down(1, c)
                    ins.then_inc(S["w2_out"], 1)

            def state_space():
                def transpose_h(slot, quad):
                    pe.wait_ge(S["m_hn"], START + quad)
                    for k in range(KT):
                        ins = nc.tensor.transpose(SC[0][:, k * P:(k + 1) * P], hm[:, slot, k * P:(k + 1) * P], ident[:])
                    ins.then_inc(S["m_hT_psum"], 1)

                def in_project(out, c0, n, done):
                    for k in range(KT):
                        ins = split_product(out, [a[:, k, 0:P] for a in mh], [a[:, k, c0:c0 + n] for a in w_in],
                                            k == 0, k == KT - 1)
                    ins.then_inc(S[done], 1)

                def project_bcdt(x):
                    pe.wait_ge(S["m_hT"], START + x + 1)
                    in_project(VB[:, 0:BCDT], 2 * INNER, BCDT, "m_b_proj")

                def transpose_bc(x, s):
                    pe.wait_ge(S["m_bc"], START + x + 1)
                    pe.wait_ge(S["m_scT"], START + x)
                    pe.wait_ge(S["m_ex"], START + x)
                    nc.tensor.transpose(TP[1][0:D_STATE, 0:P], bcr[s][:, 0:D_STATE], ident[:])
                    nc.tensor.transpose(TP[1][0:D_STATE, P:2 * P], bcr[s][:, D_STATE:2 * D_STATE], ident[:]).then_inc(S["m_bcT_psum"], 1)

                def sums(x):
                    pe.wait_ge(S["m_bcT"], START + x + 1)
                    nc.tensor.matmul(TP[1][:, 2 * P:3 * P], bcT[:, 0:P], bcT[:, P:2 * P], start=True, stop=True)
                    pe.wait_ge(S["m_a"], START + x + 1)
                    for n, left in enumerate((tri, after, ones)):
                        ins = nc.tensor.matmul(TP[1][:, 3 * P + n * NH:3 * P + (n + 1) * NH], left, a_, start=True, stop=True)
                    ins.then_inc(S["m_misc"], 1)

                def segment_sums(x):
                    pe.wait_ge(S["m_atri"], START + x + 1)
                    pe.wait_ge(S["m_hTf"], START + x + 2)
                    for n in range(2):
                        ins = nc.tensor.matmul(SC[n][:], after, a_tri[:, n * 4 * P:(n + 1) * 4 * P], start=True, stop=True)
                    ins.then_inc(S["m_d"], 1)

                def transpose_y(m):
                    pe.wait_ge(S["m_yn"], START + m + 1)
                    for c in range(OT):
                        ins = nc.tensor.transpose(TP[0][:, c * P:(c + 1) * P],
                                                  yn[:, 2 * c:2 * c + 2, :].rearrange("p h d -> p (h d)"), ident[:])
                    ins.then_inc(S["m_yT_psum"], 1)

                def out_project(m):
                    pe.wait_ge(S["m_yT"], START + m + 1)
                    for c in range(OT):
                        ins = split_product(TP[0][:, 0:DIM], [a[:, c, :] for a in oT], [a[:, c, :] for a in w_out],
                                            c == 0, c == OT - 1)
                    ins.then_inc(S["m_mo"], 1)

                pe.wait_ge(S["m_par_done"], START + 2)
                transpose_h(0, 1)
                project_bcdt(0)
                in_project(QK[:, INNER:2 * INNER], INNER, INNER, "m_x_proj")
                in_project(QK[:, 0:INNER], 0, INNER, "m_z_proj")
                transpose_bc(0, 0)
                sums(0)
                transpose_h(1, 1)
                segment_sums(0)
                pe.wait_ge(S["m_v"], START + 1)
                project_bcdt(1)
                with pe.Fori(0, QUADS) as q:
                    for j in range(QW):
                        m = 4 * q + j
                        x = m + 1
                        if j:
                            pe.wait_ge(S["m_t2"], START + m)
                            project_bcdt(x)
                        pe.wait_ge(S["m_x2h"], START + x)
                        in_project(QK[:, INNER:2 * INNER], INNER, INNER, "m_x_proj")
                        pe.wait_ge(S["m_out"], START + (m if j == 0 else m - 1))
                        if j:
                            transpose_y(m - 1)
                        pe.wait_ge(S["m_z2h"], START + x)
                        in_project(QK[:, 0:INNER], 0, INNER, "m_z_proj")
                        pe.wait_ge(S["m_L"], START + x)
                        transpose_h((j + 2) % QW, q + (2 if j >= QW - 2 else 1))
                        pe.wait_ge(S["m_state"], START + m + 1)
                        nc.tensor.matmul(OB[:], bcT[:, P:2 * P], state, start=True, stop=True).then_inc(S["m_yo"], 1)
                        pe.wait_ge(S["m_v"], START + x + 1)
                        pe.wait_ge(S["m_MT"], START + m + 1)
                        pe.wait_ge(S["m_xc"], START + m + 1)
                        for h in range(NH):
                            ins = nc.tensor.matmul(VB[:, h * HD:(h + 1) * HD], mT[:, h * P:(h + 1) * P],
                                                   xc[:, h * HD:(h + 1) * HD], start=True, stop=True)
                        ins.then_inc(S["m_yd"], 1)
                        transpose_bc(x, (j + 1) % 2)
                        if j:
                            out_project(m - 1)
                        sums(x)
                        pe.wait_ge(S["m_t1"], START + m + 1)
                        pe.wait_ge(S["m_xcd"], START + m + 1)
                        nc.tensor.matmul(OB[0:D_STATE, :], bcr[j % 2][:, 0:D_STATE], xcd, start=True, stop=True).then_inc(S["m_upd"], 1)
                        segment_sums(x)
                        if j == QW - 1:
                            pe.wait_ge(S["m_t2"], START + m + 1)
                            project_bcdt(x + 1)
                            pe.wait_ge(S["m_out"], START + m)
                            transpose_y(m)
                            out_project(m)

            pe.wait_ge(S["const_done"], START + 3)
            for b in blocks:
                stack(b)
                if b == 0 and mix:
                    state_space()
            if not blocks:
                state_space()

        @block.scalar
        def _(act):
            start_counts(act, 2)

            def load_constants():
                for dst, src in ((ident[:], t["ident"]), (mask_first[:, 0:P], t["mask"][:, P:2 * P]), (mask_rest[:], t["mask"])):
                    act.dma_start(dst, src).then_inc(S["const_loaded"], 16)
                for l in range(LAYERS):
                    sm = small_raw[:, l, :]
                    for g, w in ((0, t["q_scale"]), (1, t["k_scale"])):
                        for cs in range(2):
                            o = FAC + (2 * g + cs) * HD
                            if cs == 0:
                                parts = ((0, 0, HD),)
                            else:
                                parts = ((0, HD // 2, HD // 2), (HD // 2, 0, HD // 2))
                            for d0, s0, n in parts:
                                act.dma_start(sm[:, o + d0:o + d0 + n], w[l:l + 1, s0:s0 + n].to_broadcast([P, n])).then_inc(S["const_loaded"], 16)
                    act.dma_start(sm[:, B2:B2 + DIM], t["b2"][l:l + 1, :].to_broadcast([P, DIM])).then_inc(S["const_loaded"], 16)
                    with nc.allow_non_contiguous_dma("parameters laid along partitions, once"):
                        for o, w in ((LG, t["ln_g"]), (LB, t["ln_b"])):
                            act.dma_start(sm[:, o:o + KT], w[l, :].rearrange("(k p) -> p k", p=P)).then_inc(S["const_loaded"], 16)
                        for o, h in ((B1A, 0), (B1G, HID)):
                            act.dma_start(sm[:, o:o + HC - 1], t["b1"][l, h:h + (HC - 1) * P].rearrange("(k p) -> p k", p=P)).then_inc(S["const_loaded"], 16)
                act.wait_ge(S["const_done"], START + 1)
                with nc.allow_non_contiguous_dma("parameters laid along partitions, once"):
                    for l in range(LAYERS):
                        for o, h in ((B1A, 0), (B1G, HID)):
                            act.dma_start(small_raw[0:HTAIL, l, o + HC - 1:o + HC],
                                         t["b1"][l, h + (HC - 1) * P:h + HID].rearrange("(p k) -> p k", k=1)).then_inc(S["const_loaded"], 16)
                for r in range(LAYERS + 1):
                    act.dma_start(U[r * REGION + QUAD - 1:r * REGION + QUAD, :], zrow[:]).then_inc(S["zero_stored"], 16)

            def split_hi(raw, hi, loaded, count, done):
                act.wait_ge(S[loaded], START + count)
                nc.scalar.activation(hi, raw, ACT.Copy).then_inc(S[done], 1)

            def hi_qkv(n):
                split_hi(wqkv_raw[:].rearrange("p k n -> p (k n)"), wqkv[0][:].rearrange("p k n -> p (k n)"), "raw_qkv", 16 * n, "wqkv_hi")

            def hi_rest(n):
                split_hi(wo_raw[:].rearrange("p k n -> p (k n)"), wo[0][:].rearrange("p k n -> p (k n)"), "raw_o", 16 * n, "rest_hi")
                split_hi(w1_raw[:].rearrange("p k s n -> p (k s n)"), w1[0][:].rearrange("p k s n -> p (k s n)"), "raw_1", 32 * n, "rest_hi")
                split_hi(w2_raw[:].rearrange("p k n -> p (k n)"), w2[0][:].rearrange("p k n -> p (k n)"), "raw_2", 32 * n, "rest_hi")

            def xT_high(x):
                act.wait_ge(S["xT_psum"], START + x + 1)
                nc.scalar.activation(xT[0][:], TP[0][:, 0:DIM], ACT.Copy).then_inc(S["xT_hi"], 1)

            def squares_k(x):
                act.wait_ge(S["k_proj"], START + x + 1)
                act.wait_ge(S["ss_done"], START + 2 * x)
                nc.scalar.activation(sq[:, INNER:2 * INNER], QK[:, INNER:2 * INNER], ACT.Square).then_inc(S["sq_done"], 1)

            def squares_q(x):
                act.wait_ge(S["q_proj"], START + x + 1)
                nc.scalar.activation(sq[:, 0:INNER], QK[:, 0:INNER], ACT.Square).then_inc(S["sq_done"], 1)

            def qT_out(x):
                act.wait_ge(S["qT_psum"], START + x + 1)
                nc.scalar.activation(qT[:].rearrange("p c t -> p (c t)"), QK[:, 0:INNER], ACT.Copy).then_inc(S["qT_sb"], 1)

            def v_out(x, slot):
                act.wait_ge(S["v_proj"], START + x + 1)
                nc.scalar.activation(V[:, slot, :], VB[:], ACT.Copy).then_inc(S["v_sb"], 1)

            def oT_high(w):
                act.wait_ge(S["oT_psum"], START + w + 1)
                nc.scalar.activation(oT[0][:].rearrange("p c t -> p (c t)"), VB[:], ACT.Copy).then_inc(S["oT_hi"], 1)

            def attention(b, i, j):
                w = 64 * b + 4 * i + j
                x = 65 * b + 4 * i + j + 1

                def exps(hp):
                    act.wait_ge(S["negmax"], START + 4 * w + hp + 1)
                    for hh, h in enumerate(pair_heads(hp)):
                        ins = nc.scalar.activation(probs[:, hp % 2, hh, :], probs[:, hp % 2, hh, :],
                                                   ACT.Exp, bias=neg_maxima[:, h:h + 1], scale=inv_norm[:, j % 2, h:h + 1],
                                                   accum_out=rowsum[:, h:h + 1])
                    ins.then_inc(S["exp_done"], 1)

                def pT_out(hp):
                    act.wait_ge(S["probsT_psum"], START + 4 * w + hp + 1)
                    nc.scalar.activation(pT[:, hp % 2].rearrange("p q t -> p (q t)"), TP[hp % 2][:], ACT.Copy).then_inc(S["ptA"], 1)

                xT_high(x)
                if j:
                    oT_high(w - 1)
                exps(0)
                squares_k(x)
                exps(1)
                squares_q(x)
                pT_out(0)
                pT_out(1)
                if j == QW - 1:
                    v_out(x, (j + 1) % QW)
                exps(2)
                exps(3)
                pT_out(2)
                if j == QW - 1:
                    hidden_in(2 * (16 * b + i), hTf[0], VB)
                else:
                    v_out(x, (j + 1) % QW)
                qT_out(x)

            def hidden_in(f, hTf, bank):
                act.wait_ge(S["hT_psum"], START + f + 1)
                for k in range(KT):
                    ins = nc.scalar.activation(hTf[:, k, :], bank[:, k * 2 * P:(k + 1) * 2 * P], ACT.Identity,
                                               bias=small[:, LB + k:LB + k + 1], scale=small[:, LG + k:LG + k + 1])
                ins.then_inc(S["hT_f"], 1)

            def feed_forward(b, i):
                for h in range(2):
                    f = 2 * (16 * b + i) + h
                    if h == 0:
                        oT_high(64 * b + 4 * i + 3)
                    for c in range(HC):
                        act.wait_ge(S["ga_psum"], START + 6 * f + c + 1)
                        if c < 2:
                            act.wait_ge(S["gf_done"], START + 6 * f)
                        else:
                            act.wait_ge(S["gf_done"], START + 6 * f + c - 1)
                        nc.scalar.activation(gl[:, c % 2, :], (SC[0], SC[1], TP[1])[c % 3][:, 0:2 * P], ACT.Gelu,
                                             bias=small[:, B1G + c:B1G + c + 1]).then_inc(S["gelu_done"], 1)
                    if h == 0:
                        hidden_in(f + 1, hTf[1], TP[0])

            def stack(b):
                hi_qkv(2 * b + 1)
                hi_rest(2 * b + 1)
                act.wait_ge(S["const_done"], START + 3)
                xT_high(65 * b)
                squares_k(65 * b)
                squares_q(65 * b)
                v_out(65 * b, 0)
                qT_out(65 * b)
                with act.Fori(0, TRIPS) as i:
                    for j in range(QW):
                        if j == QW - 1:
                            with act.If(i == QUADS - 1):
                                act.wait_ge(S["v_proj"], START + 65 * b + 32)
                                hi_qkv(2 * b + 2)
                        attention(b, i, j)
                    feed_forward(b, i)
                    with act.If(i == QUADS - 1):
                        act.wait_ge(S["w2_out"], START + 32 * b + 16)
                        hi_rest(2 * b + 2)

            def state_space():
                A = nc.scalar.activation
                act.wait_ge(S["m_par"], START + 16 * 11)

                A(w_in[0], w_in_raw, ACT.Copy)
                for c in range(OT):
                    A(w_out[0][:, c, :], w_out_raw[:, c, :], ACT.Copy, scale=small[:, RMSW + c:RMSW + c + 1])
                A(small[:, NEGA:NEGA + NH], small[:, NEGA:NEGA + NH], ACT.Exp).then_inc(S["m_par_done"], 1)

                def h_out(x):
                    act.wait_ge(S["m_hT_psum"], START + x + 1)
                    for k in range(KT):
                        ins = A(mhf[:, k, 0:P], SC[0][:, k * P:(k + 1) * P], ACT.Identity,
                                bias=small[:, LNBM + k:LNBM + k + 1], scale=small[:, LNW + k:LNW + k + 1])
                    ins.then_inc(S["m_hTf"], 1)

                def gates_bcdt(x):
                    act.wait_ge(S["m_b_proj"], START + x + 1)
                    A(tbc, VB[:, 0:2 * D_STATE], ACT.Tanh, scale=0.5).then_inc(S["m_tbc"], 1)
                    act.wait_ge(S["m_v"], START + x + 1)
                    A(av_, v_, ACT.Abs).then_inc(S["m_abs"], 1)
                    act.wait_ge(S["m_abs"], START + x + 1)
                    A(e_, av_, ACT.Exp, scale=-1.0).then_inc(S["m_e"], 1)

                def gates_xz(x):
                    act.wait_ge(S["m_x_proj"], START + x + 1)
                    A(sq[:, INNER:2 * INNER], QK[:, INNER:2 * INNER], ACT.Tanh, scale=0.5).then_inc(S["m_tx"], 1)
                    act.wait_ge(S["m_z_proj"], START + x + 1)
                    A(sq[:, 0:INNER], QK[:, 0:INNER], ACT.Tanh, scale=0.5).then_inc(S["m_tz"], 1)

                def yT_high(m):
                    act.wait_ge(S["m_yT_psum"], START + m + 1)
                    A(oT[0][:].rearrange("p c t -> p (c t)"), TP[0][:], ACT.Copy).then_inc(S["m_yT_hi"], 1)

                def decays(x, s):
                    act.wait_ge(S["m_misc"], START + x + 1)
                    A(ex[s], TP[1][:, 3 * P:3 * P + 3 * NH], ACT.Exp).then_inc(S["m_ex"], 1)
                    act.wait_ge(S["m_MT"], START + x)
                    act.wait_ge(S["m_d"], START + x + 1)
                    for n in range(2):
                        ins = A(decay[:, n * 4 * P:(n + 1) * 4 * P], SC[n][:], ACT.Exp)
                    ins.then_inc(S["m_L"], 1)

                h_out(0)
                gates_bcdt(0)
                gates_xz(0)
                h_out(1)
                decays(0, 0)
                gates_bcdt(1)
                with act.Fori(0, QUADS) as q:
                    for j in range(QW):
                        m = 4 * q + j
                        x = m + 1
                        if j:
                            gates_bcdt(x)
                            yT_high(m - 1)
                        gates_xz(x)
                        h_out(m + 2)
                        act.wait_ge(S["m_y2"], START + m + 1)
                        A(ysq[:], y2, ACT.Square, accum_out=ssum).then_inc(S["m_sq"], 1)
                        decays(x, (j + 1) % 2)
                        if j == QW - 1:
                            yT_high(m)
                            gates_bcdt(x + 1)

            load_constants()
            for b in blocks:
                stack(b)
                if b == 0 and mix:
                    state_space()
            if not blocks:
                state_space()

        @block.vector
        def _(dve):
            V_ = nc.vector
            start_counts(dve, 3)

            def split_lo(raw, pair, hi_done, n, done):
                dve.wait_ge(S[hi_done], START + n)
                V_.tensor_tensor(pair[1], raw, pair[0].bitcast(F32), ALU.subtract).then_inc(S[done], 1)

            def lo_qkv(n):
                split_lo(wqkv_raw[:].rearrange("p k n -> p (k n)"), [a[:].rearrange("p k n -> p (k n)") for a in wqkv], "wqkv_hi", n, "wqkv_ready")

            def lo_rest(n):
                split_lo(wo_raw[:].rearrange("p k n -> p (k n)"), [a[:].rearrange("p k n -> p (k n)") for a in wo], "rest_hi", 3 * n - 2, "rest_ready")
                split_lo(w1_raw[:].rearrange("p k s n -> p (k s n)"), [a[:].rearrange("p k s n -> p (k s n)") for a in w1], "rest_hi", 3 * n - 1, "rest_ready")
                split_lo(w2_raw[:].rearrange("p k n -> p (k n)"), [a[:].rearrange("p k n -> p (k n)") for a in w2], "rest_hi", 3 * n, "rest_ready")

            def xT_low(x):
                dve.wait_ge(S["xT_hi"], START + x + 1)
                V_.tensor_tensor(xT[1][:], TP[0][:, 0:DIM], xT[0][:].bitcast(F32), ALU.subtract).then_inc(S["xT_lo"], 1)

            def rope_products(x, xs, part, done):
                dve.wait_ge(S["sq_done"], START + 2 * x + 2 - part)
                if part:
                    dve.wait_ge(S["fold_done"], START + x + 1)
                    dve.wait_ge(S["k_ready"], START + x)
                else:
                    dve.wait_ge(S["rope_q"], START + x)
                src = QK[:, part * INNER:(part + 1) * INNER].rearrange("p (h d) -> p h d", d=HD)
                H2 = HD // 2
                cos = rope[:, xs, part, 0, :].unsqueeze(1).to_broadcast([P, HEADS, HD])
                V_.tensor_tensor(by_cos[:, part], src, cos, ALU.mult)
                for o, s in ((0, H2), (H2, 0)):
                    sin = rope[:, xs, part, 1, o:o + H2].unsqueeze(1).to_broadcast([P, HEADS, H2])
                    ins = V_.tensor_tensor(by_sin[:, part, :, o:o + H2], src[:, :, s:s + H2], sin, ALU.mult)
                ins.then_inc(S[done], 1)

            def kT_out(x, slot):
                dve.wait_ge(S["kT_psum"], START + x + 1)
                V_.tensor_copy(kT[:, :, slot, :], QK[:, INNER:2 * INNER].rearrange("p (c t) -> p c t", c=OT)).then_inc(S["kT_sb"], 1)

            def sum_squares(x, part):
                n = 2 * x + 2 - part
                o = part * HEADS
                dve.wait_ge(S["sq_done"], START + n)
                V_.tensor_reduce(sq_sums[:, o:o + HEADS], sq[:, part * INNER:(part + 1) * INNER].rearrange("p (h d) -> p h d", d=HD),
                                 AX.X, ALU.add).then_inc(S["ss_done"], 1)
                dve.wait_ge(S["ss_done"], START + n)
                V_.tensor_scalar(sq_sums_clipped[:, o:o + HEADS], sq_sums[:, o:o + HEADS], 1e-24, None, ALU.max).then_inc(S["rn_clip"], 1)

            def oT_low(w):
                dve.wait_ge(S["oT_hi"], START + w + 1)
                V_.tensor_tensor(oT[1][:].rearrange("p c t -> p (c t)"), VB[:],
                                 oT[0][:].rearrange("p c t -> p (c t)").bitcast(F32), ALU.subtract).then_inc(S["oT_lo"], 1)

            def residual1(w, b, i, j):
                dve.wait_ge(S["wo_out"], START + w + 1)
                dve.wait_ge(S["bias_added"], START + 2 * (16 * b + i))
                V_.tensor_tensor(x1[:, j, :], OB[:, 0:DIM], u_in[:, j, :], ALU.add).then_inc(S["x1_done"], 1)

            def attention(b, i, j):
                w = 64 * b + 4 * i + j
                x = 65 * b + 4 * i + j + 1
                f0 = 2 * (16 * b + i)

                def mask_max(hp):
                    dve.wait_ge(S["scores"], START + 4 * w + hp + 1)
                    V_.memset(gap[:], 0.0)
                    m = mask_rest if j else mask_first
                    for hh, h in enumerate(pair_heads(hp)):
                        ins = V_.tensor_tensor_reduce(probs[:, hp % 2, hh, :], SC[hp % 2][:, hh * 2 * P:(hh + 1) * 2 * P], m[:],
                                                      1.0, LOWEST, ALU.add, ALU.max, row_maxima[:, h:h + 1])
                    ins.then_inc(S["max_done"], 1)

                def neg_max(hp):
                    h0, h1 = pair_heads(hp)
                    dve.wait_ge(S["max_done"], START + 4 * w + hp + 1)
                    if hp == 0:
                        dve.wait_ge(S["rn_done"], START + 2 * x)
                    V_.scalar_tensor_tensor(neg_maxima[:, h0:h1 + 1:2], row_maxima[:, h0:h1 + 1:2], -1.0,
                                            inv_norm[:, j % 2, h0:h1 + 1:2], ALU.mult, ALU.mult).then_inc(S["negmax"], 1)

                def row_max(hp):
                    mask_max(hp)
                    neg_max(hp)

                def pT_out(hp):
                    dve.wait_ge(S["probsT_psum"], START + 4 * w + hp + 1)
                    V_.tensor_copy(pT[:, hp % 2].rearrange("p q t -> p (q t)"), TP[hp % 2][:]).then_inc(S["ptD"], 1)

                xT_low(x)
                mask_max(0)
                neg_max(0)
                if j:
                    oT_low(w - 1)
                row_max(1)
                if j == QW - 1:
                    norm_stats(f0, 48 * (16 * b + i + 1), 0)
                sum_squares(x, 1)
                rope_products(x, (j + 1) % 2, 1, "mulk")
                if j:
                    residual1(w - 1, b, i, j - 1)
                if j == QW - 1:
                    dve.wait_ge(S["out_done1"], START + 16 * b + i)
                    normalise(f0, 0)
                    row_max(2)
                rope_products(x, (j + 1) % 2, 0, "mulq")
                if j < QW - 1:
                    row_max(2)
                if j == 1:
                    V_.tensor_copy(mask_first[:, P:2 * P], mask_rest[:, 0:P])
                row_max(3)
                sum_squares(x, 0)
                pT_out(3)
                if j == QW - 1:
                    with dve.If(((i + 1) & (QUADS - 1)) == 0):
                        dve.wait_ge(S["kT_psum"], START + x + 1)
                        V_.memset(kT[:, :, QW - 1, :], 0.0)
                        V_.memset(mask_first[:, P:2 * P], MASKED)
                kT_out(x, (j + 1) % QW)
                if j == QW - 1:
                    hidden_split(f0, 0)
                dve.wait_ge(S["exp_done"], START + 4 * w + 4)
                V_.reciprocal(rinv[:], rowsum[:]).then_inc(S["rinv_done"], 1)
                dve.wait_ge(S["attn_psum"], START + w + 1)
                dve.wait_ge(S["rinv_done"], START + w + 1)
                V_.tensor_tensor(o_sb[:], OB[:].rearrange("p (h d) -> p h d", d=HD),
                                 rinv[:].unsqueeze(2).to_broadcast([P, HEADS, HD]), ALU.mult).then_inc(S["o_norm"], 1)

            def norm_stats(f, loaded, h):
                dve.wait_ge(S[f"x1s_loaded{h}"], START + loaded)
                for tt in range(2):
                    V_.bn_stats(stats[:, tt, 0, :], x1[:, 2 * h + tt, 0:P])
                    ins = V_.bn_stats(stats[:, tt, 1, :], x1s[:, h, tt, :])
                ins.then_inc(S["stats_done"], 1)
                dve.wait_ge(S["stats_done"], START + f + 1)
                V_.memset(gap[:], 0.0)
                for tt in range(2):
                    ins = V_.bn_aggr(mv[:, tt, :], stats[:, tt].rearrange("p a s -> p (a s)"))
                ins.then_inc(S["mv_done"], 1)

            def normalise(f, h):
                dve.wait_ge(S["rstd_done"], START + f + 1)
                for tt in range(2):
                    for k, src in ((0, x1[:, 2 * h + tt, 0:P]), (1, x1s[:, h, tt, :])):
                        ins = V_.tensor_scalar(hn[h][:, tt, k * P:(k + 1) * P], src, mv[:, tt, 0:1], rstd[:, tt:tt + 1],
                                               ALU.subtract, ALU.mult)
                ins.then_inc(S["hn_done"], 1)

            def hidden_split(f, h):
                dve.wait_ge(S["hT_f"], START + f + 1)
                V_.tensor_copy(hT[h][0], hTf[h]).then_inc(S["hT_hi"], 1)
                dve.wait_ge(S["hT_hi"], START + f + 1)
                V_.tensor_tensor(hT[h][1], hTf[h], hT[h][0].bitcast(F32), ALU.subtract).then_inc(S["hT_ready"], 1)

            def feed_forward(b, i):
                w3 = 64 * b + 4 * i + 3
                for h in range(2):
                    f = 2 * (16 * b + i) + h
                    if h == 0:
                        oT_low(w3)
                    for c in range(HC):
                        dve.wait_ge(S["gelu_done"], START + 6 * f + c + 1)
                        if c < 2:
                            dve.wait_ge(S["gg_ready"], START + 6 * f)
                        else:
                            dve.wait_ge(S["gg_ready"], START + 6 * f + c - 1)
                        V_.scalar_tensor_tensor(gf[:, c % 2, :], (SC[0], SC[1], TP[1])[c % 3][:, 2 * P:4 * P],
                                                small[:, B1A + c:B1A + c + 1], gl[:, c % 2, :],
                                                ALU.add, ALU.mult).then_inc(S["gf_done"], 1)
                        dve.wait_ge(S["gf_done"], START + 6 * f + c + 1)
                        V_.tensor_copy(gg[0][:, c, :], gf[:, c % 2, :]).then_inc(S["gg_hi"], 1)
                        if c == HC - 1:
                            dve.wait_ge(S["gg_hi"], START + 6 * f + 6)
                            dve.wait_ge(S["gg_ready"], START + 6 * f + 5)
                            V_.tensor_tensor(gg[1][:, c, :], gf[:, c % 2, :], gg[0][:, c, :].bitcast(F32),
                                             ALU.subtract).then_inc(S["gg_ready"], 1)
                        if h == 0 and c == 1:
                            residual1(w3, b, i, 3)
                        if h == 0 and c == 3:
                            norm_stats(f + 1, 32 * (16 * b + i + 1), 1)
                    if h == 0:
                        normalise(f + 1, 1)
                        hidden_split(f + 1, 1)
                    dve.wait_ge(S["w2_out"], START + f + 1)
                    dve.wait_ge(S["bias_added"], START + f + 1)
                    x2h_ = x2[:, h].rearrange("p t c -> p (t c)")
                    V_.tensor_tensor(x2h_, OB[:], x2h_, ALU.add).then_inc(S["x2_done"], 1)
            def input_norm():
                with dve.Fori(0, QUADS // 2) as n:
                    for s in range(2):
                        dve.wait_ge(S[f"ln_loaded{s}"], START + 16 * (n + 1))
                        dve.wait_ge(S["ln_mv"], START + 2 * n + s)
                        for tt in range(QW):
                            ins = V_.bn_stats(stats[:, tt // 2, tt % 2, :], ln_in[s][:, tt, :])
                        ins.then_inc(S["ln_stats"], 1)
                        dve.wait_ge(S["ln_stats"], START + 2 * n + s + 1)
                        V_.memset(gap[:], 0.0)
                        for tt in range(QW):
                            ins = V_.bn_aggr(mmv[:, s, tt, :], stats[:, tt // 2, tt % 2, :])
                        ins.then_inc(S["ln_mv"], 1)
                    for h in range(2):
                        dve.wait_ge(S[f"u_stored{h}"], START + 32 * n)
                    for s in range(2):
                        dve.wait_ge(S["ln_rstd"], START + 2 * n + s + 1)
                        for tt in range(QW):
                            ins = V_.tensor_scalar(ln_out[s][:, tt, :], ln_in[s][:, tt, :], mmv[:, s, tt, 0:1], mrs[:, s, tt:tt + 1],
                                                   ALU.subtract, ALU.mult)
                        ins.then_inc(S["ln_done"], 1)

            def stack(b):
                V_.tensor_copy(small[:], small_raw[:, 0, :]).then_inc(S["small_done"], 1)
                lo_qkv(2 * b + 1)
                lo_rest(2 * b + 1)
                xT_low(65 * b)
                sum_squares(65 * b, 1)
                rope_products(65 * b, 0, 1, "mulk")
                rope_products(65 * b, 0, 0, "mulq")
                sum_squares(65 * b, 0)
                V_.memset(kT[:, :, QW - 1, :], 0.0)
                V_.memset(mask_first[:, P:2 * P], MASKED)
                kT_out(65 * b, 0)
                with dve.Fori(0, TRIPS) as i:
                    for j in range(QW):
                        if j == QW - 1:
                            with dve.If(i == QUADS - 1):
                                lo_qkv(2 * b + 2)
                                dve.wait_ge(S["fold_done"], START + 65 * b + 32)
                                V_.tensor_copy(small[:, FAC:B2], small_raw[:, 1, FAC:B2]).then_inc(S["small_done"], 1)
                        attention(b, i, j)
                    feed_forward(b, i)
                    with dve.If(i == QUADS - 1):
                        lo_rest(2 * b + 2)
                        V_.tensor_copy(small[:, B2:SMALL], small_raw[:, 1, B2:SMALL])

            def state_space():
                T = V_.tensor_tensor

                def heads(a):
                    return a.unsqueeze(2).to_broadcast([a.shape[0], NH, HD])

                def chain(ins, n):
                    ins.then_inc(S["m_dchain"], 1)
                    dve.wait_ge(S["m_dchain"], START + n)

                def norm_stats(n, src, which):
                    for tt in range(QW):
                        ins = V_.bn_stats(stats[:, tt // 2, tt % 2, :], src[:, tt, :])
                    ins.then_inc(S["m_stats"], 1)
                    dve.wait_ge(S["m_stats"], START + n)
                    V_.memset(gap[:], 0.0)
                    for tt in range(QW):
                        ins = V_.bn_aggr(mmv[:, which, tt, :], stats[:, tt // 2, tt % 2, :])
                    ins.then_inc(S["m_mv"], 1)

                def normalise(dst, src, which, done):
                    for tt in range(QW):
                        ins = V_.tensor_scalar(dst[:, tt, :], src[:, tt, :], mmv[:, which, tt, 0:1], mrs[:, which, tt:tt + 1],
                                               ALU.subtract, ALU.mult)
                    ins.then_inc(S[done], 1)

                def input_stats(g):
                    dve.wait_ge(S["m_loaded"], START + 16 * (g + 1))
                    norm_stats(2 * g + 1, u_in, 0)

                def first_norm(g):
                    dve.wait_ge(S["m_rstd"], START + 2 * g + 1)
                    dve.wait_ge(S["m_xsum"], START + g)
                    normalise(xln, u_in, 0, "m_xln")
                    dve.wait_ge(S["m_xln"], START + g + 1)
                    norm_stats(2 * g + 2, xln, 1)

                def second_norm(g):
                    dve.wait_ge(S["m_rstd"], START + 2 * g + 2)
                    normalise(hm, xln, 1, "m_hn")

                def h_split(x):
                    dve.wait_ge(S["m_hTf"], START + x + 1)
                    V_.tensor_copy(mh[0][:, :, 0:P], mhf[:, :, 0:P]).then_inc(S["m_hT_hi"], 1)
                    dve.wait_ge(S["m_hT_hi"], START + x + 1)
                    T(mh[1][:, :, 0:P], mhf[:, :, 0:P], mh[0][:, :, 0:P].bitcast(F32), ALU.subtract).then_inc(S["m_hT"], 1)

                STEPS = LOG1P_TERMS + 8

                def gates_bcdt(x, slot, tabs):
                    bcr_ = bcr[slot % 2]
                    c = STEPS * x
                    dve.wait_ge(S["m_tbc"], START + x + 1)
                    chain(T(v_, VB[:, 2 * D_STATE:BCDT], mp[:, DTB:DTB + NH], ALU.add), c + 1)
                    V_.scalar_tensor_tensor(bc2, tbc, 1.0, VB[:, 0:2 * D_STATE], ALU.add, ALU.mult).then_inc(S["m_v"], 1)
                    dve.wait_ge(S["m_v"], START + x + 1)
                    dve.wait_ge(S["m_tab"], START + 16 * tabs)
                    tab = rope_raw[:].rearrange("p w a b c -> p w (a b c)")[:, slot]
                    cos, sin = tab[:, 0:D_STATE], tab[:, D_STATE:2 * D_STATE]
                    b3 = bc2.rearrange("p (g d) -> p g d", g=2)
                    T(bcr_.rearrange("p (g d) -> p g d", g=2), b3, cos.unsqueeze(1).to_broadcast([P, 2, D_STATE]), ALU.mult)
                    for o in range(2):
                        ins = T(bsin.rearrange("p (g d) -> p g d", g=2)[:, :, o:ROPE_DIM:2], b3[:, :, 1 - o:ROPE_DIM:2],
                                sin[:, o:ROPE_DIM:2].unsqueeze(1).to_broadcast([P, 2, ROPE_DIM // 2]), ALU.mult)
                    ins.then_inc(S["m_bmul"], 1)
                    dve.wait_ge(S["m_bmul"], START + x + 1)
                    b4 = bcr_.rearrange("p (g d) -> p g d", g=2)[:, :, 0:ROPE_DIM]
                    T(b4, b4, bsin.rearrange("p (g d) -> p g d", g=2)[:, :, 0:ROPE_DIM], ALU.add).then_inc(S["m_bc"], 1)
                    dve.wait_ge(S["m_e"], START + x + 1)
                    chain(V_.tensor_scalar(d_, e_, 2.0, None, ALU.add), c + 2)
                    chain(V_.reciprocal(r_, d_), c + 3)
                    chain(T(s_, e_, r_, ALU.mult), c + 4)
                    chain(T(s2_, s_, s_, ALU.mult), c + 5)
                    chain(V_.tensor_scalar(p_, s2_, 1.0 / (2 * LOG1P_TERMS - 1), None, ALU.mult), c + 6)
                    for n in range(LOG1P_TERMS - 2, 0, -1):
                        chain(V_.scalar_tensor_tensor(p_, p_, 1.0 / (2 * n + 1), s2_, ALU.add, ALU.mult), c + 6 + LOG1P_TERMS - 1 - n)
                    chain(V_.scalar_tensor_tensor(p_, p_, 1.0, s_, ALU.add, ALU.mult), c + LOG1P_TERMS + 5)
                    chain(V_.tensor_scalar(d_, v_, 0.0, None, ALU.max), c + LOG1P_TERMS + 6)
                    chain(V_.scalar_tensor_tensor(dt_, p_, 2.0, d_, ALU.mult, ALU.add), c + LOG1P_TERMS + 7)
                    chain(V_.tensor_scalar(dth_, dt_, 0.5, None, ALU.mult), c + LOG1P_TERMS + 8)
                    T(a_, dt_, mp[:, NEGA:NEGA + NH], ALU.mult).then_inc(S["m_a"], 1)

                def gate_x(x):
                    dve.wait_ge(S["m_tx"], START + x + 1)
                    dve.wait_ge(S["m_dx"], START + x)
                    V_.scalar_tensor_tensor(x2h.rearrange("p h d -> p (h d)"), sq[:, INNER:2 * INNER], 1.0, QK[:, INNER:2 * INNER],
                                            ALU.add, ALU.mult).then_inc(S["m_x2h"], 1)
                    dve.wait_ge(S["m_x2h"], START + x + 1)
                    dve.wait_ge(S["m_xcd"], START + x)
                    T(xc.rearrange("p (h d) -> p h d", h=NH), x2h, heads(dth_), ALU.mult).then_inc(S["m_xc"], 1)

                def gate_z(x):
                    dve.wait_ge(S["m_y2"], START + x)
                    dve.wait_ge(S["m_tz"], START + x + 1)
                    V_.scalar_tensor_tensor(z2h.rearrange("p h d -> p (h d)"), sq[:, 0:INNER], 1.0, QK[:, 0:INNER],
                                            ALU.add, ALU.mult).then_inc(S["m_z2h"], 1)

                def y_norm(m):
                    dve.wait_ge(S["m_rms"], START + m + 1)
                    V_.tensor_scalar(yn, y2, rmsh, None, ALU.mult).then_inc(S["m_yn"], 1)

                def yT_low(m):
                    dve.wait_ge(S["m_yT_hi"], START + m + 1)
                    T(oT[1][:].rearrange("p c t -> p (c t)"), TP[0][:], oT[0][:].rearrange("p c t -> p (c t)").bitcast(F32),
                      ALU.subtract).then_inc(S["m_yT"], 1)

                def output(m, j):
                    dve.wait_ge(S["m_mo"], START + m + 1)
                    T(xsum[:, j, :], TP[0][:, 0:DIM], xsum[:, j, :], ALU.add).then_inc(S["m_out"], 1)

                def bcT_out(x):
                    dve.wait_ge(S["m_bcT_psum"], START + x + 1)
                    V_.tensor_copy(bcT, TP[1][0:D_STATE, 0:2 * P]).then_inc(S["m_bcT"], 1)

                def cb_out(x):
                    dve.wait_ge(S["m_ex"], START + x + 1)
                    dve.wait_ge(S["m_MT"], START + x)
                    T(scT, TP[1][:, 2 * P:3 * P], tri, ALU.mult).then_inc(S["m_scT"], 1)

                def weights(x):
                    dve.wait_ge(S["m_L"], START + x + 1)
                    dve.wait_ge(S["m_scT"], START + x + 1)
                    T(mT.rearrange("p (h l) -> p h l", h=NH), decay.rearrange("p (h l) -> p h l", h=NH),
                      scT.unsqueeze(1).to_broadcast([P, NH, P]), ALU.mult).then_inc(S["m_MT"], 1)

                dve.wait_ge(S["m_par_done"], START + 1)
                V_.tensor_scalar(small[:, NEGA:NEGA + NH], small[:, NEGA:NEGA + NH], -1.0, None, ALU.mult)
                V_.tensor_scalar(small[:, DHALF:DHALF + NH], small[:, DHALF:DHALF + NH], 0.5, None, ALU.mult)
                V_.memset(state, 0.0).then_inc(S["m_state"], 1)
                T(w_in[1], w_in_raw, w_in[0].bitcast(F32), ALU.subtract)
                for c in range(OT):
                    ins = V_.scalar_tensor_tensor(w_out[1][:, c, :], w_out_raw[:, c, :], small[:, RMSW + c:RMSW + c + 1],
                                                  w_out[0][:, c, :].bitcast(F32), ALU.mult, ALU.subtract)
                ins.then_inc(S["m_par_done"], 1)
                dve.wait_ge(S["m_par_done"], START + 2)
                input_stats(0)
                first_norm(0)
                second_norm(0)
                h_split(0)
                gates_bcdt(0, 0, 1)
                bcT_out(0)
                gate_x(0)
                gate_z(0)
                cb_out(0)
                h_split(1)
                weights(0)
                gates_bcdt(1, 1, 1)
                with dve.Fori(0, QUADS) as q:
                    for j in range(QW):
                        m = 4 * q + j
                        x = m + 1
                        if j:
                            gates_bcdt(x, (j + 1) % QW, q + (2 if j == QW - 1 else 1))
                            yT_low(m - 1)
                        dve.wait_ge(S["m_yo"], START + m + 1)
                        T(ysum, OB[:].rearrange("p (h d) -> p h d", h=NH), heads(ex[j % 2][:, 0:NH]), ALU.mult).then_inc(S["m_t1"], 1)
                        dve.wait_ge(S["m_yd"], START + m + 1)
                        dve.wait_ge(S["m_t1"], START + m + 1)
                        T(ysum, ysum, VB[:].rearrange("p (h d) -> p h d", h=NH), ALU.add).then_inc(S["m_t2"], 1)
                        bcT_out(x)
                        gate_x(x)
                        h_split(m + 2)
                        if j == 1:
                            first_norm(q + 1)
                        dve.wait_ge(S["m_t3"], START + m + 1)
                        dve.wait_ge(S["m_yn"], START + m)
                        T(y2, ysum, z2h, ALU.mult).then_inc(S["m_y2"], 1)
                        cb_out(x)
                        gate_z(x)
                        dve.wait_ge(S["m_stmp"], START + m + 1)
                        dve.wait_ge(S["m_upd"], START + m + 1)
                        T(state, s_tmp, OB[0:D_STATE, :], ALU.add).then_inc(S["m_state"], 1)
                        if j:
                            output(m - 1, j - 1)
                        dve.wait_ge(S["m_sq"], START + m + 1)
                        V_.tensor_scalar(rms, ssum, 1.0 / INNER, 4 * EPS_SSM, ALU.mult, ALU.add).then_inc(S["m_rv"], 1)
                        weights(x)
                        y_norm(m)
                        if j == 0:
                            input_stats(q + 1)
                        if j == 1:
                            dve.wait_ge(S["m_hT_psum"], START + m + 3)
                            second_norm(q + 1)
                        if j == QW - 1:
                            yT_low(m)
                            gates_bcdt(x + 1, 1, q + 2)
                            output(m, j)
                            dve.wait_ge(S["m_out"], START + 4 * q + 4)
                            for tt in range(QW):
                                ins = V_.bn_stats(stats[:, tt // 2, tt % 2, :], xsum[:, tt, :])
                            ins.then_inc(S["ln_stats"], 1)
                            dve.wait_ge(S["ln_stats"], START + LN0 + q + 1)
                            V_.memset(gap[:], 0.0)
                            for tt in range(QW):
                                ins = V_.bn_aggr(ln_mv[:, tt, :], stats[:, tt // 2, tt % 2, :])
                            ins.then_inc(S["ln_mv"], 1)
                            dve.wait_ge(S["ln_rstd"], START + LN0 + q + 1)
                            for h in range(2):
                                dve.wait_ge(S[f"u_stored{h}"], START + 16 * (24 * len(blocks[:1]) + q))
                            for tt in range(QW):
                                ins = V_.tensor_scalar(u0[:, tt, :], xsum[:, tt, :], ln_mv[:, tt, 0:1], ln_r[:, tt:tt + 1],
                                                       ALU.subtract, ALU.mult)
                            ins.then_inc(S["m_u0"], 1)

            V_.memset(w1_raw[:, :, :, HID:HC * P], 0.0)
            V_.memset(w2_raw[:, HC - 1, :], 0.0)
            V_.memset(zrow[:], 0.0)
            V_.memset(V[:, QW - 1, :], 0.0)
            V_.memset(halfpow[:], -0.5)
            V_.memset(half[:], 0.5)
            V_.memset(eps[:, 0, :], EPS_LN)
            V_.memset(eps[:, 1, :], EPS_SSM)
            for l in range(LAYERS):
                for o in (B1A, B1G):
                    ins = V_.memset(small_raw[:, l, o + HC - 1:o + HC], 0.0)
            ins.then_inc(S["const_done"], 1)
            if 0 in blocks:
                input_norm()
            dve.wait_ge(S["const_loaded"], START + 16 * (3 + LAYERS * (6 + 1 + 2 + 2 + 2)))
            for l in range(LAYERS):
                V_.tensor_scalar(small_raw[:, l, FAC:FAC + HD], small_raw[:, l, FAC:FAC + HD], QK_SCALE, None, ALU.mult)
                V_.tensor_scalar(small_raw[:, l, FAC + HD:FAC + HD + HD // 2], small_raw[:, l, FAC + HD:FAC + HD + HD // 2], -QK_SCALE, None, ALU.mult)
                V_.tensor_scalar(small_raw[:, l, FAC + HD + HD // 2:FAC + 2 * HD], small_raw[:, l, FAC + HD + HD // 2:FAC + 2 * HD], QK_SCALE, None, ALU.mult)
                ins = V_.tensor_scalar(small_raw[:, l, FAC + 3 * HD:FAC + 3 * HD + HD // 2], small_raw[:, l, FAC + 3 * HD:FAC + 3 * HD + HD // 2], -1.0, None, ALU.mult)
            ins.then_inc(S["const_done"], 2)
            dve.wait_ge(S["const_done"], START + 3)
            for b in blocks:
                stack(b)
                if b == 0 and mix:
                    state_space()
            if not blocks:
                state_space()

        @block.gpsimd
        def _(pool):
            G = nc.gpsimd
            H2 = HD // 2
            start_counts(pool, 4)

            def rope_window(b, x, xs, slot, loads, factors):
                pool.wait_ge(S["small_done"], START + factors)
                pool.wait_ge(S[f"rope_loaded{slot}"], START + 16 * loads)
                for g in range(2):
                    ins = G.tensor_tensor(rope[:, xs, g].rearrange("p c (e d) -> p c e d", e=2),
                                          rope_raw[:, slot, g].unsqueeze(2).to_broadcast([P, 2, 2, H2]),
                                          small[:, FAC + 2 * g * HD:FAC + 2 * (g + 1) * HD].rearrange("p (c e d) -> p c e d", c=2, e=2), ALU.mult)
                ins.then_inc(S["fold_done"], 1)
                pool.wait_ge(S["rn_clip"], START + 2 * x + 1)
                G.tensor_tensor(inv_norm[:, xs, HEADS:2 * HEADS], sq_sums_clipped[:, HEADS:2 * HEADS], halfpow[:, 0:HEADS], ALU.pow).then_inc(S["rn_done"], 1)
                pool.wait_ge(S["mulk"], START + x + 1)
                G.tensor_tensor(by_cos[:, 1], by_cos[:, 1], by_sin[:, 1], ALU.add).then_inc(S["k_sum"], 1)
                pool.wait_ge(S["rn_done"], START + 2 * x + 1)
                pool.wait_ge(S["k_sum"], START + x + 1)
                G.tensor_tensor(qk[:, 1], by_cos[:, 1], inv_norm[:, xs, HEADS:2 * HEADS].unsqueeze(2).to_broadcast([P, HEADS, HD]),
                                ALU.mult).then_inc(S["k_ready"], 1)
                pool.wait_ge(S["mulq"], START + x + 1)
                G.tensor_tensor(qk[:, 0], by_cos[:, 0], by_sin[:, 0], ALU.add).then_inc(S["rope_q"], 1)
                pool.wait_ge(S["rn_clip"], START + 2 * x + 2)
                G.tensor_tensor(inv_norm[:, xs, 0:HEADS], sq_sums_clipped[:, 0:HEADS], halfpow[:, 0:HEADS], ALU.pow).then_inc(S["rn_done"], 1)

            def norm_root(b, i, h):
                f = 2 * (16 * b + i) + h
                pool.wait_ge(S["mv_done"], START + f + 1)
                G.tensor_tensor(var_e[:], mv[:, :, 1], eps[:, 0, 0:2], ALU.add).then_inc(S["var_done"], 1)
                pool.wait_ge(S["var_done"], START + f + 1)
                G.tensor_tensor(rstd[:], var_e[:], halfpow[:, 0:2], ALU.pow).then_inc(S["rstd_done"], 1)

            def add_bias(b, i, h):
                pool.wait_ge(S[f"u_stored{h}"], START + 16 * (24 * b + 8 + i))
                pool.wait_ge(S["x1_done"], START + 64 * b + 4 * i + 2 * h + 2)
                for tt in range(2):
                    ins = G.tensor_tensor(x2[:, h, tt, :], x1[:, 2 * h + tt, :], small[:, B2:B2 + DIM], ALU.add)
                ins.then_inc(S["bias_added"], 1)

            def feed_forward(b, i):
                add_bias(b, i, 0)
                for h in range(2):
                    f = 2 * (16 * b + i) + h
                    for c in range(HC - 1):
                        pool.wait_ge(S["gg_hi"], START + 6 * f + c + 1)
                        G.tensor_tensor(gg[1][:, c, :], gf[:, c % 2, :], gg[0][:, c, :].bitcast(F32), ALU.subtract).then_inc(S["gg_ready"], 1)
                        if h == 0 and c == 3:
                            norm_root(b, i, 1)
                    if h == 0:
                        add_bias(b, i, 1)
                    flat = x2[:, h].rearrange("p t c -> p (t c)")
                    pool.wait_ge(S["x2_done"], START + f + 1)
                    G.tensor_tensor(hn_tile[:], flat, half[:].to_broadcast([P, 2 * DIM]), ALU.mult).then_inc(S["x2_half"], 1)
                    pool.wait_ge(S["x2_half"], START + f + 1)
                    pool.wait_ge(S[f"xres_loaded{h}"], START + 16 * (16 * b + i + 1))
                    res = xres[:, h].rearrange("p t c -> p (t c)")
                    G.tensor_tensor(res, hn_tile[:], res, ALU.add).then_inc(S[f"out_done{h}"], 1)

            def input_norm():
                with pool.Fori(0, QUADS // 2) as n:
                    for s in range(2):
                        pool.wait_ge(S["ln_mv"], START + 2 * n + s + 1)
                        G.tensor_tensor(mvar[:, s], mmv[:, s, :, 1], eps[:, 0, :], ALU.add).then_inc(S["ln_var"], 1)
                        pool.wait_ge(S["ln_var"], START + 2 * n + s + 1)
                        G.tensor_tensor(mrs[:, s], mvar[:, s], halfpow[:, 0:4], ALU.pow).then_inc(S["ln_rstd"], 1)

            def stack(b):
                rope_window(b, 65 * b, 0, 0, 17 * b + 1, 2 * b + 1)
                with pool.Fori(0, TRIPS) as i:
                    for j in range(QW):
                        nj = (j + 1) % QW
                        loads = 17 * b + i + 2 if nj == 0 else 17 * b + i + 1
                        factors = 2 * b + 1 + ((((i + 1) >> 3) & 1) if j == QW - 1 else (i >> 3))
                        if j == QW - 1:
                            norm_root(b, i, 0)
                        rope_window(b, 65 * b + 4 * i + j + 1, (j + 1) % 2, nj, loads, factors)
                    feed_forward(b, i)

            def state_space():
                T = G.tensor_tensor

                def heads(a):
                    return a.unsqueeze(2).to_broadcast([P, NH, HD])

                def root(n, which, mv_n):
                    pool.wait_ge(S["m_mv"], START + mv_n)
                    T(mvar[:, which], mmv[:, which, :, 1], eps[:, which, :], ALU.add).then_inc(S["m_var"], 1)
                    pool.wait_ge(S["m_var"], START + mv_n)
                    T(mrs[:, which], mvar[:, which], halfpow[:, 0:QW], ALU.pow).then_inc(S["m_rstd"], 1)

                def sum_input():
                    T(xsum, u_in[:], xln[:], ALU.add).then_inc(S["m_xsum"], 1)

                def a_masked(x):
                    pool.wait_ge(S["m_a"], START + x + 1)
                    pool.wait_ge(S["m_d"], START + x)
                    T(a_tri.rearrange("p (h l) -> p h l", h=NH), a_.unsqueeze(2).to_broadcast([P, NH, P]),
                      tri.unsqueeze(1).to_broadcast([P, NH, P]), ALU.mult).then_inc(S["m_atri"], 1)

                def inputs(x, s):
                    pool.wait_ge(S["m_x2h"], START + x + 1)
                    pool.wait_ge(S["m_t3"], START + x)
                    T(dx, x2h, heads(mp[:, DHALF:DHALF + NH]), ALU.mult).then_inc(S["m_dx"], 1)
                    pool.wait_ge(S["m_xc"], START + x + 1)
                    pool.wait_ge(S["m_ex"], START + x + 1)
                    pool.wait_ge(S["m_upd"], START + x)
                    T(xcd.rearrange("p (h d) -> p h d", h=NH), xc.rearrange("p (h d) -> p h d", h=NH),
                      heads(ex[s][:, NH:2 * NH]), ALU.mult).then_inc(S["m_xcd"], 1)

                root(0, 0, 1)
                root(0, 1, 2)
                sum_input()
                a_masked(0)
                inputs(0, 0)
                with pool.Fori(0, QUADS) as q:
                    for j in range(QW):
                        m = 4 * q + j
                        pool.wait_ge(S["m_state"], START + m + 1)
                        T(s_tmp.rearrange("p (h d) -> p h d", h=NH), state.rearrange("p (h d) -> p h d", h=NH),
                          ex[j % 2][0:D_STATE, 2 * NH:3 * NH].unsqueeze(2).to_broadcast([D_STATE, NH, HD]), ALU.mult).then_inc(S["m_stmp"], 1)
                        a_masked(m + 1)
                        pool.wait_ge(S["m_t2"], START + m + 1)
                        pool.wait_ge(S["m_dx"], START + m + 1)
                        T(ysum, ysum, dx, ALU.add).then_inc(S["m_t3"], 1)
                        inputs(m + 1, (j + 1) % 2)
                        if j == 1:
                            root(q + 1, 1, 2 * q + 4)
                        pool.wait_ge(S["m_rv"], START + m + 1)
                        T(rmsh, rms, halfpow[:, 0:1], ALU.pow).then_inc(S["m_rms"], 1)
                        if j == 0:
                            root(q + 1, 0, 2 * q + 3)
                    pool.wait_ge(S["ln_mv"], START + LN0 + q + 1)
                    G.tensor_tensor(ln_v[:], ln_mv[:, :, 1], eps[:, 0, :], ALU.add).then_inc(S["ln_var"], 1)
                    pool.wait_ge(S["ln_var"], START + LN0 + q + 1)
                    T(ln_r[:], ln_v[:], halfpow[:, 0:QW], ALU.pow).then_inc(S["ln_rstd"], 1)
                    pool.wait_ge(S["m_u0"], START + q + 1)
                    pool.wait_ge(S["m_out_stored"], START + 16 * (q + 1))
                    sum_input()

            pool.wait_ge(S["const_done"], START + 1)
            if 0 in blocks:
                input_norm()
            pool.wait_ge(S["const_done"], START + 3)
            for b in blocks:
                stack(b)
                if b == 0 and mix:
                    state_space()
            if not blocks:
                state_space()


def rope_table():
    f = np.float32
    half = np.arange(0, HD, 2, dtype=f)
    inv = (f(1.0) / np.power(f(10000.0), half / f(HD))).astype(f)
    pos = np.arange(N, dtype=f)
    ang = (pos[:, None] * inv[None, :]).astype(f)
    base = ((half + f(0.4 * HD)) / f(1.4 * HD)).astype(f)
    power = ((pos - f(N // 2)) / f(P // 2)).astype(f)
    scale = np.power(base[None, :], power[:, None]).astype(f)
    c, s = np.cos(ang).astype(f), np.sin(ang).astype(f)
    return np.ascontiguousarray(np.concatenate([c * scale, s * scale, c / scale, s / scale], axis=1).astype(f))


def state_rope_table():
    f = np.float32
    inv = (f(1.0) / np.power(f(10000.0), np.arange(0, ROPE_DIM, 2, dtype=f) / f(ROPE_DIM))).astype(f)
    ang = (np.arange(N, dtype=f)[:, None] * inv[None, :]).astype(f)
    c, s = np.cos(ang).astype(f), np.sin(ang).astype(f)
    own, partner = np.full((N, D_STATE), f(0.5)), np.zeros((N, D_STATE), f)
    own[:, 0:ROPE_DIM:2], own[:, 1:ROPE_DIM:2] = f(0.5) * c, f(0.5) * c
    partner[:, 0:ROPE_DIM:2], partner[:, 1:ROPE_DIM:2] = f(-0.5) * s, f(0.5) * s
    return np.ascontiguousarray(np.concatenate([own, partner], axis=1).astype(f))


def mask_table():
    q, k = np.arange(P)[:, None], np.arange(P)[None, :]
    m = [np.where(k < q, MASKED, 0.0), np.where(k > q, MASKED, 0.0)]
    return np.concatenate(m, axis=1).astype(np.float32)


def build(nc, arrays, blocks=(0, 1)):
    t = {}
    for name, a in arrays.items():
        t[name] = nc.dram_tensor("in_" + name, a.shape, mybir.dt.from_np(a.dtype), kind="ExternalInput").ap()
    t["u_dram"] = nc.dram_tensor("u_dram", ((LAYERS + 2) * REGION, DIM), F32, kind="Internal").ap()
    out = nc.dram_tensor("out", (N, DIM), F32, kind="ExternalOutput").ap()
    if blocks == (0, 1):
        mid = [nc.dram_tensor(f"mid_{n}", (N, DIM), F32, kind="Internal").ap() for n in range(2)]
        t["x_in"], t["x_out"] = (t["x"], mid[1]), (mid[0], out)
        t["m_in"], t["m_out"] = mid
    else:
        t["x_in"], t["x_out"] = (t["x"],), (out,)
        t["m_in"], t["m_out"] = t["x"], out
    macaron_program(nc, t, blocks)


def host_arrays(inp):
    a = {"x": np.ascontiguousarray(inp["L0_attn_x"]).reshape(N, DIM)}
    for k in ("wqkv", "wo", "w1", "w2", "q_scale", "k_scale", "ln_g", "ln_b", "b1", "b2"):
        a[k] = np.ascontiguousarray(inp["L0_ffn_" + k])
    for k, name in (("w_in", "W_in"), ("w_out", "W_out"), ("dt_bias", "dt_bias"), ("A_log", "A_log"), ("D", "D"),
                    ("m_ln_w", "ln_w"), ("m_ln_b", "ln_b"), ("rms_w", "rms_w")):
        a[k] = np.ascontiguousarray(inp["L0_attn_" + name])
    a["m_rope"] = state_rope_table()
    a["tri"] = np.triu(np.ones((P, P), np.float32))
    a["after"] = np.tril(np.ones((P, P), np.float32), -1)
    a["ones"] = np.ones((P, P), np.float32)
    a["rope"], a["mask"], a["ident"] = rope_table(), mask_table(), np.eye(P, dtype=np.float32)
    return a


def kernel(**inputs):
    import concourse.bacc as bacc
    from concourse.bass_utils import run_bass_kernel_spmd

    nc = bacc.Bacc("TRN2", target_bir_lowering=False, num_devices=1, dynamic_dma_scratch_size=1024)
    arrays = host_arrays({k: np.asarray(v) for k, v in inputs.items()})
    build(nc, arrays)
    r = run_bass_kernel_spmd(nc, [{"in_" + k: v for k, v in arrays.items()}], core_ids=[0])
    return r.results[0]["out"].reshape(1, N, DIM)
```
